# Optimizing a Trainium2 kernel written in Bass

```python
import numpy as np
import jax
import jax.numpy as jnp

def _softmax(x, axis=-1):
    return jax.nn.softmax(x, axis=axis)

def _gelu(x):
    return jax.nn.gelu(x, approximate=True)

def _silu(x):
    return jax.nn.silu(x)

def _sigmoid(x):
    return jax.nn.sigmoid(x)

def _layernorm(x, axis=-1, eps=1e-05):
    m = jnp.mean(x, axis=axis, keepdims=True)
    v = jnp.var(x, axis=axis, keepdims=True)
    return (x - m) / jnp.sqrt(v + eps)

def _scatter_add(tgt, idx, src, axis=0):
    return tgt.at[idx].add(src)

def _segment_sum(src, seg, n):
    return jax.ops.segment_sum(src, seg, n)
kernel_name = 'mk_xattn_ffn_d2_seqx_r4_d40efd'

def setup_inputs(seed: int=0):
    np.random.seed(seed)
    _w = jnp.asarray

    def _rec_inputs():
        import jax
        import jax.numpy as jnp
        _rk = jax.random.key(seed)
        x = 7.22e-05 + 1 * jax.random.normal(jax.random.fold_in(_rk, 1), (16, 112, 256), jnp.float32)
        _lenS = 112 - jax.random.randint(jax.random.fold_in(_rk, 7), (16,), 0, max(1, 112 // 4) + 1, jnp.int32)
        _lenS2 = 375 - jax.random.randint(jax.random.fold_in(_rk, 8), (16,), 0, max(1, 375 // 4) + 1, jnp.int32)
        _ctx_768P = jax.random.normal(jax.random.fold_in(_rk, 11), (16, 16, 192), jnp.float32)
        _ctx_768c = jax.random.dirichlet(jax.random.fold_in(_rk, 511), 0.3 * jnp.ones((16,), jnp.float32), (16, 375))
        _ctx_768t = jnp.einsum('bsk,bkd->bsd', _ctx_768c, _ctx_768P)
        _ctx_768t = _ctx_768t * jax.lax.rsqrt(jnp.mean(jnp.square(_ctx_768t)) + 1e-12) * 0.953939
        ctx_768 = 2.09791e-05 + 1.00001 * (_ctx_768t + 0.3 * jax.random.normal(jax.random.fold_in(_rk, 611), (16, 375, 192), jnp.float32))
        _validS = jnp.arange(112)[None, :] < _lenS[:, None]
        _validS2 = jnp.arange(375)[None, :] < _lenS2[:, None]
        _causal = jnp.tril(jnp.ones((112, 112), dtype=bool))
        mask_BxS_bf1 = jnp.ones((16, 112), dtype=bool)
        mask_BxS2_bf1 = jnp.ones((16, 375), dtype=bool)
        return (x, ctx_768, mask_BxS_bf1, mask_BxS2_bf1)
    x, ctx_768, mask_BxS_bf1, mask_BxS2_bf1 = _rec_inputs()

    def _L0_xattn_setup():
        import jax, jax.numpy as jnp
        import numpy as np
        HEADS = 16
        DIM_HEAD = 64
        key = jax.random.key(seed)
        ks = jax.random.split(key, 7)
        B, Nq, Dq = (4, 512, 256)
        Nk, Dc = (256, 192)
        inner = HEADS * DIM_HEAD
        sq = 1.0 / np.sqrt(Dq)
        sc = 1.0 / np.sqrt(Dc)
        si = 1.0 / np.sqrt(inner)
        return {'x': jax.random.normal(ks[0], (B, Nq, Dq), dtype=jnp.float32), 'context': jax.random.normal(ks[1], (B, Nk, Dc), dtype=jnp.float32), 'Wq': jax.random.normal(ks[2], (Dq, inner), dtype=jnp.float32) * sq, 'Wk': jax.random.normal(ks[3], (Dc, inner), dtype=jnp.float32) * sc, 'Wv': jax.random.normal(ks[4], (Dc, inner), dtype=jnp.float32) * sc, 'Wo': jax.random.normal(ks[5], (inner, Dq), dtype=jnp.float32) * si, 'bo': jax.random.normal(ks[6], (Dq,), dtype=jnp.float32) * 0.01}
    _L0_xattn_all = _L0_xattn_setup()
    _L0_xattn_in = {k: v for k, v in _L0_xattn_all.items() if k in ('Wq', 'Wk', 'Wv', 'Wo', 'bo')}
    del _L0_xattn_all

    def _L0_ffn_setup():
        import jax, jax.numpy as jnp
        import numpy as np
        LN_EPS = 1e-05

        def layernorm(x, g, b):
            mu = jnp.mean(x, axis=-1, keepdims=True)
            var = jnp.mean((x - mu) ** 2, axis=-1, keepdims=True)
            return (x - mu) * jax.lax.rsqrt(var + LN_EPS) * g + b

        def act_quant_fake(x):
            scale = 127.0 / jnp.clip(jnp.max(jnp.abs(x), axis=-1, keepdims=True), 1e-05)
            return jnp.clip(jnp.round(x * scale), -128.0, 127.0) / scale

        def weight_quant_fake(w):
            scale = 1.0 / jnp.clip(jnp.mean(jnp.abs(w)), 1e-05)
            return jnp.clip(jnp.round(w * scale), -1.0, 1.0) / scale

        def bitlinear(x, w, b):
            dqx = act_quant_fake(x)
            dqw = weight_quant_fake(w)
            return jnp.einsum('btd,hd->bth', dqx, dqw) + b
        key = jax.random.key(seed)
        ks = jax.random.split(key, 5)
        B, T, D, H = (8, 1024, 256, 1024)
        return {'x': jax.random.normal(ks[0], (B, T, D), dtype=jnp.float32), 'ln1_g': jnp.ones((D,), jnp.float32), 'ln1_b': jnp.zeros((D,), jnp.float32), 'w1': jax.random.normal(ks[1], (H, D), dtype=jnp.float32) * (1.0 / np.sqrt(D)), 'b1': jax.random.normal(ks[2], (H,), dtype=jnp.float32) * 0.02, 'ln2_g': jnp.ones((H,), jnp.float32), 'ln2_b': jnp.zeros((H,), jnp.float32), 'w2': jax.random.normal(ks[3], (D, H), dtype=jnp.float32) * (1.0 / np.sqrt(H)), 'b2': jax.random.normal(ks[4], (D,), jnp.float32) * 0.02}
    _L0_ffn_all = _L0_ffn_setup()
    _L0_ffn_in = {k: v for k, v in _L0_ffn_all.items() if k in ('ln1_g', 'ln1_b', 'w1', 'b1', 'ln2_g', 'ln2_b', 'w2', 'b2')}
    del _L0_ffn_all

    def _L1_xattn_setup():
        import jax, jax.numpy as jnp
        import numpy as np
        B, T, DT, G, DV = (16, 128, 256, 144, 192)
        H, DH = (4, 32)
        INNER = H * DH
        HID = 4 * DT
        N_STATE = 64
        K_TOP = 32

        def layernorm(x, g, b, eps=1e-05):
            m = x.mean(-1, keepdims=True)
            v = x.var(-1, keepdims=True)
            return (x - m) * jax.lax.rsqrt(v + eps) * g + b

        def s4d(x, log_dt, A_re, A_im, C_re, C_im, D_skip):
            Bb, L, D = x.shape
            dt = jnp.exp(log_dt)
            A = A_re + 1j * A_im
            C = C_re + 1j * C_im
            dtA = dt[:, None] * A
            dC = C * (jnp.exp(dtA) - 1.0) / A
            powers = jnp.exp(dtA[:, :, None] * jnp.arange(L))
            K = 2.0 * jnp.einsum('dn,dnl->dl', dC, powers).real
            n = 2 * L
            Kf = jnp.fft.rfft(K, n=n, axis=-1)
            xf = jnp.fft.rfft(x, n=n, axis=1)
            y = jnp.fft.irfft(xf * Kf.T[None], n=n, axis=1)[:, :L]
            return y + x * D_skip
        key = jax.random.key(seed)
        ks = jax.random.split(key, 16)
        s = 0.02
        inp = {'x_text': jax.random.normal(ks[0], (B, T, DT), jnp.float32), 'x_vision': jax.random.normal(ks[1], (B, G, DV), jnp.float32), 'text_mask': jnp.ones((B, T), bool), 'vision_mask': jnp.ones((B, G), bool), 'Wq': jax.random.normal(ks[2], (DT, INNER), jnp.float32) * s, 'Wk': jax.random.normal(ks[3], (DV, INNER), jnp.float32) * s, 'Wv': jax.random.normal(ks[4], (DV, DT), jnp.float32) * s, 'W_film_in': jax.random.normal(ks[5], (DT, 2 * DT), jnp.float32) * s, 'b_film_in': jnp.zeros((2 * DT,), jnp.float32), 'W_film_out': jax.random.normal(ks[6], (DT, 2 * DT), jnp.float32) * s, 'b_film_out': jnp.zeros((2 * DT,), jnp.float32), 'g_norm_in': jnp.ones((DT,), jnp.float32), 'b_norm_in': jnp.zeros((DT,), jnp.float32), 'g_norm_out': jnp.ones((DT,), jnp.float32), 'b_norm_out': jnp.zeros((DT,), jnp.float32), 'g_ffn': jnp.ones((DT,), jnp.float32), 'b_ffn': jnp.zeros((DT,), jnp.float32), 'W1': jax.random.normal(ks[7], (DT, HID), jnp.float32) * s, 'b1': jnp.zeros((HID,), jnp.float32), 'W2': jax.random.normal(ks[8], (HID, DT), jnp.float32) * s, 'b2': jnp.zeros((DT,), jnp.float32), 'log_dt': jnp.log(0.001) + jax.random.uniform(ks[9], (DT,), jnp.float32) * (jnp.log(0.1) - jnp.log(0.001)), 'A_re': -0.5 * jnp.ones((DT, N_STATE), jnp.float32), 'A_im': jnp.tile(jnp.pi * jnp.arange(N_STATE, dtype=jnp.float32), (DT, 1)), 'C_re': jax.random.normal(ks[10], (DT, N_STATE), jnp.float32) * 0.5 ** 0.5, 'C_im': jax.random.normal(ks[11], (DT, N_STATE), jnp.float32) * 0.5 ** 0.5, 'D_skip': jax.random.normal(ks[12], (DT,), jnp.float32), 'mod_gate': jnp.array(0.5, jnp.float32)}
        return inp
    _L1_xattn_all = _L1_xattn_setup()
    _L1_xattn_in = {k: v for k, v in _L1_xattn_all.items() if k in ('Wq', 'Wk', 'Wv', 'W_film_in', 'b_film_in', 'W_film_out', 'b_film_out', 'g_norm_in', 'b_norm_in', 'g_norm_out', 'b_norm_out', 'g_ffn', 'b_ffn', 'W1', 'b1', 'W2', 'b2', 'log_dt', 'A_re', 'A_im', 'C_re', 'C_im', 'D_skip', 'mod_gate')}
    del _L1_xattn_all

    def _L1_ffn_setup():
        import jax, jax.numpy as jnp
        import numpy as np
        B, S, H, I, E_ROUTED, TOP_K = (8, 512, 256, 512, 8, 2)

        def _expert(x, Wg, Wu, Wd):
            return jax.nn.silu(x @ Wg.T) * (x @ Wu.T) @ Wd.T
        key = jax.random.key(seed)
        ks = jax.random.split(key, 9)
        s = 0.02
        return {'x': jax.random.normal(ks[0], (B, S, H), dtype=jnp.float32), 'Wg_s': jax.random.normal(ks[1], (I, H), dtype=jnp.float32) * s, 'Wu_s': jax.random.normal(ks[2], (I, H), dtype=jnp.float32) * s, 'Wd_s': jax.random.normal(ks[3], (H, I), dtype=jnp.float32) * s, 'Wg': jax.random.normal(ks[4], (E_ROUTED, I, H), dtype=jnp.float32) * s, 'Wu': jax.random.normal(ks[5], (E_ROUTED, I, H), dtype=jnp.float32) * s, 'Wd': jax.random.normal(ks[6], (E_ROUTED, H, I), dtype=jnp.float32) * s, 'Wr': jax.random.normal(ks[7], (E_ROUTED, H), dtype=jnp.float32) * s, 'rb': jnp.zeros((E_ROUTED,), dtype=jnp.float32)}
    _L1_ffn_all = _L1_ffn_setup()
    _L1_ffn_in = {k: v for k, v in _L1_ffn_all.items() if k in ('Wg_s', 'Wu_s', 'Wd_s', 'Wg', 'Wu', 'Wd', 'Wr', 'rb')}
    del _L1_ffn_all
    return {'x': x, 'ctx_768': ctx_768, 'mask_BxS_bf1': mask_BxS_bf1, 'mask_BxS2_bf1': mask_BxS2_bf1, 'L0_xattn_Wq': _L0_xattn_in['Wq'], 'L0_xattn_Wk': _L0_xattn_in['Wk'], 'L0_xattn_Wv': _L0_xattn_in['Wv'], 'L0_xattn_Wo': _L0_xattn_in['Wo'], 'L0_xattn_bo': _L0_xattn_in['bo'], 'L0_ffn_ln1_g': _L0_ffn_in['ln1_g'], 'L0_ffn_ln1_b': _L0_ffn_in['ln1_b'], 'L0_ffn_w1': _L0_ffn_in['w1'], 'L0_ffn_b1': _L0_ffn_in['b1'], 'L0_ffn_ln2_g': _L0_ffn_in['ln2_g'], 'L0_ffn_ln2_b': _L0_ffn_in['ln2_b'], 'L0_ffn_w2': _L0_ffn_in['w2'], 'L0_ffn_b2': _L0_ffn_in['b2'], 'L1_xattn_Wq': _L1_xattn_in['Wq'], 'L1_xattn_Wk': _L1_xattn_in['Wk'], 'L1_xattn_Wv': _L1_xattn_in['Wv'], 'L1_xattn_W_film_in': _L1_xattn_in['W_film_in'], 'L1_xattn_b_film_in': _L1_xattn_in['b_film_in'], 'L1_xattn_W_film_out': _L1_xattn_in['W_film_out'], 'L1_xattn_b_film_out': _L1_xattn_in['b_film_out'], 'L1_xattn_g_norm_in': _L1_xattn_in['g_norm_in'], 'L1_xattn_b_norm_in': _L1_xattn_in['b_norm_in'], 'L1_xattn_g_norm_out': _L1_xattn_in['g_norm_out'], 'L1_xattn_b_norm_out': _L1_xattn_in['b_norm_out'], 'L1_xattn_g_ffn': _L1_xattn_in['g_ffn'], 'L1_xattn_b_ffn': _L1_xattn_in['b_ffn'], 'L1_xattn_W1': _L1_xattn_in['W1'], 'L1_xattn_b1': _L1_xattn_in['b1'], 'L1_xattn_W2': _L1_xattn_in['W2'], 'L1_xattn_b2': _L1_xattn_in['b2'], 'L1_xattn_log_dt': _L1_xattn_in['log_dt'], 'L1_xattn_A_re': _L1_xattn_in['A_re'], 'L1_xattn_A_im': _L1_xattn_in['A_im'], 'L1_xattn_C_re': _L1_xattn_in['C_re'], 'L1_xattn_C_im': _L1_xattn_in['C_im'], 'L1_xattn_D_skip': _L1_xattn_in['D_skip'], 'L1_xattn_mod_gate': _L1_xattn_in['mod_gate'], 'L1_ffn_Wg_s': _L1_ffn_in['Wg_s'], 'L1_ffn_Wu_s': _L1_ffn_in['Wu_s'], 'L1_ffn_Wd_s': _L1_ffn_in['Wd_s'], 'L1_ffn_Wg': _L1_ffn_in['Wg'], 'L1_ffn_Wu': _L1_ffn_in['Wu'], 'L1_ffn_Wd': _L1_ffn_in['Wd'], 'L1_ffn_Wr': _L1_ffn_in['Wr'], 'L1_ffn_rb': _L1_ffn_in['rb']}

def reference(x, ctx_768, mask_BxS_bf1, mask_BxS2_bf1, L0_xattn_Wq, L0_xattn_Wk, L0_xattn_Wv, L0_xattn_Wo, L0_xattn_bo, L0_ffn_ln1_g, L0_ffn_ln1_b, L0_ffn_w1, L0_ffn_b1, L0_ffn_ln2_g, L0_ffn_ln2_b, L0_ffn_w2, L0_ffn_b2, L1_xattn_Wq, L1_xattn_Wk, L1_xattn_Wv, L1_xattn_W_film_in, L1_xattn_b_film_in, L1_xattn_W_film_out, L1_xattn_b_film_out, L1_xattn_g_norm_in, L1_xattn_b_norm_in, L1_xattn_g_norm_out, L1_xattn_b_norm_out, L1_xattn_g_ffn, L1_xattn_b_ffn, L1_xattn_W1, L1_xattn_b1, L1_xattn_W2, L1_xattn_b2, L1_xattn_log_dt, L1_xattn_A_re, L1_xattn_A_im, L1_xattn_C_re, L1_xattn_C_im, L1_xattn_D_skip, L1_xattn_mod_gate, L1_ffn_Wg_s, L1_ffn_Wu_s, L1_ffn_Wd_s, L1_ffn_Wg, L1_ffn_Wu, L1_ffn_Wd, L1_ffn_Wr, L1_ffn_rb):
    import jax
    import jax.numpy as jnp

    def _L0_xattn_ref(x, context, Wq, Wk, Wv, Wo, bo):
        import jax, jax.numpy as jnp
        import numpy as np
        HEADS = 16
        DIM_HEAD = 64
        B, Nq, _ = x.shape
        Nk = context.shape[1]
        h, dh = (HEADS, DIM_HEAD)
        q = (x @ Wq).reshape(B, Nq, h, dh)
        k = (context @ Wk).reshape(B, Nk, h, dh)
        v = (context @ Wv).reshape(B, Nk, h, dh)
        scale = 1.0 / jnp.sqrt(jnp.asarray(dh, dtype=x.dtype))
        scores = jnp.einsum('bqhd,bkhd->bhqk', q, k) * scale
        attn = jax.nn.softmax(scores, axis=-1)
        out = jnp.einsum('bhqk,bkhd->bqhd', attn, v).reshape(B, Nq, h * dh)
        return out @ Wo + bo

    def _L0_ffn_ref(x, ln1_g, ln1_b, w1, b1, ln2_g, ln2_b, w2, b2):
        import jax, jax.numpy as jnp
        import numpy as np
        LN_EPS = 1e-05

        def layernorm(x, g, b):
            mu = jnp.mean(x, axis=-1, keepdims=True)
            var = jnp.mean((x - mu) ** 2, axis=-1, keepdims=True)
            return (x - mu) * jax.lax.rsqrt(var + LN_EPS) * g + b

        def act_quant_fake(x):
            scale = 127.0 / jnp.clip(jnp.max(jnp.abs(x), axis=-1, keepdims=True), 1e-05)
            return jnp.clip(jnp.round(x * scale), -128.0, 127.0) / scale

        def weight_quant_fake(w):
            scale = 1.0 / jnp.clip(jnp.mean(jnp.abs(w)), 1e-05)
            return jnp.clip(jnp.round(w * scale), -1.0, 1.0) / scale

        def bitlinear(x, w, b):
            dqx = act_quant_fake(x)
            dqw = weight_quant_fake(w)
            return jnp.einsum('btd,hd->bth', dqx, dqw) + b
        h = layernorm(x, ln1_g, ln1_b)
        h = bitlinear(h, w1, b1)
        h = jax.nn.gelu(h, approximate=False)
        h = layernorm(h, ln2_g, ln2_b)
        h = bitlinear(h, w2, b2)
        return h

    def _L1_xattn_ref(x_text, x_vision, text_mask, vision_mask, Wq, Wk, Wv, W_film_in, b_film_in, W_film_out, b_film_out, g_norm_in, b_norm_in, g_norm_out, b_norm_out, g_ffn, b_ffn, W1, b1, W2, b2, log_dt, A_re, A_im, C_re, C_im, D_skip, mod_gate):
        import jax, jax.numpy as jnp
        import numpy as np
        B, T, DT, G, DV = (16, 128, 256, 144, 192)
        H, DH = (4, 32)
        INNER = H * DH
        HID = 4 * DT
        N_STATE = 64
        K_TOP = 32

        def layernorm(x, g, b, eps=1e-05):
            m = x.mean(-1, keepdims=True)
            v = x.var(-1, keepdims=True)
            return (x - m) * jax.lax.rsqrt(v + eps) * g + b

        def s4d(x, log_dt, A_re, A_im, C_re, C_im, D_skip):
            Bb, L, D = x.shape
            dt = jnp.exp(log_dt)
            A = A_re + 1j * A_im
            C = C_re + 1j * C_im
            dtA = dt[:, None] * A
            dC = C * (jnp.exp(dtA) - 1.0) / A
            powers = jnp.exp(dtA[:, :, None] * jnp.arange(L))
            K = 2.0 * jnp.einsum('dn,dnl->dl', dC, powers).real
            n = 2 * L
            Kf = jnp.fft.rfft(K, n=n, axis=-1)
            xf = jnp.fft.rfft(x, n=n, axis=1)
            y = jnp.fft.irfft(xf * Kf.T[None], n=n, axis=1)[:, :L]
            return y + x * D_skip
        Bb, Tt, D = x_text.shape
        Gg = x_vision.shape[1]
        Q = (x_text @ Wq).reshape(Bb, Tt, H, DH)
        K = (x_vision @ Wk).reshape(Bb, Gg, H, DH)
        scores = jnp.einsum('bthd,bghd->bhtg', Q, K) / np.sqrt(DH).astype(np.float32)
        scores = jnp.where(vision_mask[:, None, None, :], scores, -jnp.inf)
        topv, topi = jax.lax.top_k(scores, K_TOP)
        probs = jax.nn.softmax(topv, axis=-1)
        bi = jnp.arange(Bb)[:, None, None, None]
        hi = jnp.arange(H)[None, :, None, None]
        ti = jnp.arange(Tt)[None, None, :, None]
        attn = jnp.zeros_like(scores).at[bi, hi, ti, topi].set(probs)
        attn_mean = attn.mean(axis=1)
        V = x_vision @ Wv
        c_t = jnp.einsum('btg,bgd->btd', attn_mean, V)
        c_t = c_t * text_mask[..., None]
        x = layernorm(x_text, g_norm_in, b_norm_in)
        scale_in, shift_in = jnp.split(c_t @ W_film_in + b_film_in, 2, axis=-1)
        x = x * (1.0 + mod_gate * scale_in) + mod_gate * shift_in
        y = s4d(x, log_dt, A_re, A_im, C_re, C_im, D_skip)
        scale_out, shift_out = jnp.split(c_t @ W_film_out + b_film_out, 2, axis=-1)
        y = y * (1.0 + mod_gate * scale_out) + mod_gate * shift_out
        xt = x_text + y
        h = layernorm(xt, g_ffn, b_ffn)
        h = jax.nn.gelu(h @ W1 + b1, approximate=False) @ W2 + b2
        xt = xt + h
        return layernorm(xt, g_norm_out, b_norm_out)

    def _L1_ffn_ref(x, Wg_s, Wu_s, Wd_s, Wg, Wu, Wd, Wr, rb):
        import jax, jax.numpy as jnp
        import numpy as np
        B, S, H, I, E_ROUTED, TOP_K = (8, 512, 256, 512, 8, 2)

        def _expert(x, Wg, Wu, Wd):
            return jax.nn.silu(x @ Wg.T) * (x @ Wu.T) @ Wd.T
        shared = _expert(x, Wg_s, Wu_s, Wd_s)
        logits = jnp.einsum('bsh,eh->bse', x, Wr) + rb
        probs = jax.nn.sigmoid(logits)
        scores, idx = jax.lax.top_k(probs, TOP_K)
        cw = (jax.nn.one_hot(idx, E_ROUTED, dtype=x.dtype) * scores[..., None]).sum(-2)
        out = shared
        for e in range(E_ROUTED):
            out = out + cw[..., e:e + 1] * _expert(x, Wg[e], Wu[e], Wd[e])
        return out
    x = x + _L0_xattn_ref(_layernorm(x, axis=-1), ctx_768, L0_xattn_Wq, L0_xattn_Wk, L0_xattn_Wv, L0_xattn_Wo, L0_xattn_bo)
    x = x + _L0_ffn_ref(_layernorm(x, axis=-1), L0_ffn_ln1_g, L0_ffn_ln1_b, L0_ffn_w1, L0_ffn_b1, L0_ffn_ln2_g, L0_ffn_ln2_b, L0_ffn_w2, L0_ffn_b2)
    x = x + _L1_xattn_ref(_layernorm(x, axis=-1), ctx_768, mask_BxS_bf1, mask_BxS2_bf1, L1_xattn_Wq, L1_xattn_Wk, L1_xattn_Wv, L1_xattn_W_film_in, L1_xattn_b_film_in, L1_xattn_W_film_out, L1_xattn_b_film_out, L1_xattn_g_norm_in, L1_xattn_b_norm_in, L1_xattn_g_norm_out, L1_xattn_b_norm_out, L1_xattn_g_ffn, L1_xattn_b_ffn, L1_xattn_W1, L1_xattn_b1, L1_xattn_W2, L1_xattn_b2, L1_xattn_log_dt, L1_xattn_A_re, L1_xattn_A_im, L1_xattn_C_re, L1_xattn_C_im, L1_xattn_D_skip, L1_xattn_mod_gate)
    x = x + _L1_ffn_ref(_layernorm(x, axis=-1), L1_ffn_Wg_s, L1_ffn_Wu_s, L1_ffn_Wd_s, L1_ffn_Wg, L1_ffn_Wu, L1_ffn_Wd, L1_ffn_Wr, L1_ffn_rb)
    return x

_drawn_inputs = setup_inputs


def setup_inputs(seed=0):
    import zlib

    import numpy as np

    out = dict(_drawn_inputs(seed))
    spreads = {'L0_ffn_ln1_g': (1.0, 0.2),
     'L0_ffn_ln1_b': (0.0, 0.1),
     'L0_ffn_ln2_g': (1.0, 0.2),
     'L0_ffn_ln2_b': (0.0, 0.1),
     'L1_xattn_b_film_in': (0.0, 0.286),
     'L1_xattn_b_film_out': (0.0, 0.346),
     'L1_xattn_g_norm_in': (1.0, 0.2),
     'L1_xattn_b_norm_in': (0.0, 0.1),
     'L1_xattn_g_norm_out': (1.0, 0.2),
     'L1_xattn_b_norm_out': (0.0, 0.1),
     'L1_xattn_g_ffn': (1.0, 0.6),
     'L1_xattn_b_ffn': (0.0, 0.8),
     'L1_xattn_b1': (0.0, 0.8),
     'L1_xattn_b2': (0.0, 0.289),
     'L1_xattn_A_re': (-0.5, 0.6),
     'L1_ffn_rb': (0.0, 0.8)}
    factors = {'L0_xattn_bo': 3.946,
     'L0_ffn_b1': 2.775,
     'L0_ffn_b2': 3.823,
     'L1_xattn_Wq': 8.0,
     'L1_xattn_Wk': 8.0,
     'L1_xattn_Wv': 3.269,
     'L1_xattn_W_film_in': 4.276,
     'L1_xattn_W_film_out': 5.155,
     'L1_ffn_Wg_s': 4.76,
     'L1_ffn_Wu_s': 4.46,
     'L1_ffn_Wd_s': 4.493,
     'L1_ffn_Wg': 5.972,
     'L1_ffn_Wu': 5.908,
     'L1_ffn_Wd': 5.892,
     'L1_ffn_Wr': 6.722}
    for name, (base, spread) in spreads.items():
        noise = np.random.default_rng([zlib.crc32(name.encode()), seed]).standard_normal(out[name].shape)
        drawn = base * np.exp(spread * noise) if base else spread * noise
        out[name] = jnp.asarray(drawn.astype(out[name].dtype))
    for name, factor in factors.items():
        out[name] = (out[name] * factor).astype(out[name].dtype)
    return out
```

```python
from contextlib import ExitStack

import numpy as np

import concourse.bass as bass
from concourse import mybir

ALU = mybir.AluOpType
ACT = mybir.ActivationFunctionType
F32 = mybir.dt.float32
F16 = mybir.dt.float16
BF16 = mybir.dt.bfloat16
U8 = mybir.dt.uint8
AX_X = mybir.AxisListType.X

NB, T, D = 16, 112, 256
G, DC = 375, 192
GJ, GC = 3, 125
CK = DC // 2
H0, DH0, IN0 = 16, 64, 1024
H1, DH1 = 4, 32
HID = 1024
NEXP, EI = 9, 512
NST = 64
PA, PBS = 7, 16
CHB = 4
CH = CHB * T
NCH = NB // CHB
WS = 256.0
IWS = 1.0 / WS
MAGIC = 12582912.0
EPS = 1e-5
NEG = -3.0e38
MASKED = 1.0e30
TWO_PI = 6.283185307179586
TP1 = 6.28125
TP2 = float(np.float32(TWO_PI - TP1))
TP3 = float(TWO_PI - TP1 - TP2)


class Ring:

    def __init__(self, items, banks, full, act, dve):
        self.names = [n for n, _ in items]
        self.who = dict(items)
        self.bank = {n: banks[k % len(banks)] for k, n in enumerate(self.names)}
        self.full, self.act, self.dve = full, act, dve
        self.n = len(items)
        self.na = sum("A" in w for _, w in items)
        self.nd = sum("D" in w for _, w in items)

    def upto(self, name, letter):
        k = self.names.index(name)
        return sum(letter in self.who[m] for m in self.names[: k + 1])

    def wait_full(self, eng, i, name):
        eng.wait_ge(self.full, i * self.n + self.names.index(name) + 1)

    def wait_act(self, eng, i, name):
        eng.wait_ge(self.act, i * self.na + self.upto(name, "A"))

    def wait_dve(self, eng, i, name):
        eng.wait_ge(self.dve, i * self.nd + self.upto(name, "D"))

    def wait_emptied(self, eng, i, name):
        if "D" in self.who[name]:
            self.wait_dve(eng, i, name)
        else:
            self.wait_act(eng, i, name)

    def wait_free(self, pe, i, name):
        k = self.names.index(name)
        before = [m for m in self.names[:k] if self.bank[m] == self.bank[name]]
        if before:
            self.wait_emptied(pe, i, before[-1])
            return
        last = [m for m in self.names if self.bank[m] == self.bank[name]][-1]
        if "D" in self.who[last]:
            pe.wait_ge(self.dve, i * self.nd)
        else:
            pe.wait_ge(self.act, i * self.na)


def build(nc, t, out):
    with ExitStack() as ctx:
        def sem(name):
            return ctx.enter_context(nc.semaphore(name))

        SB = 206 * 1024
        arena = ctx.enter_context(nc.sbuf_tensor("arena", [128, SB], U8))
        top = [0]

        def carve(parts, shape, dt, at=None):
            n = int(np.prod(shape)) * {F32: 4, F16: 2, BF16: 2, U8: 1}[dt]
            start = top[0] if at is None else at[0]
            end = start + (n + 31) // 32 * 32
            if at is None:
                top[0] = end
            else:
                at[0] = end
            assert end <= SB, (end, SB)
            v = arena[0:parts, start:start + n].bitcast(dt)
            if len(shape) == 2:
                v = v.rearrange("p (a b) -> p a b", a=shape[0])
            elif len(shape) == 3:
                v = v.rearrange("p (a b c) -> p a b c", a=shape[0], b=shape[1])
            return v

        psum = ctx.enter_context(nc.psum_tensor("psum", [128, 8, 512], F32))

        def bank(k, parts, n, off=0):
            return psum[0:parts, k, off:off + n]

        def bank16(k, parts, n):
            return psum[0:parts, k, :].bitcast(BF16)[:, 0:n]

        X = carve(T, (NB, D), F32)
        identf = carve(128, (128,), F32)
        identb = carve(128, (128,), BF16)
        neghalf = carve(T, (1,), F32)
        ones_b = carve(128, (T,), BF16)
        ones_f = carve(128, (128,), F32)
        st = carve(T, (2, 6), F32)
        mv = carve(T, (2,), F32)
        ve = carve(T, (1,), F32)
        rstd = carve(T, (1,), F32)
        amax = carve(T, (1,), F32)
        amc = carve(T, (1,), F32)
        rcp = carve(T, (1,), F32)
        qsc = carve(T, (1,), F32)
        dq1 = carve(T, (1,), F32)
        dq2 = carve(T, (1,), F32)
        cw = carve(T, (NB, NEXP), F32)
        rbrow = carve(T, (8,), F32)
        wr_f = carve(128, (2, 8), F32)
        wr_hi = carve(128, (2, 8), F16)
        wr_lo = carve(128, (2, 8), F16)
        kept = top[0]

        def pair(parts, shape):
            return carve(parts, shape, F16), carve(parts, shape, F16)

        wq = pair(128, (2, IN0))
        wk = pair(CK, (2, IN0))
        wv = pair(CK, (2, IN0))
        wo = pair(128, (8, D))
        w1q = carve(128, (2, HID), BF16)
        w2q = carve(128, (8, D), BF16)
        uq = pair(128, (2, 128))
        uk = pair(CK, (2, 128))
        uv = pair(CK, (2, D))
        ufi = pair(128, (2, 2 * D))
        ufo = pair(128, (2, 2 * D))
        u1 = pair(128, (2, HID))
        u2 = pair(128, (8, D))
        dft = carve(T, (8, T), F32)
        coef = carve(T, (4, D), F32)
        b1row = carve(T, (HID,), F32)
        g2row = carve(T, (HID,), F32)
        h2row = carve(T, (HID,), F32)
        rows = carve(T, (12, D), F32)
        (bo_r, g1_r, h1_r, b2_r, gi_r, hi_r, go_r, ho_r, gf_r, hf_r, dsk_r, c2_r) = (rows[:, k, :] for k in range(12))
        mbi = carve(T, (2 * D,), F32)
        mbo = carve(T, (2 * D,), F32)
        b1col = carve(128, (8,), F32)
        mg = carve(T, (1,), F32)
        mgs = carve(T, (1,), F32)
        tmask8 = carve(T, (NB,), U8)
        tmask = carve(T, (NB,), F32)
        wmean = carve(128, (2,), F32)
        wsc = carve(128, (2,), F32)
        wab = carve(128, (2,), F32)
        kpow = carve(128, (2, T), F32)
        kt = carve(T, (D,), F32)
        work = top[0]

        w = [work]
        ctx_sb = carve(GC, (GJ, DC), F32, w)
        cT = carve(CK, (2, G), F16, w), carve(CK, (2, G), F16, w)
        xn = carve(T, (D,), F32, w)
        xT = carve(128, (2, T), F16, w), carve(128, (2, T), F16, w)
        xb = carve(T, (D,), F32, w)
        qT = carve(128, (8, T), F32, w)
        kT = carve(128, (8, G), F32, w)
        V = carve(GC, (GJ, IN0), F32, w)
        Pr = carve(T, (2, G), F32, w)
        PTs = carve(GC, (2, GJ * T), F32, w)
        nmx = carve(T, (H0,), F32, w)
        rsum = carve(T, (H0,), F32, w)
        rinv = carve(T, (H0,), F32, w)
        On = carve(T, (IN0,), F32, w)
        aT = carve(128, (8, T), F16, w), carve(128, (8, T), F16, w)
        after_a = w[0]
        ws = [work + 12 * 1024]
        stage = carve(128, (2, 2048), F32, ws)
        w = [after_a]
        s4 = {n: carve(128, (2, NST), F32, w) for n in
              ("ar", "ai", "cr", "ci", "re", "im", "th", "k", "s", "sh", "e1", "zr", "zi", "mr", "t1", "t2", "dr", "di")}
        ldt = carve(128, (2,), F32, w)
        dtc = carve(128, (2,), F32, w)
        vr = carve(128, (PBS + 1, NST), F32, w)
        vi = carve(128, (PBS + 1, NST), F32, w)
        ur = carve(128, (PA, NST), F32, w)
        ui = carve(128, (PA, NST), F32, w)
        p1 = carve(128, (PBS, NST), F32, w)
        p2 = carve(128, (PBS, NST), F32, w)
        w = [work]
        zb = carve(T, (D,), F32, w)
        hb = carve(T, (D,), F32, w)
        q1 = carve(T, (D,), BF16, w)
        hq1 = carve(128, (2, T), BF16, w)
        ub = carve(T, (HID,), F32, w)
        q2 = carve(T, (HID,), BF16, w)
        hq2 = carve(128, (8, T), BF16, w)
        xb2 = carve(T, (D,), F32, w)
        w = [work]
        ctx_c = carve(GC, (GJ, DC), F32, w)
        cTc = carve(CK, (2, G), F16, w), carve(CK, (2, G), F16, w)
        z = carve(T, (D,), F32, w)
        zT = carve(128, (2, T), F16, w), carve(128, (2, T), F16, w)
        q1T = carve(128, (T,), F32, w)
        k1T = carve(128, (G,), F32, w)
        V1 = carve(GC, (GJ, D), F32, w)
        vm8 = carve(128, (G,), U8, w)
        vmb = carve(128, (G,), BF16, w)
        top8 = carve(T, (2, 4, 8), F32, w)
        nmx1 = carve(T, (H1,), F32, w)
        R1 = carve(T, (2, G), F32, w)
        E1 = carve(T, (H1, G), F32, w)
        P1 = carve(T, (H1, G), F32, w)
        sum1 = carve(T, (H1,), F32, w)
        r1 = carve(T, (H1,), F32, w)
        r2 = carve(T, (H1,), F32, w)
        dg = carve(T, (H1, T), F32, w)
        atT = carve(GC, (GJ * T,), F32, w)
        ctT = carve(128, (2, T), F16, w), carve(128, (2, T), F16, w)
        mi = carve(T, (2 * D,), F32, w)
        mo = carve(T, (2 * D,), F32, w)
        x1 = carve(T, (D,), F32, w)
        xd = carve(T, (D,), F32, w)
        t1 = carve(T, (2 * D,), F32, w)
        t2 = carve(T, (2 * D,), F32, w)
        Y = carve(T, (2 * D,), F32, w)
        y = carve(T, (D,), F32, w)
        h2 = carve(T, (D,), F32, w)
        h2T = carve(128, (2, T), F16, w), carve(128, (2, T), F16, w)
        hid = carve(128, (8, T), F32, w)
        hidT = carve(128, (8, T), F16, w), carve(128, (8, T), F16, w)
        xo = carve(T, (D,), F32, w)
        w = [kept]
        ZT = carve(128, (2, NB * T), F16, w), carve(128, (2, NB * T), F16, w)
        ze = carve(T, (D,), F32, w)
        zt_t = carve(128, (2, T), F16, w), carve(128, (2, T), F16, w)
        pr = carve(T, (16,), F32, w)
        pm8 = carve(T, (8,), F32, w)
        pin = carve(T, (8,), F32, w)
        prr = carve(T, (16,), F32, w)
        pne = carve(T, (8,), F32, w)
        lg = carve(T, (8,), F32, w)
        estage = carve(128, (3, 1024), F32, w)
        eg = [(carve(128, (2, EI), F16, w), carve(128, (2, EI), F16, w)) for _ in range(2)]
        eu = [(carve(128, (2, EI), F16, w), carve(128, (2, EI), F16, w)) for _ in range(2)]
        ed = [(carve(128, (4, D), F16, w), carve(128, (4, D), F16, w)) for _ in range(2)]
        sg = carve(128, (2, CH), F32, w)
        hf = carve(128, (2, CH), F32, w)
        hT = [(carve(128, (4, CH), F16, w), carve(128, (4, CH), F16, w)) for _ in range(2)]

        s_x = sem("x_loaded")
        s_const = sem("constants_loaded")
        s_stage = [sem("weight_staged_even"), sem("weight_staged_odd")]
        s_hi = sem("weight_high_part")
        s_lo = sem("weight_done")
        s_wsum = sem("weight_magnitude_summed")
        s_misc = sem("small_constants_ready")
        s_pmisc = sem("pool_constants_ready")
        s_dset = sem("vector_setup_step")
        s_s4a = sem("s4d_activation")
        s_s4v = sem("s4d_vector_step")
        s_s4p = sem("s4d_pool_step")
        s_s4h = sem("s4d_half_loaded")

        consts = []
        for k, n in enumerate(("L0_xattn_bo", "L0_ffn_ln1_g", "L0_ffn_ln1_b", "L0_ffn_b2", "L1_xattn_g_norm_in",
                               "L1_xattn_b_norm_in", "L1_xattn_g_norm_out", "L1_xattn_b_norm_out", "L1_xattn_g_ffn",
                               "L1_xattn_b_ffn", "L1_xattn_D_skip", "L1_xattn_b2")):
            consts.append((rows[:, k, :], t[n].partition_broadcast(T)))
        consts += [(b1row, t["L0_ffn_b1"].partition_broadcast(T)), (g2row, t["L0_ffn_ln2_g"].partition_broadcast(T)),
                   (h2row, t["L0_ffn_ln2_b"].partition_broadcast(T)),
                   (mbi, t["L1_xattn_b_film_in"].partition_broadcast(T)),
                   (mbo, t["L1_xattn_b_film_out"].partition_broadcast(T)),
                   (b1col, t["L1_xattn_b1"]),
                   (mg, t["L1_xattn_mod_gate"].partition_broadcast(T)),
                   (rbrow, t["L1_ffn_rb"].partition_broadcast(T)),
                   (tmask8, t["mask_BxS_bf1"]),
                   (wr_f, t["L1_ffn_Wr"].rearrange("(k p) e -> p k e", p=128)),
                   (dft, t["dft"].rearrange("m p k -> p m k")),
                   (identf, t["ident"]),
                   (ldt, t["L1_xattn_log_dt"])]
        for n, k in (("L1_xattn_A_re", "ar"), ("L1_xattn_A_im", "ai"), ("L1_xattn_C_re", "cr"), ("L1_xattn_C_im", "ci")):
            consts.append((s4[k], t[n].rearrange("(h p) n -> p h n", p=128)))
        NCONST = len(consts)

        def kview(name, k):
            return t[name].rearrange("(k p) n -> p k n", k=k)

        splits = [("L0_xattn_Wq", 128, 2, IN0, wq), ("L0_xattn_Wk", CK, 2, IN0, wk), ("L0_xattn_Wv", CK, 2, IN0, wv),
                  ("L0_xattn_Wo", 128, 8, D, wo),
                  ("L1_xattn_Wq", 128, 2, 128, uq), ("L1_xattn_Wk", CK, 2, 128, uk), ("L1_xattn_Wv", CK, 2, D, uv),
                  ("L1_xattn_W_film_in", 128, 2, 2 * D, ufi), ("L1_xattn_W_film_out", 128, 2, 2 * D, ufo),
                  ("L1_xattn_W1", 128, 2, HID, u1), ("L1_xattn_W2", 128, 8, D, u2)]
        quants = [("L0_ffn_w1", 2, HID, w1q), ("L0_ffn_w2", 8, D, w2q)]
        NSPL = len(splits)
        NW = NSPL + len(quants)

        def staged(k, parts, a, b):
            return stage[0:parts, k % 2, 0:a * b].rearrange("p (a b) -> p a b", a=a)

        a_ctx = sem("a_context_loaded")
        a_var = sem("a_variance_ready")
        a_rstd = sem("a_inverse_deviation")
        a_step = sem("a_vector_step")
        a_xn = sem("a_normed")
        a_xb = sem("a_residual_with_bias")
        a_S = sem("a_scores_ready")
        a_mx = sem("a_maximum_ready")
        a_E = sem("a_probs_ready")
        a_pt = sem("a_probs_transposed")
        a_pd = sem("a_transposed_kept_by_vector")
        a_pa = sem("a_transposed_kept_by_scalar")
        a_O = sem("a_head_outputs_ready")
        a_On = sem("a_outputs_normed")
        itemsA = ([("c0", "AD"), ("c1", "AD"), ("xn", "AD"), ("q0", "A"), ("q1", "A")]
                  + [(f"k{m}", "DA"[m % 2]) for m in range(8)]
                  + [(f"v{m}", "DA"[m % 2]) for m in range(6)]
                  + [("o0", "AD"), ("o1", "AD"), ("wo", "D")])
        ra = Ring(itemsA, (0, 1), sem("a_bank_filled"), sem("a_bank_read_by_scalar"), sem("a_bank_read_by_vector"))
        b_var = sem("b_variance_ready")
        b_rstd = sem("b_inverse_deviation")
        b_step = sem("b_vector_step")
        b_q = sem("b_quantized")
        b_g = sem("b_gelu_done")
        b_xb = sem("b_residual_with_bias")
        rb = Ring([("t1", "A"), ("m0", "D"), ("m1", "D"), ("t2", "A"), ("m2", "D")], (0, 1, 2, 3, 4),
                  sem("b_bank_filled"), sem("b_bank_read_by_scalar"), sem("b_bank_read_by_vector"))
        c_ctx = sem("c_context_loaded")
        c_vm8 = sem("c_mask_loaded")
        c_vm = sem("c_mask_bias_ready")
        c_var = sem("c_variance_ready")
        c_rstd = sem("c_inverse_deviation")
        c_step = sem("c_vector_step")
        c_z = sem("c_normed")
        c_S = sem("c_scores_ready")
        c_top = sem("c_top_values")
        c_nm = sem("c_maximum_scaled")
        c_E = sem("c_exponentials")
        c_P = sem("c_kept_probs")
        c_r = sem("c_row_factors")
        c_dg = sem("c_diagonals")
        c_x1 = sem("c_modulated")
        c_xd = sem("c_skip_term")
        c_Y = sem("c_spectrum_ready")
        c_h2 = sem("c_ffn_input")
        c_gl = sem("c_gelu_done")
        c_hh = sem("c_hidden_high_part")
        c_hl = sem("c_hidden_split")
        c_xo = sem("c_residual_updated")
        rc = Ring([("c0", "AD"), ("c1", "AD"), ("z", "AD"), ("q", "A"), ("k", "D"), ("v0", "A"), ("v1", "A"),
                   ("at", "A"), ("ct", "AD"), ("fi", "D"), ("fo", "D"), ("ab", "D"), ("y", "D"), ("h", "AD"),
                   ("m0", "A"), ("m1", "A"), ("m2", "D")], (0, 1), sem("c_bank_filled"), sem("c_bank_read_by_scalar"),
                  sem("c_bank_read_by_vector"))
        s_kf = sem("kernel_spectrum_filled")
        s_kr = sem("kernel_spectrum_kept")
        e_var = sem("e_variance_ready")
        e_rstd = sem("e_inverse_deviation")
        e_step = sem("e_vector_step")
        e_z = sem("e_normed")
        e_tr = sem("e_transposed")
        e_zh = sem("e_tokens_high_part")
        e_zl = sem("e_tokens_split")
        e_zc = sem("e_tokens_copied")
        e_lg = sem("e_logits_ready")
        e_lb = sem("e_logits_biased")
        e_sg = sem("e_gates_ready")
        e_cw = sem("e_gate_weights")
        e_wd = [sem("e_gate_loaded"), sem("e_up_loaded"), sem("e_down_loaded")]
        e_wh = sem("e_expert_weights_high_part")
        e_wl = sem("e_expert_weights_split")
        e_gu = sem("e_gate_up_filled")
        e_si = sem("e_silu_done")
        e_h = sem("e_hidden_ready")
        e_hh = sem("e_hidden_high_part")
        e_hl = sem("e_hidden_split")
        e_o = sem("e_down_filled")
        e_oa = sem("e_down_added")
        s_out = sem("output_written")

        def wait_apart(eng, semaphore, count):
            if not isinstance(count, int):
                eng.lower_val(count)
            eng.wait_ge(s_x, 16)
            eng.wait_ge(semaphore, count)

        block = ctx.enter_context(nc.Block())

        @block.sync
        def _(sp):
            sp.dma_start(X, t["x"].rearrange("b t d -> t b d")).then_inc(s_x, 16)
            for dst, src in consts:
                sp.dma_start(dst, src).then_inc(s_const, 16)
            for k in range(NW):
                if k >= 2:
                    sp.wait_ge(s_lo, k - 1)
                name = splits[k][0] if k < NSPL else quants[k - NSPL][0]
                parts, a, b = splits[k][1:4] if k < NSPL else (128,) + quants[k - NSPL][1:3]
                sp.dma_start(staged(k, parts, a, b), kview(name, a)).then_inc(s_stage[k % 2], 16)
            with sp.Fori(0, NB) as b:
                ra_need = b * ra.n - (ra.n - ra.names.index("c1") - 1)
                sp.wait_ge(a_S, b * H0)
                sp.dma_start(ctx_sb, t["ctx_768"][b].rearrange("(j p) c -> p j c", p=GC)).then_inc(a_ctx, 16)
            with sp.Fori(0, NB) as b:
                sp.wait_ge(c_S, b * H1)
                sp.wait_ge(rb.dve, NB * rb.nd)
                sp.dma_start(ctx_c, t["ctx_768"][b].rearrange("(j p) c -> p j c", p=GC)).then_inc(c_ctx, 16)
                sp.dma_start(vm8, t["mask_BxS2_bf1"][b].partition_broadcast(128)).then_inc(c_vm8, 16)
            sp.wait_ge(c_xo, NB)
            for e in range(NEXP):
                if e >= 1:
                    sp.wait_ge(e_wl, 3 * e)
                sp.dma_start(estage[:, 0, :].rearrange("p (k n) -> p k n", k=2),
                             t["e_gate"][e].rearrange("(k p) n -> p k n", p=128)).then_inc(e_wd[0], 16)
                sp.dma_start(estage[:, 1, :].rearrange("p (k n) -> p k n", k=2),
                             t["e_up"][e].rearrange("(k p) n -> p k n", p=128)).then_inc(e_wd[1], 16)
                sp.dma_start(estage[:, 2, :].rearrange("p (k n) -> p k n", k=4),
                             t["e_down"][e].rearrange("(k p) n -> p k n", p=128)).then_inc(e_wd[2], 16)
            sp.wait_ge(e_oa, NEXP * NB)
            sp.dma_start(out.rearrange("b t d -> t b d"), X).then_inc(s_out, 16)
            sp.wait_ge(s_out, 16)

        @block.tensor
        def _(pe):
            mm = nc.tensor.matmul

            def mm3(o, lh, rh, first, last):
                mm(o, lh[0], rh[0], start=first, stop=False)
                mm(o, lh[0], rh[1], start=False, stop=False)
                return mm(o, lh[1], rh[0], start=False, stop=last)

            def part(p, *ix):
                return p[0][ix], p[1][ix]

            A = slice(None)
            for k in range(2):
                pe.wait_ge(s_dset, 1 + k)
                pe.wait_ge(s_pmisc, 1)
                mm(bank(6 + k, 128, 1), ones_f, wab[:, k:k + 1], start=True, stop=True).then_inc(s_wsum, 1)
            pe.wait_ge(s_lo, NW)

            with pe.Fori(0, NB) as b:
                pe.wait_ge(a_ctx, b * 16 + 16)
                for k in range(2):
                    n = f"c{k}"
                    ra.wait_free(pe, b, n)
                    for j in range(GJ):
                        i = nc.tensor.transpose(bank(ra.bank[n], CK, GC, j * GC), ctx_sb[:, j, k * CK:(k + 1) * CK],
                                                identf[0:GC, 0:GC])
                    i.then_inc(ra.full, 1)
                pe.wait_ge(a_xn, b + 1)
                ra.wait_free(pe, b, "xn")
                for k in range(2):
                    i = nc.tensor.transpose(bank(ra.bank["xn"], 128, T, k * T), xn[:, k * 128:(k + 1) * 128],
                                            identf[0:T, 0:T])
                i.then_inc(ra.full, 1)
                ra.wait_emptied(pe, b, "xn")
                for q in range(2):
                    ra.wait_free(pe, b, f"q{q}")
                    for m in range(4):
                        for k in range(2):
                            c = (q * 4 + m) * 128
                            i = mm3(bank(ra.bank[f"q{q}"], 128, T, m * T), part(wq, A, k, slice(c, c + 128)),
                                    part(xT, A, k, A), k == 0, k == 1)
                    i.then_inc(ra.full, 1)
                for m in range(8):
                    ra.wait_free(pe, b, f"k{m}")
                    for k in range(2):
                        i = mm3(bank(ra.bank[f"k{m}"], 128, G), part(wk, A, k, slice(m * 128, m * 128 + 128)),
                                part(cT, A, k, A), k == 0, k == 1)
                    i.then_inc(ra.full, 1)
                for m in range(6):
                    j, hf_ = m // 2, m % 2
                    ra.wait_free(pe, b, f"v{m}")
                    for k in range(2):
                        i = mm3(bank(ra.bank[f"v{m}"], GC, 512), part(cT, A, k, slice(j * GC, j * GC + GC)),
                                part(wv, A, k, slice(hf_ * 512, hf_ * 512 + 512)), k == 0, k == 1)
                    i.then_inc(ra.full, 1)

                def scores(h):
                    r = 64 * (h % 2)
                    mm(bank(2 + h % 2, T, G), qT[r:r + 64, h // 2, :], kT[r:r + 64, h // 2, :], start=True,
                       stop=True).then_inc(a_S, 1)

                def pv(h):
                    pe.wait_ge((a_pd, a_pa)[h % 2], b * 8 + h // 2 + 1)
                    for j in range(GJ):
                        i = mm(bank(6 + h // 8, T, DH0, (h % 8) * DH0), PTs[:, h % 2, j * T:(j + 1) * T],
                               V[:, j, h * DH0:(h + 1) * DH0], start=(j == 0), stop=(j == GJ - 1))
                    if h % 8 == 7:
                        i.then_inc(a_O, 1)

                ra.wait_emptied(pe, b, "k6")
                ra.wait_emptied(pe, b, "k7")
                scores(0)
                scores(1)
                ra.wait_emptied(pe, b, "v4")
                ra.wait_emptied(pe, b, "v5")
                for h in range(H0):
                    pe.wait_ge(a_E, b * H0 + h + 1)
                    for j in range(GJ):
                        i = nc.tensor.transpose(bank(4 + h % 2, GC, T, j * T), Pr[:, h % 2, j * GC:(j + 1) * GC],
                                                identf[0:T, 0:T])
                    i.then_inc(a_pt, 1)
                    if h + 2 < H0:
                        scores(h + 2)
                    if h >= 1:
                        pv(h - 1)
                pv(H0 - 1)
                for q in range(2):
                    n = f"o{q}"
                    pe.wait_ge(a_On, b * 2 + q + 1)
                    ra.wait_free(pe, b, n)
                    for m in range(4):
                        c = (q * 4 + m) * 128
                        i = nc.tensor.transpose(bank(ra.bank[n], 128, T, m * T), On[:, c:c + 128], identf[0:T, 0:T])
                    i.then_inc(ra.full, 1)
                ra.wait_emptied(pe, b, "o0")
                ra.wait_free(pe, b, "wo")
                for m in range(8):
                    if m == 4:
                        ra.wait_emptied(pe, b, "o1")
                    i = mm3(bank(ra.bank["wo"], T, D), part(aT, A, m, A), part(wo, A, m, A), m == 0, m == 7)
                i.then_inc(ra.full, 1)

            pe.wait_ge(ra.dve, NB * ra.nd)
            with pe.Fori(0, NB) as b:
                pe.wait_ge(b_q, b * 2 + 1)
                rb.wait_free(pe, b, "t1")
                for k in range(2):
                    i = nc.tensor.transpose(bank16(0, 128, 2 * T)[:, k * T:(k + 1) * T], q1[:, k * 128:(k + 1) * 128],
                                            identb[0:T, 0:T])
                i.then_inc(rb.full, 1)
                rb.wait_emptied(pe, b, "t1")
                for m in range(2):
                    rb.wait_free(pe, b, f"m{m}")
                    for k in range(2):
                        i = mm(bank(1 + m, T, 512), hq1[:, k, :], w1q[:, k, m * 512:(m + 1) * 512], start=(k == 0),
                               stop=(k == 1))
                    i.then_inc(rb.full, 1)
                pe.wait_ge(b_q, b * 2 + 2)
                rb.wait_free(pe, b, "t2")
                for k in range(8):
                    i = nc.tensor.transpose(bank16(3, 128, 8 * T)[:, k * T:(k + 1) * T], q2[:, k * 128:(k + 1) * 128],
                                            identb[0:T, 0:T])
                i.then_inc(rb.full, 1)
                rb.wait_emptied(pe, b, "t2")
                rb.wait_free(pe, b, "m2")
                for k in range(8):
                    i = mm(bank(4, T, D), hq2[:, k, :], w2q[:, k, :], start=(k == 0), stop=(k == 7))
                i.then_inc(rb.full, 1)

            pe.wait_ge(s_s4p, S4P_ALL)
            pe.wait_ge(rb.dve, NB * rb.nd)
            for h in range(2):
                i = nc.tensor.transpose(bank(7, T, 128, h * 128), kpow[:, h, :], identf)
            i.then_inc(s_kf, 1)
            pe.wait_ge(s_kr, 1)
            for q in range(2):
                for m in range(2):
                    i = mm(bank(6 - q, T, D, m * D), dft[:, 4 + q * 2 + m, :], kt, start=True, stop=True)
                i.then_inc(s_kf, 1)

            with pe.Fori(0, NB) as b:
                pe.wait_ge(c_ctx, b * 16 + 16)
                for k in range(2):
                    n = f"c{k}"
                    rc.wait_free(pe, b, n)
                    for j in range(GJ):
                        i = nc.tensor.transpose(bank(rc.bank[n], CK, GC, j * GC), ctx_c[:, j, k * CK:(k + 1) * CK],
                                                identf[0:GC, 0:GC])
                    i.then_inc(rc.full, 1)
                pe.wait_ge(c_z, b + 1)
                rc.wait_free(pe, b, "z")
                for k in range(2):
                    i = nc.tensor.transpose(bank(rc.bank["z"], 128, T, k * T), z[:, k * 128:(k + 1) * 128],
                                            identf[0:T, 0:T])
                i.then_inc(rc.full, 1)
                rc.wait_emptied(pe, b, "z")
                rc.wait_free(pe, b, "q")
                for k in range(2):
                    i = mm3(bank(rc.bank["q"], 128, T), part(uq, A, k, A), part(zT, A, k, A), k == 0, k == 1)
                i.then_inc(rc.full, 1)
                rc.wait_free(pe, b, "k")
                for k in range(2):
                    i = mm3(bank(rc.bank["k"], 128, G), part(uk, A, k, A), part(cTc, A, k, A), k == 0, k == 1)
                i.then_inc(rc.full, 1)
                for n, js in (("v0", (0, 1)), ("v1", (2,))):
                    rc.wait_free(pe, b, n)
                    for j in js:
                        for k in range(2):
                            i = mm3(bank(rc.bank[n], GC, D, (j % 2) * D), part(cTc, A, k, slice(j * GC, j * GC + GC)),
                                    part(uv, A, k, A), k == 0, k == 1)
                    i.then_inc(rc.full, 1)
                rc.wait_emptied(pe, b, "q")
                rc.wait_emptied(pe, b, "k")
                pe.wait_ge(c_vm, b + 1)
                for h in range(H1):
                    r = 32 * h
                    mm(bank(2 + h, T, G), ones_b[r:r + 1, :], vmb[r:r + 1, :], start=True, stop=False)
                    mm(bank(2 + h, T, G), q1T[r:r + 32, :], k1T[r:r + 32, :], start=False,
                       stop=True).then_inc(c_S, 1)
                rc.wait_free(pe, b, "at")
                for j in range(GJ):
                    for h in range(H1):
                        if j == 0:
                            pe.wait_ge(c_dg, b * H1 + h + 1)
                        i = mm(bank(rc.bank["at"], GC, T, j * T), P1[:, h, j * GC:(j + 1) * GC], dg[:, h, :],
                               start=(h == 0), stop=(h == H1 - 1))
                i.then_inc(rc.full, 1)
                rc.wait_emptied(pe, b, "at")
                rc.wait_emptied(pe, b, "v1")
                rc.wait_free(pe, b, "ct")
                for m in range(2):
                    for j in range(GJ):
                        i = mm(bank(rc.bank["ct"], 128, T, m * T), V1[:, j, m * 128:(m + 1) * 128],
                               atT[:, j * T:(j + 1) * T], start=(j == 0), stop=(j == GJ - 1))
                i.then_inc(rc.full, 1)
                rc.wait_emptied(pe, b, "ct")
                for n, u in (("fi", ufi), ("fo", ufo)):
                    rc.wait_free(pe, b, n)
                    for k in range(2):
                        i = mm3(bank(rc.bank[n], T, 2 * D), part(ctT, A, k, A), part(u, A, k, A), k == 0, k == 1)
                    i.then_inc(rc.full, 1)
                pe.wait_ge(c_x1, b + 1)
                rc.wait_free(pe, b, "ab")
                for m in range(2):
                    i = mm(bank(rc.bank["ab"], T, D, m * D), dft[:, m, :], x1, start=True, stop=True)
                i.then_inc(rc.full, 1)
                pe.wait_ge(c_Y, b * 2 + 2)
                rc.wait_free(pe, b, "y")
                for m in range(2):
                    i = mm(bank(rc.bank["y"], T, D), dft[:, 2 + m, :], Y[:, m * D:(m + 1) * D], start=(m == 0),
                           stop=(m == 1))
                i.then_inc(rc.full, 1)
                pe.wait_ge(c_h2, b + 1)
                rc.wait_free(pe, b, "h")
                for k in range(2):
                    i = nc.tensor.transpose(bank(rc.bank["h"], 128, T, k * T), h2[:, k * 128:(k + 1) * 128],
                                            identf[0:T, 0:T])
                i.then_inc(rc.full, 1)
                rc.wait_emptied(pe, b, "h")
                for q in range(2):
                    rc.wait_free(pe, b, f"m{q}")
                    for m in range(4):
                        for k in range(2):
                            c = (q * 4 + m) * 128
                            i = mm3(bank(rc.bank[f"m{q}"], 128, T, m * T), part(u1, A, k, slice(c, c + 128)),
                                    part(h2T, A, k, A), k == 0, k == 1)
                    i.then_inc(rc.full, 1)
                pe.wait_ge(c_hl, b + 1)
                rc.wait_free(pe, b, "m2")
                for m in range(8):
                    i = mm3(bank(rc.bank["m2"], T, D), part(hidT, A, m, A), part(u2, A, m, A), m == 0, m == 7)
                i.then_inc(rc.full, 1)

            with pe.Fori(0, NB) as b:
                pe.wait_ge(e_z, b + 1)
                for k in range(2):
                    i = nc.tensor.transpose(bank(0, 128, T, k * T), ze[:, k * 128:(k + 1) * 128], identf[0:T, 0:T])
                i.then_inc(e_tr, 1)
                pe.wait_ge(e_zl, b + 1)
                for k in range(2):
                    i = mm3(bank(1, T, 8), part(zt_t, A, k, A), part((wr_hi, wr_lo), A, k, A), k == 0, k == 1)
                i.then_inc(e_lg, 1)
            pe.wait_ge(e_zc, 2 * NB)

            def expert(e, f):
                def gate_up(c):
                    tok = slice(c * CH, (c + 1) * CH)
                    for i4 in range(4):
                        n = (e * NCH + c) * 4 + i4
                        cs = slice(i4 * 128, i4 * 128 + 128)
                        pe.wait_ge(e_h, n - 1) if not isinstance(n, int) or n >= 2 else None
                        for k in range(2):
                            mm3(bank(2 * (i4 % 2), 128, CH), part(eg[f], A, k, cs), part(ZT, A, k, tok), k == 0, k == 1)
                        for k in range(2):
                            i = mm3(bank(2 * (i4 % 2) + 1, 128, CH), part(eu[f], A, k, cs), part(ZT, A, k, tok), k == 0,
                                    k == 1)
                        i.then_inc(e_gu, 1)

                def down(c):
                    for s in range(CHB):
                        n = (e * NCH + c) * CHB + s
                        if s == 0:
                            pe.wait_ge(e_hl, ((e * NCH + c) + 1) * 4)
                        pe.wait_ge(e_oa, n - 3) if not isinstance(n, int) or n >= 4 else None
                        for m in range(4):
                            i = mm3(bank(4 + s, T, D), part(hT[c % 2], A, m, slice(s * T, s * T + T)),
                                    part(ed[f], A, m, A), m == 0, m == 3)
                        i.then_inc(e_o, 1)

                pe.wait_ge(e_wl, e * 3 + 3)
                gate_up(0)
                for c in range(1, NCH):
                    gate_up(c)
                    down(c - 1)
                down(NCH - 1)

            expert(0, 0)
            with pe.Fori(0, (NEXP - 1) // 2) as g:
                expert(g * 2 + 1, 1)
                expert(g * 2 + 2, 0)

        @block.scalar
        def _(act):
            def copy(o, i, scale=1.0):
                return nc.scalar.activation(o, i, ACT.Copy, scale=scale)

            act.wait_ge(s_const, 16 * NCONST)
            copy(identb, identf).then_inc(s_misc, 1)
            copy(wr_hi, wr_f, WS).then_inc(s_misc, 1)
            copy(tmask, tmask8).then_inc(s_misc, 1)
            for k in range(NSPL):
                act.wait_ge(s_stage[k % 2], 16 * (k // 2 + 1))
                _, parts, a, b_, (hi, lo) = splits[k]
                copy(hi, staged(k, parts, a, b_), WS).then_inc(s_hi, 1)
            nc.scalar.activation(dtc, ldt, ACT.Exp).then_inc(s_s4a, 1)
            act.wait_ge(s_s4v, S4_RE)
            nc.scalar.activation(s4["th"], s4["re"], ACT.Tanh, scale=0.5).then_inc(s_s4a, 1)
            act.wait_ge(s_s4v, S4_ANG)
            nc.scalar.activation(s4["s"], s4["k"], ACT.Sin).then_inc(s_s4a, 1)
            nc.scalar.activation(s4["sh"], s4["k"], ACT.Sin, scale=0.5).then_inc(s_s4a, 1)

            def keep(ring, i, name, dst, src, scale=1.0):
                ring.wait_full(act, i, name)
                copy(dst, src, scale).then_inc(ring.act, 1)

            with act.Fori(0, NB) as b:
                for k in range(2):
                    keep(ra, b, f"c{k}", cT[0][:, k, :], bank(ra.bank[f"c{k}"], CK, G))
                keep(ra, b, "xn", xT[0], bank(ra.bank["xn"], 128, 2 * T).rearrange("p (k t) -> p k t", k=2))
                for q in range(2):
                    keep(ra, b, f"q{q}", qT[:, q * 4:q * 4 + 4, :],
                         bank(ra.bank[f"q{q}"], 128, 4 * T).rearrange("p (m t) -> p m t", m=4), IWS * DH0 ** -0.5)
                for m in range(1, 8, 2):
                    keep(ra, b, f"k{m}", kT[:, m, :], bank(ra.bank[f"k{m}"], 128, G), IWS)
                for m in range(1, 6, 2):
                    keep(ra, b, f"v{m}", V[:, m // 2, 512:1024], bank(ra.bank[f"v{m}"], GC, 512), IWS)

                def exp(h):
                    act.wait_ge(a_mx, b * H0 + h + 1)
                    act.wait_ge(a_pt, b * H0 + h - 1) if h >= 2 else None
                    nc.scalar.activation(Pr[:, h % 2, :], bank(2 + h % 2, T, G), ACT.Exp, bias=nmx[:, h:h + 1],
                                         accum_out=rsum[:, h:h + 1]).then_inc(a_E, 1)

                exp(0)
                exp(1)
                for h in range(H0):
                    if h % 2:
                        act.wait_ge(a_pt, b * H0 + h + 1)
                        copy(PTs[:, 1, :], bank(5, GC, GJ * T)).then_inc(a_pa, 1)
                    if h + 2 < H0:
                        exp(h + 2)
                for q in range(2):
                    keep(ra, b, f"o{q}", aT[0][:, q * 4:q * 4 + 4, :],
                         bank(ra.bank[f"o{q}"], 128, 4 * T).rearrange("p (m t) -> p m t", m=4))

            with act.Fori(0, NB) as b:
                keep(rb, b, "t1", hq1, bank16(0, 128, 2 * T).rearrange("p (k t) -> p k t", k=2))
                for m in range(2):
                    rb.wait_dve(act, b, f"m{m}")
                    u = ub[:, m * 512:(m + 1) * 512]
                    nc.scalar.activation(u, u, ACT.Gelu).then_inc(b_g, 1)
                keep(rb, b, "t2", hq2, bank16(3, 128, 8 * T).rearrange("p (k t) -> p k t", k=8))

            act.wait_ge(s_kf, 1)
            copy(kt, bank(7, T, D)).then_inc(s_kr, 1)
            for q in range(2):
                act.wait_ge(s_kf, 2 + q)
                copy(coef[:, q * 2:q * 2 + 2, :], bank(6 - q, T, 2 * D).rearrange("p (m d) -> p m d", m=2)).then_inc(s_kr, 1)

            with act.Fori(0, NB) as b:
                for k in range(2):
                    keep(rc, b, f"c{k}", cTc[0][:, k, :], bank(rc.bank[f"c{k}"], CK, G))
                keep(rc, b, "z", zT[0], bank(rc.bank["z"], 128, 2 * T).rearrange("p (k t) -> p k t", k=2))
                keep(rc, b, "q", q1T, bank(rc.bank["q"], 128, T), IWS)
                keep(rc, b, "v0", V1[:, 0:2, :], bank(rc.bank["v0"], GC, 2 * D).rearrange("p (j d) -> p j d", j=2), IWS)
                keep(rc, b, "v1", V1[:, 2, :], bank(rc.bank["v1"], GC, D), IWS)
                for h in range(H1):
                    act.wait_ge(c_nm, b * H1 + h + 1)
                    nc.scalar.activation(E1[:, h, :], bank(2 + h, T, G), ACT.Exp, bias=nmx1[:, h:h + 1],
                                         scale=DH1 ** -0.5).then_inc(c_E, 1)
                keep(rc, b, "at", atT, bank(rc.bank["at"], GC, GJ * T))
                keep(rc, b, "ct", ctT[0], bank(rc.bank["ct"], 128, 2 * T).rearrange("p (k t) -> p k t", k=2))
                keep(rc, b, "h", h2T[0], bank(rc.bank["h"], 128, 2 * T).rearrange("p (k t) -> p k t", k=2))
                for q in range(2):
                    rc.wait_full(act, b, f"m{q}")
                    for m in range(4):
                        i = nc.scalar.activation(hid[:, q * 4 + m, :], bank(rc.bank[f"m{q}"], 128, T, m * T), ACT.Gelu,
                                                 bias=b1col[:, q * 4 + m:q * 4 + m + 1], scale=IWS)
                    i.then_inc(rc.act, 1)
                rc.wait_act(act, b, "m1")
                copy(hidT[0], hid).then_inc(c_hh, 1)

            with act.Fori(0, NB) as b:
                act.wait_ge(e_tr, b + 1)
                act.wait_ge(e_zc, b * 2)
                copy(zt_t[0], bank(0, 128, 2 * T).rearrange("p (k t) -> p k t", k=2)).then_inc(e_zh, 1)
                act.wait_ge(e_lb, b + 1)
                nc.scalar.activation(pr[:, 0:8], lg, ACT.Sigmoid).then_inc(e_sg, 1)

            def expert_weights(e, f):
                for k, dst in enumerate((eg[f][0], eu[f][0], ed[f][0])):
                    act.wait_ge(e_wd[k], (e + 1) * 16)
                    copy(dst, estage[:, k, :].rearrange("p (a b) -> p a b", a=(2, 2, 4)[k]), WS).then_inc(e_wh, 1)

            def expert(e, f, ahead):
                for c in range(NCH):
                    for i4 in range(4):
                        n = (e * NCH + c) * 4 + i4
                        act.wait_ge(e_gu, n + 1)
                        act.wait_ge(e_h, n - 1) if not isinstance(n, int) or n >= 2 else None
                        nc.scalar.activation(sg[:, i4 % 2, :], bank(2 * (i4 % 2), 128, CH), ACT.Silu,
                                             scale=IWS).then_inc(e_si, 1)
                        act.wait_ge(e_h, n + 1)
                        if i4 == 0:
                            k = (e * NCH + c) * CHB
                            act.wait_ge(e_o, k - CHB) if not isinstance(k, int) or k >= 2 * CHB else None
                        copy(hT[c % 2][0][:, i4, :], hf[:, i4 % 2, :]).then_inc(e_hh, 1)
                    if c == 1 and ahead:
                        act.wait_ge(e_o, e * NB)
                        expert_weights(e + 1, 1 - f)

            act.wait_ge(c_xo, NB)
            expert_weights(0, 0)
            expert(0, 0, True)
            with act.Fori(0, (NEXP - 1) // 2 - 1) as g:
                expert(g * 2 + 1, 1, True)
                expert(g * 2 + 2, 0, True)
            expert(NEXP - 2, 1, True)
            expert(NEXP - 1, 0, False)

        @block.gpsimd
        def _(pool):
            def tt(o, a, b, op):
                return nc.gpsimd.tensor_tensor(o, a, b, op)

            nc.gpsimd.memset(ones_f, 1.0).then_inc(s_pmisc, 1)
            nc.gpsimd.memset(ones_b, 1.0).then_inc(s_pmisc, 1)
            nc.gpsimd.memset(neghalf, -0.5).then_inc(s_pmisc, 1)
            pool.wait_ge(s_pmisc, 3)
            pool.wait_ge(s_x, 16)
            pool.wait_ge(s_const, 16 * NCONST)

            def rsqrt(var_sem, rstd_sem, n):
                pool.wait_ge(var_sem, n + 1)
                tt(rstd, ve, neghalf, ALU.pow).then_inc(rstd_sem, 1)

            def s4d_kernel():
                pool.wait_ge(s_s4v, S4V_ALL)
                with pool.Fori(0, 2) as h:
                    n = [0]

                    def link(ins):
                        n[0] += 1
                        ins.then_inc(s_s4p, 1)
                        pool.wait_ge(s_s4p, h * S4P_HALF + n[0])

                    def cmul(o, a, c, m):
                        cr_, ci_ = (x.to_broadcast([128, m, NST]) for x in c)
                        f1, f2 = p1[:, 0:m, :], p2[:, 0:m, :]
                        link(tt(f1, a[0], cr_, ALU.mult))
                        link(tt(f2, a[1], ci_, ALU.mult))
                        link(tt(o[0], f1, f2, ALU.subtract))
                        link(tt(f1, a[0], ci_, ALU.mult))
                        link(tt(f2, a[1], cr_, ALU.mult))
                        link(tt(o[1], f1, f2, ALU.add))

                    def at(p, lo, hi):
                        return p[0][:, lo:hi, :], p[1][:, lo:hi, :]

                    v, u = (vr, vi), (ur, ui)
                    nc.gpsimd.memset(vr[:, 0, :], 1.0)
                    link(nc.gpsimd.memset(vi[:, 0, :], 0.0))
                    link(nc.gpsimd.tensor_copy(vr[:, 1, :], s4["zr"][:, h, :]))
                    link(nc.gpsimd.tensor_copy(vi[:, 1, :], s4["zi"][:, h, :]))
                    link(nc.gpsimd.tensor_copy(ur[:, 0, :], s4["dr"][:, h, :]))
                    link(nc.gpsimd.tensor_copy(ui[:, 0, :], s4["di"][:, h, :]))
                    for m in (1, 2, 4, 8):
                        cmul(at(v, m + 1, 2 * m + 1), at(v, 1, m + 1), at(v, m, m + 1), m)
                    z16 = at(v, PBS, PBS + 1)
                    cmul(at(u, 1, 2), at(u, 0, 1), z16, 1)
                    cmul(at(u, 2, 3), at(u, 1, 2), z16, 1)
                    cmul(at(u, 3, 4), at(u, 2, 3), z16, 1)
                    cmul(at(u, 4, 5), at(u, 3, 4), z16, 1)
                    cmul(at(u, 5, 6), at(u, 4, 5), z16, 1)
                    cmul(at(u, 6, 7), at(u, 5, 6), z16, 1)
                    for a in range(PA):
                        link(tt(p1, vr[:, 0:PBS, :], ur[:, a:a + 1, :].to_broadcast([128, PBS, NST]), ALU.mult))
                        link(tt(p2, vi[:, 0:PBS, :], ui[:, a:a + 1, :].to_broadcast([128, PBS, NST]), ALU.mult))
                        link(tt(p1, p1, p2, ALU.subtract))
                        m = NST // 2
                        while m >= 2:
                            src, dst = (p1, p2) if (NST // 2 // m) in (1, 4, 16) else (p2, p1)
                            link(tt(dst[:, :, 0:m], src[:, :, 0:m], src[:, :, m:2 * m], ALU.add))
                            m //= 2
                        src = p2
                        link(tt(kpow[:, h, a * PBS:(a + 1) * PBS].rearrange("p (b o) -> p b o", o=1),
                                src[:, :, 0:1], src[:, :, 1:2], ALU.add))
                    assert n[0] == S4P_HALF, n[0]

            with pool.Fori(0, NB) as b:
                rsqrt(a_var, a_rstd, b)
                pool.wait_ge(ra.dve, b * ra.nd)
                tt(xb, X[:, b, :], bo_r, ALU.add).then_inc(a_xb, 1)
            s4d_kernel()
            with pool.Fori(0, NB) as b:
                rsqrt(b_var, b_rstd, b * 3)
                rsqrt(b_var, b_rstd, b * 3 + 1)
                pool.wait_ge(rb.dve, b * rb.nd)
                tt(xb2, X[:, b, :], b2_r, ALU.add).then_inc(b_xb, 1)
                rsqrt(b_var, b_rstd, b * 3 + 2)
            with pool.Fori(0, NB) as b:
                wait_apart(pool, c_vm8, b * 16 + 16)
                wait_apart(pool, c_S, b * H1)
                nc.gpsimd.tensor_scalar(vmb, vm8, MASKED, -MASKED, ALU.mult, ALU.add).then_inc(c_vm, 1)
                rsqrt(c_var, c_rstd, b * 4)
                rsqrt(c_var, c_rstd, b * 4 + 1)
                for h in range(H1):
                    wait_apart(pool, c_r, b * H1 + h + 1)
                    nc.gpsimd.tensor_scalar(dg[:, h, :], identf[0:T, 0:T], r2[:, h:h + 1], 1.0, ALU.mult,
                                            ALU.mult).then_inc(c_dg, 1)
                pool.wait_ge(c_x1, b + 1)
                tt(xd, x1, dsk_r, ALU.mult).then_inc(c_xd, 1)
                rsqrt(c_var, c_rstd, b * 4 + 2)
                rsqrt(c_var, c_rstd, b * 4 + 3)
            with pool.Fori(0, NB) as b:
                rsqrt(e_var, e_rstd, b)
                pool.wait_ge(e_zl, b + 1)
                for k in range(2):
                    nc.gpsimd.tensor_copy(ZT[k][:, :, bass.ds(b * T, T)], zt_t[k]).then_inc(e_zc, 1)

        @block.vector
        def _(dve):
            V_ = nc.vector

            def ts(o, i, a, b, op0, op1=None):
                return V_.tensor_scalar(o, i, a, b, op0, op1) if op1 is not None else V_.tensor_scalar(o, i, a, None, op0)

            def tt(o, a, b, op):
                return V_.tensor_tensor(o, a, b, op)

            def stt(o, a, s, b, op0, op1, **kw):
                return V_.scalar_tensor_tensor(o, a, s, b, op0, op1, **kw)

            n_set = [0]

            def linkset(ins):
                n_set[0] += 1
                ins.then_inc(s_dset, 1)
                dve.wait_ge(s_dset, n_set[0])

            dve.wait_ge(s_const, 16 * NCONST)
            for k in range(NSPL):
                _, parts, a, b_, (hi, lo) = splits[k]
                dve.wait_ge(s_hi, k + 1)
                stt(lo, staged(k, parts, a, b_), WS, hi, ALU.mult, ALU.subtract).then_inc(s_lo, 1)
            for k in range(2):
                dve.wait_ge(s_stage[(NSPL + k) % 2], 16 * ((NSPL + k) // 2 + 1))
                src = stage[:, (NSPL + k) % 2, :]
                linkset(V_.tensor_reduce(wab[:, k:k + 1], src, AX_X, ALU.add, apply_absolute_value=True))
                if k == 0:
                    continue
            for k in range(2):
                name, a, b_, dst = quants[k]
                src = stage[:, (NSPL + k) % 2, :]
                dve.wait_ge(s_wsum, k + 1)
                linkset(ts(wmean[:, k:k + 1], bank(6 + k, 128, 1), 1.0 / (a * b_ * 128), EPS, ALU.mult, ALU.max))
                linkset(V_.reciprocal(wsc[:, k:k + 1], wmean[:, k:k + 1]))
                linkset(ts(src, src, wsc[:, k:k + 1], 1.0, ALU.mult, ALU.min))
                linkset(ts(src, src, -1.0, MAGIC, ALU.max, ALU.add))
                ts(dst, src.rearrange("p (a b) -> p a b", a=a), -MAGIC, None, ALU.add).then_inc(s_lo, 1)
            dve.wait_ge(s_misc, 3)
            linkset(ts(mbi, mbi, mg, None, ALU.mult))
            linkset(ts(mbo, mbo, mg, None, ALU.mult))
            linkset(ts(mbi[:, 0:D], mbi[:, 0:D], 1.0, None, ALU.add))
            linkset(ts(mbo[:, 0:D], mbo[:, 0:D], 1.0, None, ALU.add))
            linkset(ts(mgs, mg, IWS, None, ALU.mult))
            linkset(stt(wr_lo, wr_f, WS, wr_hi, ALU.mult, ALU.subtract))

            n4 = [0]

            def link4(ins):
                n4[0] += 1
                ins.then_inc(s_s4v, 1)
                dve.wait_ge(s_s4v, n4[0])

            f = s4
            dve.wait_ge(s_s4a, 1)
            dtb = dtc.rearrange("p (h o) -> p h o", o=1).to_broadcast([128, 2, NST])
            link4(tt(f["re"], f["ar"], dtb, ALU.mult))
            link4(tt(f["im"], f["ai"], dtb, ALU.mult))
            assert S4_RE == 1
            link4(ts(f["t1"], f["im"], 1.0 / TWO_PI, MAGIC, ALU.mult, ALU.add))
            link4(ts(f["t1"], f["t1"], -MAGIC, None, ALU.add))
            link4(stt(f["k"], f["t1"], -TP1, f["im"], ALU.mult, ALU.add))
            link4(stt(f["k"], f["t1"], -TP2, f["k"], ALU.mult, ALU.add))
            link4(stt(f["k"], f["t1"], -TP3, f["k"], ALU.mult, ALU.add))
            link4(ts(f["k"], f["k"], 3.1415925, -3.1415925, ALU.min, ALU.max))
            assert n4[0] == S4_ANG
            dve.wait_ge(s_s4a, 4)
            link4(ts(f["t1"], f["th"], -1.0, 1.0, ALU.mult, ALU.add))
            link4(V_.reciprocal(f["t2"], f["t1"]))
            link4(stt(f["e1"], f["th"], 2.0, f["t2"], ALU.mult, ALU.mult))
            link4(stt(f["t2"], f["sh"], -2.0, f["sh"], ALU.mult, ALU.mult))
            link4(ts(f["re"], f["e1"], 1.0, None, ALU.add))
            link4(ts(f["im"], f["t2"], 1.0, None, ALU.add))
            link4(tt(f["zr"], f["re"], f["im"], ALU.mult))
            link4(tt(f["zi"], f["re"], f["s"], ALU.mult))
            link4(tt(f["t1"], f["e1"], f["im"], ALU.mult))
            link4(tt(f["mr"], f["t1"], f["t2"], ALU.add))
            link4(tt(f["t1"], f["ar"], f["ar"], ALU.mult))
            link4(tt(f["t2"], f["ai"], f["ai"], ALU.mult))
            link4(tt(f["t1"], f["t1"], f["t2"], ALU.add))
            link4(V_.reciprocal(f["e1"], f["t1"]))
            link4(tt(f["t1"], f["mr"], f["ar"], ALU.mult))
            link4(tt(f["t2"], f["zi"], f["ai"], ALU.mult))
            link4(tt(f["re"], f["t1"], f["t2"], ALU.add))
            link4(tt(f["t1"], f["zi"], f["ar"], ALU.mult))
            link4(tt(f["t2"], f["mr"], f["ai"], ALU.mult))
            link4(tt(f["im"], f["t1"], f["t2"], ALU.subtract))
            link4(stt(f["re"], f["re"], 2.0, f["e1"], ALU.mult, ALU.mult))
            link4(stt(f["im"], f["im"], 2.0, f["e1"], ALU.mult, ALU.mult))
            link4(tt(f["t1"], f["cr"], f["re"], ALU.mult))
            link4(tt(f["t2"], f["ci"], f["im"], ALU.mult))
            link4(tt(f["dr"], f["t1"], f["t2"], ALU.subtract))
            link4(tt(f["t1"], f["cr"], f["im"], ALU.mult))
            link4(tt(f["t2"], f["ci"], f["re"], ALU.mult))
            link4(tt(f["di"], f["t1"], f["t2"], ALU.add))
            assert n4[0] == S4V_ALL, n4[0]

            def layer_norm(link, var_sem, rstd_sem, n, dst, src, width=D):
                for c in range(0, width, 512):
                    e = min(width, c + 512)
                    link(V_.bn_stats(st[:, c // 512, :], src[:, c:e]), hold=(e == width))
                k = (width + 511) // 512
                link(V_.bn_aggr(mv, st[:, 0:k, :]))
                ts(ve, mv[:, 1:2], EPS, None, ALU.add).then_inc(var_sem, 1)
                dve.wait_ge(rstd_sem, n + 1)
                return ts(dst, src, mv[:, 0:1], rstd, ALU.subtract, ALU.mult)

            class Link:
                def __init__(self, s, per):
                    self.s, self.per, self.n = s, per, 0

                def at(self, i):
                    self.i, self.n = i, 0
                    return self

                def __call__(self, ins, hold=False):
                    self.n += 1
                    ins.then_inc(self.s, 1)
                    (wait_apart if hold else type(dve).wait_ge)(dve, self.s, self.i * self.per + self.n)

                def done(self):
                    assert self.n == self.per, self.n

            def split_low(ring, i, name, lo, hi, src):
                ring.wait_act(dve, i, name)
                tt(lo, src, hi, ALU.subtract).then_inc(ring.dve, 1)

            link = Link(a_step, 3)
            dve.wait_ge(s_x, 16)
            with dve.Fori(0, NB) as b:
                link.at(b)
                layer_norm(link, a_var, a_rstd, b, xn, X[:, b, :]).then_inc(a_xn, 1)
                for k in range(2):
                    split_low(ra, b, f"c{k}", cT[1][:, k, :], cT[0][:, k, :], bank(ra.bank[f"c{k}"], CK, G))
                split_low(ra, b, "xn", xT[1], xT[0], bank(ra.bank["xn"], 128, 2 * T).rearrange("p (k t) -> p k t", k=2))
                for m in range(0, 8, 2):
                    ra.wait_full(dve, b, f"k{m}")
                    ts(kT[:, m, :], bank(ra.bank[f"k{m}"], 128, G), IWS, None, ALU.mult).then_inc(ra.dve, 1)
                for m in range(0, 6, 2):
                    ra.wait_full(dve, b, f"v{m}")
                    ts(V[:, m // 2, 0:512], bank(ra.bank[f"v{m}"], GC, 512), IWS, None, ALU.mult).then_inc(ra.dve, 1)

                def row_max(h):
                    dve.wait_ge(a_S, b * H0 + h + 1)
                    V_.tensor_reduce(nmx[:, h:h + 1], bank(2 + h % 2, T, G), AX_X, ALU.max, negate=True).then_inc(a_mx, 1)

                row_max(0)
                row_max(1)
                for h in range(H0):
                    if h % 2 == 0:
                        dve.wait_ge(a_pt, b * H0 + h + 1)
                        V_.tensor_copy(PTs[:, 0, :], bank(4, GC, GJ * T)).then_inc(a_pd, 1)
                    if h + 2 < H0:
                        row_max(h + 2)
                dve.wait_ge(a_E, b * H0 + H0)
                link(V_.reciprocal(rinv, rsum))
                for q in range(2):
                    dve.wait_ge(a_O, b * 2 + q + 1)
                    tt(On[:, q * 512:(q + 1) * 512].rearrange("p (h e) -> p h e", h=8),
                       bank(6 + q, T, 512).rearrange("p (h e) -> p h e", h=8),
                       rinv[:, q * 8:q * 8 + 8].rearrange("p (h o) -> p h o", o=1).to_broadcast([T, 8, DH0]),
                       ALU.mult).then_inc(a_On, 1)
                for q in range(2):
                    split_low(ra, b, f"o{q}", aT[1][:, q * 4:q * 4 + 4, :], aT[0][:, q * 4:q * 4 + 4, :],
                              bank(ra.bank[f"o{q}"], 128, 4 * T).rearrange("p (m t) -> p m t", m=4))
                ra.wait_full(dve, b, "wo")
                dve.wait_ge(a_xb, b + 1)
                stt(X[:, b, :], bank(ra.bank["wo"], T, D), IWS, xb, ALU.mult, ALU.add).then_inc(ra.dve, 1)
                link.done()

            def quantize(link, dst, src, qf, dq, wm):
                link(V_.tensor_reduce(amax, src, AX_X, ALU.max, apply_absolute_value=True))
                link(ts(amc, amax, EPS, None, ALU.max))
                link(V_.reciprocal(rcp, amc))
                link(ts(qsc, rcp, 127.0, None, ALU.mult))
                link(ts(dq, amc, wm, 1.0 / 127.0, ALU.mult, ALU.mult))
                link(ts(qf, src, qsc, MAGIC, ALU.mult, ALU.add))
                ts(dst, qf, -MAGIC, 127.0, ALU.add, ALU.min).then_inc(b_q, 1)

            link = Link(b_step, 26)
            dve.wait_ge(ra.dve, NB * ra.nd)
            with dve.Fori(0, NB) as b:
                link.at(b)
                link(layer_norm(link, b_var, b_rstd, b * 3, zb, X[:, b, :]))
                link(layer_norm(link, b_var, b_rstd, b * 3 + 1, hb, zb))
                link(tt(hb, hb, g1_r, ALU.mult))
                link(tt(hb, hb, h1_r, ALU.add))
                quantize(link, q1, hb, hb, dq1, wmean[0:T, 0:1])
                for m in range(2):
                    rb.wait_full(dve, b, f"m{m}")
                    cs = slice(m * 512, (m + 1) * 512)
                    stt(ub[:, cs], bank(1 + m, T, 512), dq1, b1row[:, cs], ALU.mult, ALU.add).then_inc(rb.dve, 1)
                dve.wait_ge(b_g, b * 2 + 2)
                link(layer_norm(link, b_var, b_rstd, b * 3 + 2, ub, ub, HID))
                link(tt(ub, ub, g2row, ALU.mult))
                link(tt(ub, ub, h2row, ALU.add))
                quantize(link, q2, ub, ub, dq2, wmean[0:T, 1:2])
                rb.wait_full(dve, b, "m2")
                dve.wait_ge(b_xb, b + 1)
                stt(X[:, b, :], bank(4, T, D), dq2, xb2, ALU.mult, ALU.add).then_inc(rb.dve, 1)
                link.done()

            link = Link(c_step, C_LINKS)
            dve.wait_ge(rb.dve, NB * rb.nd)
            dve.wait_ge(s_kr, 3)
            with dve.Fori(0, NB) as b:
                link.at(b)
                layer_norm(link, c_var, c_rstd, b * 4, z, X[:, b, :]).then_inc(c_z, 1)
                dve.wait_ge(c_z, b + 1)
                for k in range(2):
                    split_low(rc, b, f"c{k}", cTc[1][:, k, :], cTc[0][:, k, :], bank(rc.bank[f"c{k}"], CK, G))
                split_low(rc, b, "z", zT[1], zT[0], bank(rc.bank["z"], 128, 2 * T).rearrange("p (k t) -> p k t", k=2))
                rc.wait_full(dve, b, "k")
                ts(k1T, bank(rc.bank["k"], 128, G), IWS, None, ALU.mult).then_inc(rc.dve, 1)
                link(layer_norm(link, c_var, c_rstd, b * 4 + 1, x1, z))
                link(tt(x1, x1, gi_r, ALU.mult))
                link(tt(x1, x1, hi_r, ALU.add), hold=True)
                for h in range(H1):
                    S = bank(2 + h, T, G)
                    R = R1[:, h % 2, :]
                    wait_apart(dve, c_S, b * H1 + h + 1)
                    for r in range(4):
                        src = S if r == 0 else R
                        m8 = top8[:, h % 2, r, :]
                        V_.max(m8, src).then_inc(c_top, 1)
                        if r:
                            wait_apart(dve, c_top, (b * H1 + h) * 4 + r + 1)
                        else:
                            dve.wait_ge(c_top, (b * H1 + h) * 4 + r + 1)
                        if r == 0:
                            link(ts(nmx1[:, h:h + 1], m8[:, 0:1], -(DH1 ** -0.5), None, ALU.mult), hold=True)
                            V_.match_replace(R, m8, src, NEG).then_inc(c_nm, 1)
                            wait_apart(dve, c_nm, b * H1 + h + 1)
                        else:
                            link(V_.match_replace(R, m8, src, NEG), hold=(r < 3))
                    dve.wait_ge(c_E, b * H1 + h + 1)
                    link(stt(P1[:, h, :], R, 0.9 * NEG, E1[:, h, :], ALU.is_lt, ALU.mult, accum_out=sum1[:, h:h + 1]))
                    link(V_.reciprocal(r1[:, h:h + 1], sum1[:, h:h + 1]))
                    ts(r2[:, h:h + 1], r1[:, h:h + 1], tmask[:, bass.ds(b, 1)], 1.0 / H1, ALU.mult,
                       ALU.mult).then_inc(c_r, 1)
                split_low(rc, b, "ct", ctT[1], ctT[0], bank(rc.bank["ct"], 128, 2 * T).rearrange("p (k t) -> p k t", k=2))
                rc.wait_full(dve, b, "fi")
                stt(mi, bank(rc.bank["fi"], T, 2 * D), mgs, mbi, ALU.mult, ALU.add).then_inc(rc.dve, 1)
                rc.wait_dve(dve, b, "fi")
                link(tt(x1, x1, mi[:, 0:D], ALU.mult))
                tt(x1, x1, mi[:, D:2 * D], ALU.add).then_inc(c_x1, 1)
                rc.wait_full(dve, b, "fo")
                stt(mo, bank(rc.bank["fo"], T, 2 * D), mgs, mbo, ALU.mult, ALU.add).then_inc(rc.dve, 1)
                rc.wait_full(dve, b, "ab")
                ab = bank(rc.bank["ab"], T, 2 * D)
                link(tt(t1, ab, coef[:, 0:2, :].rearrange("p m d -> p (m d)"), ALU.mult))
                tt(t2, ab, coef[:, 2:4, :].rearrange("p m d -> p (m d)"), ALU.mult).then_inc(rc.dve, 1)
                rc.wait_dve(dve, b, "ab")
                tt(Y[:, 0:D], t1[:, 0:D], t2[:, D:2 * D], ALU.add).then_inc(c_Y, 1)
                tt(Y[:, D:2 * D], t1[:, D:2 * D], t2[:, 0:D], ALU.add).then_inc(c_Y, 1)
                rc.wait_full(dve, b, "y")
                dve.wait_ge(c_xd, b + 1)
                tt(y, bank(rc.bank["y"], T, D), xd, ALU.add).then_inc(rc.dve, 1)
                rc.wait_dve(dve, b, "y")
                link(tt(y, y, mo[:, 0:D], ALU.mult))
                link(tt(y, y, mo[:, D:2 * D], ALU.add))
                link(tt(z, z, y, ALU.add))
                link(layer_norm(link, c_var, c_rstd, b * 4 + 2, y, z))
                link(tt(y, y, gf_r, ALU.mult))
                tt(h2, y, hf_r, ALU.add).then_inc(c_h2, 1)
                split_low(rc, b, "h", h2T[1], h2T[0], bank(rc.bank["h"], 128, 2 * T).rearrange("p (k t) -> p k t", k=2))
                link(tt(z, z, c2_r, ALU.add))
                dve.wait_ge(c_hh, b + 1)
                tt(hidT[1], hid, hidT[0], ALU.subtract).then_inc(c_hl, 1)
                rc.wait_full(dve, b, "m2")
                stt(z, bank(rc.bank["m2"], T, D), IWS, z, ALU.mult, ALU.add).then_inc(rc.dve, 1)
                rc.wait_dve(dve, b, "m2")
                link(layer_norm(link, c_var, c_rstd, b * 4 + 3, y, z))
                link(tt(y, y, go_r, ALU.mult))
                link(tt(y, y, ho_r, ALU.add))
                tt(X[:, b, :], X[:, b, :], y, ALU.add).then_inc(c_xo, 1)
                link.done()

            link = Link(e_step, E_LINKS)
            dve.wait_ge(c_xo, NB)
            V_.memset(pr[:, 8:16], -1.0)
            V_.memset(pin[:, 2:8], -1.0)
            V_.memset(cw[:, :, 0:1], IWS)
            with dve.Fori(0, NB) as b:
                link.at(b)
                layer_norm(link, e_var, e_rstd, b, ze, X[:, b, :]).then_inc(e_z, 1)
                dve.wait_ge(e_zh, b + 1)
                tt(zt_t[1], bank(0, 128, 2 * T).rearrange("p (k t) -> p k t", k=2), zt_t[0], ALU.subtract).then_inc(e_zl, 1)
                dve.wait_ge(e_lg, b + 1)
                stt(lg, bank(1, T, 8), IWS, rbrow, ALU.mult, ALU.add).then_inc(e_lb, 1)
                wait_apart(dve, e_sg, b + 1)
                link(V_.max(pm8, pr))
                link(V_.tensor_copy(pin[:, 0:2], pm8[:, 0:2]), hold=True)
                link(V_.match_replace(prr, pin, pr, -2.0))
                link(tt(pne, pr[:, 0:8], prr[:, 0:8], ALU.not_equal))
                stt(cw[:, b, 1:9], pne, IWS, pr[:, 0:8], ALU.mult, ALU.mult).then_inc(e_cw, 1)
                link.done()

            def expert_weights(e, f):
                for k, (hi, lo) in enumerate((eg[f], eu[f], ed[f])):
                    dve.wait_ge(e_wh, e * 3 + k + 1)
                    stt(lo, estage[:, k, :].rearrange("p (a b) -> p a b", a=(2, 2, 4)[k]), WS, hi, ALU.mult,
                        ALU.subtract).then_inc(e_wl, 1)

            def expert(e, f, ahead):
                def combine(c):
                    for s in range(CHB):
                        bb = c * CHB + s
                        n = (e * NCH + c) * CHB + s
                        dve.wait_ge(e_o, n + 1)
                        dve.wait_ge(e_oa, n - NB + 1) if not isinstance(n, int) or n >= NB else None
                        stt(X[:, bb, :], bank(4 + s, T, D), cw[:, bb, bass.ds(e, 1)], X[:, bb, :], ALU.mult,
                            ALU.add).then_inc(e_oa, 1)

                for c in range(NCH):
                    for i4 in range(4):
                        n = (e * NCH + c) * 4 + i4
                        dve.wait_ge(e_si, n + 1)
                        dve.wait_ge(e_hl, n - 1) if not isinstance(n, int) or n >= 2 else None
                        stt(hf[:, i4 % 2, :], bank(2 * (i4 % 2) + 1, 128, CH), IWS, sg[:, i4 % 2, :], ALU.mult,
                            ALU.mult).then_inc(e_h, 1)
                        dve.wait_ge(e_hh, n + 1)
                        tt(hT[c % 2][1][:, i4, :], hf[:, i4 % 2, :], hT[c % 2][0][:, i4, :],
                           ALU.subtract).then_inc(e_hl, 1)
                    if c == 1 and ahead:
                        expert_weights(e + 1, 1 - f)
                    if c >= 1:
                        combine(c - 1)
                combine(NCH - 1)

            dve.wait_ge(e_cw, NB)
            expert_weights(0, 0)
            expert(0, 0, True)
            with dve.Fori(0, (NEXP - 1) // 2 - 1) as g:
                expert(g * 2 + 1, 1, True)
                expert(g * 2 + 2, 0, True)
            expert(NEXP - 2, 1, True)
            expert(NEXP - 1, 0, False)


S4_RE = 1
S4_ANG = 8
S4V_ALL = 36
S4P_HALF = 5 + 6 * 10 + 9 * PA
S4P_ALL = 2 * S4P_HALF
C_LINKS = 46
E_LINKS = 6


def _constants():
    n = 2 * T
    k = np.arange(T)
    ang = 2.0 * np.pi * (np.outer(k, k) % n) / n
    sign = (-1.0) ** k
    fa, fb = np.cos(ang), -np.sin(ang)
    fb = fb.copy()
    fb[:, 0] = sign
    scale = np.where(k == 0, 1.0, 2.0)[:, None] / n
    ia = scale * np.cos(ang)
    ib = -scale * np.sin(ang)
    ib[0] = sign / n
    m1 = np.cos(ang)
    m4 = np.cos(ang).copy()
    m4[:, 0] = sign
    m3 = -np.sin(ang)
    m3[:, 0] = 0.0
    m2 = -m3
    dft = np.stack([fa, fb, ia, ib, m1, m4, m3, m2]).astype(np.float32)
    return dft, np.eye(128, dtype=np.float32)


def kernel(**inputs):
    import numpy as _np
    import concourse.bacc as _bacc
    from concourse import mybir as _mybir
    from concourse.bass_utils import run_bass_kernel_spmd as _run

    nc = _bacc.Bacc("TRN2", target_bir_lowering=False, num_devices=1)
    data = {}
    for name, a in inputs.items():
        a = _np.asarray(a)
        if a.dtype == _np.bool_:
            a = a.view(_np.uint8)
        data[name] = a
    data["L1_xattn_mod_gate"] = data["L1_xattn_mod_gate"].reshape(1)
    data["L1_xattn_b1"] = data["L1_xattn_b1"].reshape(8, 128).T
    data["L1_xattn_log_dt"] = data["L1_xattn_log_dt"].reshape(2, 128).T
    for name in ("L0_ffn_w1", "L0_ffn_w2", "L1_ffn_Wr", "mask_BxS_bf1"):
        data[name] = data[name].T
    for new, shared, routed in (("e_gate", "L1_ffn_Wg_s", "L1_ffn_Wg"), ("e_up", "L1_ffn_Wu_s", "L1_ffn_Wu"),
                                ("e_down", "L1_ffn_Wd_s", "L1_ffn_Wd")):
        both = _np.concatenate([data.pop(shared)[None], data.pop(routed)])
        data[new] = both.transpose(0, 2, 1)
    data["dft"], data["ident"] = _constants()
    arrays, args = {}, {}
    for name, a in data.items():
        a = _np.ascontiguousarray(a)
        arrays[f"in_{name}_dram"] = a
        args[name] = nc.dram_tensor(f"in_{name}_dram", a.shape, _mybir.dt.from_np(a.dtype), kind="ExternalInput").ap()
    out = nc.dram_tensor("out_0_dram", (NB, T, D), F32, kind="ExternalOutput").ap()
    build(nc, args, out)
    r = _run(nc, [arrays], core_ids=[0])
    return r.results[0]["out_0_dram"]
```

```python
from contextlib import ExitStack

import numpy as np

import concourse.bass as bass
from concourse import mybir

ALU = mybir.AluOpType
ACT = mybir.ActivationFunctionType
F32 = mybir.dt.float32
F16 = mybir.dt.float16
BF16 = mybir.dt.bfloat16
U8 = mybir.dt.uint8
AX_X = mybir.AxisListType.X

NB, T, D = 16, 112, 256
G, DC = 375, 192
GJ, GC = 3, 125
CK = DC // 2
H0, DH0, IN0 = 16, 64, 1024
H1, DH1 = 4, 32
HID = 1024
NEXP, EI = 9, 512
NST = 64
PA, PBS = 7, 16
KR = 3
CHB = 4
CH = CHB * T
NCH = NB // CHB
WS = 256.0
IWS = 1.0 / WS
MAGIC = 12582912.0
EPS = 1e-5
NEG = -3.0e38
MASKED = 1.0e30
TWO_PI = 6.283185307179586
TP1 = 6.28125
TP2 = float(np.float32(TWO_PI - TP1))
TP3 = float(TWO_PI - TP1 - TP2)


class Ring:

    def __init__(self, items, banks, full, act, dve):
        self.names = [n for n, _ in items]
        self.who = dict(items)
        self.bank = {n: banks[k % len(banks)] for k, n in enumerate(self.names)}
        self.full, self.act, self.dve = full, act, dve
        self.n = len(items)
        self.na = sum("A" in w for _, w in items)
        self.nd = sum("D" in w for _, w in items)

    def upto(self, name, letter):
        k = self.names.index(name)
        return sum(letter in self.who[m] for m in self.names[: k + 1])

    def wait_full(self, eng, i, name):
        eng.wait_ge(self.full, i * self.n + self.names.index(name) + 1)

    def wait_act(self, eng, i, name):
        eng.wait_ge(self.act, i * self.na + self.upto(name, "A"))

    def wait_dve(self, eng, i, name):
        eng.wait_ge(self.dve, i * self.nd + self.upto(name, "D"))

    def wait_emptied(self, eng, i, name):
        if "D" in self.who[name]:
            self.wait_dve(eng, i, name)
        else:
            self.wait_act(eng, i, name)

    def wait_free(self, pe, i, name):
        k = self.names.index(name)
        before = [m for m in self.names[:k] if self.bank[m] == self.bank[name]]
        if before:
            self.wait_emptied(pe, i, before[-1])
            return
        last = [m for m in self.names if self.bank[m] == self.bank[name]][-1]
        if isinstance(i, int) and i == 0:
            return
        self.wait_emptied(pe, i - 1, last)


def build(nc, t, out):
    with ExitStack() as ctx:
        def sem(name):
            return ctx.enter_context(nc.semaphore(name))

        SB = 207 * 1024
        arena = ctx.enter_context(nc.sbuf_tensor("arena", [128, SB], U8))
        top = [0]

        def carve(parts, shape, dt, at=None):
            n = int(np.prod(shape)) * {F32: 4, F16: 2, BF16: 2, U8: 1}[dt]
            start = top[0] if at is None else at[0]
            end = start + (n + 31) // 32 * 32
            if at is None:
                top[0] = end
            else:
                at[0] = end
            assert end <= SB, (end, SB)
            v = arena[0:parts, start:start + n].bitcast(dt)
            if len(shape) == 2:
                v = v.rearrange("p (a b) -> p a b", a=shape[0])
            elif len(shape) == 3:
                v = v.rearrange("p (a b c) -> p a b c", a=shape[0], b=shape[1])
            return v

        psum = ctx.enter_context(nc.psum_tensor("psum", [128, 8, 512], F32))

        def bank(k, parts, n, off=0):
            return psum[0:parts, k, off:off + n]

        def bank16(k, parts, n):
            return psum[0:parts, k, :].bitcast(BF16)[:, 0:n]

        X = carve(T, (NB, D), F32)
        identf = carve(128, (128,), F32)
        identb = carve(128, (128,), BF16)
        neghalf = carve(T, (1,), F32)
        ones_b = carve(128, (T,), BF16)
        ones_f = carve(128, (128,), F32)
        st = carve(T, (2, 6), F32)
        mv = carve(T, (2,), F32)
        ve = carve(T, (1,), F32)
        rstd = carve(T, (1,), F32)
        amax = carve(T, (1,), F32)
        amc = carve(T, (1,), F32)
        rcp = carve(T, (1,), F32)
        qsc = carve(T, (1,), F32)
        dq1 = carve(T, (1,), F32)
        dq2 = carve(T, (1,), F32)
        cw = carve(T, (NB, NEXP), F32)
        rbrow = carve(T, (8,), F32)
        wr_f = carve(128, (2, 8), F32)
        wr_hi = carve(128, (2, 8), F16)
        wr_lo = carve(128, (2, 8), F16)
        kept = top[0]

        def pair(parts, shape):
            return carve(parts, shape, F16), carve(parts, shape, F16)

        wq = pair(128, (2, IN0))
        wk = pair(CK, (2, IN0))
        wv = pair(CK, (2, IN0))
        wo = pair(128, (8, D))
        w1q = carve(128, (2, HID), BF16)
        w2q = carve(128, (8, D), BF16)
        uq = pair(128, (2, 128))
        uk = pair(CK, (2, 128))
        uv = pair(CK, (2, D))
        ufi = pair(128, (2, 2 * D))
        ufo = pair(128, (2, 2 * D))
        u1 = pair(128, (2, HID))
        u2 = pair(128, (8, D))
        dft = carve(T, (8, T), F32)
        coef = carve(T, (4, D), F32)
        b1row = carve(T, (HID,), F32)
        g2row = carve(T, (HID,), F32)
        h2row = carve(T, (HID,), F32)
        rows = carve(T, (12, D), F32)
        (bo_r, g1_r, h1_r, b2_r, gi_r, hi_r, go_r, ho_r, gf_r, hf_r, dsk_r, c2_r) = (rows[:, k, :] for k in range(12))
        mbi = carve(T, (2 * D,), F32)
        mbo = carve(T, (2 * D,), F32)
        b1col = carve(128, (8,), F32)
        mg = carve(T, (1,), F32)
        mgs = carve(T, (1,), F32)
        tmask8 = carve(T, (NB,), U8)
        tmask = carve(T, (NB,), F32)
        wmean = carve(128, (2,), F32)
        wsc = carve(128, (2,), F32)
        wab = carve(128, (2,), F32)
        ldt = carve(128, (2,), F32)
        dtc = carve(128, (2,), F32)
        kpow = carve(128, (2, T), F32)
        kt = carve(T, (D,), F32)
        work = top[0]

        ctx_sb = carve(GC, (GJ, DC), F32)
        cT = pair(CK, (2, G))
        xn = carve(T, (D,), F32)
        xT = pair(128, (2, T))
        qT = carve(128, (8, T), F32)
        kT = carve(128, (KR, G), F32)
        V = carve(GC, (GJ, IN0), F32)
        Pr = carve(T, (2, G), F32)
        PTs = carve(GC, (2, GJ * T), F32)
        nmx = carve(T, (H0,), F32)
        rsum = carve(T, (H0,), F32)
        rinv = carve(T, (H0,), F32)
        On = carve(T, (512,), F32)
        aT = pair(128, (8, T))
        zb = carve(T, (D,), F32)
        q1 = carve(T, (D,), BF16)
        hq1 = carve(128, (2, T), BF16)
        ub = carve(T, (HID,), F32)
        q2 = carve(T, (HID,), BF16)
        hq2 = carve(128, (8, T), BF16)
        work = top[0]
        cTc = pair(CK, (2, G))
        zn = carve(T, (D,), F32)
        zT = pair(128, (2, T))
        q1T = carve(128, (T,), F32)
        k1T = carve(128, (G,), F32)
        V1 = carve(GC, (GJ, D), F32)
        vm8 = carve(128, (G,), U8)
        vmb = carve(128, (G,), BF16)
        z = carve(T, (D,), F32)
        work_c = top[0]
        top8 = carve(T, (2, 4, 8), F32)
        nmx1 = carve(T, (H1,), F32)
        R1 = carve(T, (G,), F32)
        later = [top[0]]
        P1 = carve(T, (H1, G), F32)
        hidT = carve(128, (8, T), F16, later), carve(128, (8, T), F16, later)
        h2T = carve(128, (2, T), F16, later), carve(128, (2, T), F16, later)
        h2 = carve(T, (D,), F32, later)
        assert later[0] <= top[0]
        sum1 = carve(T, (H1,), F32)
        r1 = carve(T, (H1,), F32)
        r2 = carve(T, (H1,), F32)
        dg = carve(T, (H1, T), F32)
        atT = carve(GC, (GJ * T,), F32)
        ctT = pair(128, (2, T))
        mi = carve(T, (2 * D,), F32)
        Y = mi
        mo = carve(T, (2 * D,), F32)
        x1 = carve(T, (D,), F32)
        y = x1
        xd = carve(T, (D,), F32)
        later = [top[0]]
        t1 = carve(T, (2 * D,), F32)
        t2 = carve(T, (2 * D,), F32)
        hid = carve(128, (8, T), F32, later)
        assert later[0] <= top[0]
        assert top[0] <= SB
        w = [work]
        stage = [carve(128, (2048,), F32, w)]
        assert w[0] <= work_c
        w = [work_c]
        s4 = {n: carve(128, (2, NST), F32, w) for n in ("zr", "zi", "dr", "di")}
        dead = w[0]
        s4.update({n: carve(128, (2, NST), F32, w) for n in
                   ("ar", "ai", "cr", "ci", "re", "im", "th", "k", "s", "sh", "e1", "mr", "t1", "t2")})
        w = [dead]
        p1 = carve(128, (PBS, NST), F32, w)
        p2 = carve(128, (PBS, NST), F32, w)
        vr = carve(128, (PBS + 1, NST), F32, w)
        vi = carve(128, (PBS + 1, NST), F32, w)
        ur = carve(128, (PA, NST), F32, w)
        ui = carve(128, (PA, NST), F32, w)
        assert w[0] <= SB
        stage.append(arena[0:128, SB - 8192:SB].bitcast(F32))
        w = [kept]
        ZT = carve(128, (2, NB * T), F16, w), carve(128, (2, NB * T), F16, w)
        ze = carve(T, (D,), F32, w)
        zt_t = carve(128, (2, T), F16, w), carve(128, (2, T), F16, w)
        pr = carve(T, (16,), F32, w)
        pm8 = carve(T, (8,), F32, w)
        pin = carve(T, (8,), F32, w)
        prr = carve(T, (16,), F32, w)
        pne = carve(T, (8,), F32, w)
        lg = carve(T, (8,), F32, w)
        estage = carve(128, (3, 1024), F32, w)
        eg = [(carve(128, (2, EI), F16, w), carve(128, (2, EI), F16, w)) for _ in range(2)]
        eu = [(carve(128, (2, EI), F16, w), carve(128, (2, EI), F16, w)) for _ in range(2)]
        ed = [(carve(128, (4, D), F16, w), carve(128, (4, D), F16, w)) for _ in range(2)]
        sg = carve(128, (2, CH), F32, w)
        hf = carve(128, (2, CH), F32, w)
        hT = [(carve(128, (4, CH), F16, w), carve(128, (4, CH), F16, w)) for _ in range(2)]

        s_x = sem("x_loaded")
        s_const = sem("constants_loaded")
        s_stage = [sem("weight_staged_even"), sem("weight_staged_odd")]
        s_hi = sem("weight_high_part")
        s_lo = sem("weight_done")
        s_wab = sem("weight_rows_summed")
        s_wsum = sem("weight_magnitude_summed")
        s_misc = sem("small_constants_ready")
        s_pmisc = sem("pool_constants_ready")
        s_dset = sem("vector_setup_step")
        s_s4a = sem("s4d_activation")
        s_s4v = sem("s4d_vector_step")
        s_s4p = sem("s4d_pool_step")
        s_s4h = sem("s4d_half_loaded")

        consts = []
        for k, n in enumerate(("L0_xattn_bo", "L0_ffn_ln1_g", "L0_ffn_ln1_b", "L0_ffn_b2", "L1_xattn_g_norm_in",
                               "L1_xattn_b_norm_in", "L1_xattn_g_norm_out", "L1_xattn_b_norm_out", "L1_xattn_g_ffn",
                               "L1_xattn_b_ffn", "L1_xattn_D_skip", "L1_xattn_b2")):
            consts.append((rows[:, k, :], t[n].partition_broadcast(T)))
        consts += [(b1row, t["L0_ffn_b1"].partition_broadcast(T)), (g2row, t["L0_ffn_ln2_g"].partition_broadcast(T)),
                   (h2row, t["L0_ffn_ln2_b"].partition_broadcast(T)),
                   (mbi, t["L1_xattn_b_film_in"].partition_broadcast(T)),
                   (mbo, t["L1_xattn_b_film_out"].partition_broadcast(T)),
                   (b1col, t["L1_xattn_b1"]),
                   (mg, t["L1_xattn_mod_gate"].partition_broadcast(T)),
                   (rbrow, t["L1_ffn_rb"].partition_broadcast(T)),
                   (tmask8, t["mask_BxS_bf1"]),
                   (wr_f, t["L1_ffn_Wr"].rearrange("(k p) e -> p k e", p=128)),
                   (dft, t["dft"].rearrange("m p k -> p m k")),
                   (identf, t["ident"]),
                   (ldt, t["L1_xattn_log_dt"])]
        for n, k in (("L1_xattn_A_re", "ar"), ("L1_xattn_A_im", "ai"), ("L1_xattn_C_re", "cr"), ("L1_xattn_C_im", "ci")):
            consts.append((s4[k], t[n].rearrange("(h p) n -> p h n", p=128)))
        NCONST = len(consts)

        def kview(name, k):
            return t[name].rearrange("(k p) n -> p k n", k=k)

        splits = [("L0_xattn_Wq", 128, 2, IN0, wq), ("L0_xattn_Wk", CK, 2, IN0, wk), ("L0_xattn_Wv", CK, 2, IN0, wv),
                  ("L0_xattn_Wo", 128, 8, D, wo),
                  ("L1_xattn_Wq", 128, 2, 128, uq), ("L1_xattn_Wk", CK, 2, 128, uk), ("L1_xattn_Wv", CK, 2, D, uv),
                  ("L1_xattn_W_film_in", 128, 2, 2 * D, ufi), ("L1_xattn_W_film_out", 128, 2, 2 * D, ufo),
                  ("L1_xattn_W1", 128, 2, HID, u1), ("L1_xattn_W2", 128, 8, D, u2)]
        quants = [("L0_ffn_w1", 128, 2, HID, w1q), ("L0_ffn_w2", 128, 8, D, w2q)]
        NSPL = len(splits)
        NW = NSPL + len(quants)

        NFIRST = 4

        def staged(k, parts, a, b):
            return stage[k % 2 if k < NFIRST else 0][0:parts, 0:a * b].rearrange("p (a b) -> p a b", a=a)

        def s_staged(k):
            return s_stage[k % 2 if k < NFIRST else 0], 16 * (k // 2 + 1 if k < NFIRST else NFIRST // 2 + k - NFIRST + 1)

        weights = splits[:NFIRST] + quants + splits[NFIRST:]

        s_ctx = sem("context_loaded")
        a_var = sem("a_variance_ready")
        a_rstd = sem("a_inverse_deviation")
        a_step = sem("a_vector_step")
        a_xn = sem("a_normed")
        a_xb = sem("a_bias_added")
        a_S = sem("a_scores_ready")
        a_mx = sem("a_maximum_ready")
        a_E = sem("a_probs_ready")
        a_pt = sem("a_probs_transposed")
        a_pk = sem("a_transposed_kept")
        a_O = sem("a_head_outputs_ready")
        a_ri = sem("a_sums_inverted")
        a_On = sem("a_outputs_normed")
        ra = Ring([("c0", "AD"), ("c1", "AD"), ("xn", "AD"), ("q0", "A"), ("q1", "A"), ("k0", "A"), ("v0", "A"),
                   ("v1", "A"), ("v2", "A"), ("k1", "A"), ("k2", "A"), ("v3", "A"), ("k3", "A"), ("v4", "A"),
                   ("k4", "A"), ("v5", "A"), ("k5", "A"), ("k6", "A"), ("o0", "AD"), ("k7", "A"), ("o1", "AD"),
                   ("wo", "D")], (0, 1), sem("a_bank_filled"), sem("a_bank_read_by_scalar"),
                  sem("a_bank_read_by_vector"))
        b_var = sem("b_variance_ready")
        b_rstd = sem("b_inverse_deviation")
        b_step = sem("b_vector_step")
        b_z = sem("b_normed")
        b_xb = sem("b_bias_added")
        b_q = sem("b_quantized")
        b_g = sem("b_gelu_done")
        rb = Ring([("t1", "A"), ("m0", "D"), ("m1", "D"), ("t2", "A"), ("m2", "D")], (2,),
                  sem("b_bank_filled"), sem("b_bank_read_by_scalar"), sem("b_bank_read_by_vector"))
        d_vm8 = sem("d_mask_loaded")
        d_vm = sem("d_mask_bias_ready")
        d_var = sem("d_variance_ready")
        d_rstd = sem("d_inverse_deviation")
        d_step = sem("d_vector_step")
        d_zn = sem("d_normed")
        rd = Ring([("c0", "AD"), ("c1", "AD"), ("z", "AD"), ("q", "A"), ("k", "A"), ("v0", "A"), ("v1", "A")], (2,),
                  sem("d_bank_filled"), sem("d_bank_read_by_scalar"), sem("d_bank_read_by_vector"))
        c_z = sem("c_normed_copied")
        c_var = sem("c_variance_ready")
        c_rstd = sem("c_inverse_deviation")
        c_step = sem("c_vector_step")
        c_S = sem("c_scores_ready")
        c_top = sem("c_top_values")
        c_nm = sem("c_maximum_scaled")
        c_E = sem("c_exponentials")
        c_r = sem("c_row_factors")
        c_dg = sem("c_diagonals")
        c_x1 = sem("c_modulated")
        c_xd = sem("c_skip_term")
        c_Y = sem("c_spectrum_ready")
        c_h2 = sem("c_ffn_input")
        c_hh = sem("c_hidden_high_part")
        c_hl = sem("c_hidden_split")
        c_xo = sem("c_residual_updated")
        rc = Ring([("at", "A"), ("ct", "AD"), ("fi", "D"), ("fo", "D"), ("ab", "D"), ("y", "D"), ("h", "AD"),
                   ("m0", "A"), ("m1", "A"), ("m2", "D")], (2,), sem("c_bank_filled"), sem("c_bank_read_by_scalar"),
                  sem("c_bank_read_by_vector"))
        rings = {"B": (rb, 1), "C": (rc, 2), "D": (rd, 1)}
        ORDER = [("B", "t1"), ("B", "m0"), ("B", "m1"), ("B", "t2"), ("B", "m2"), ("C", "at"), ("C", "ct"), ("C", "fi"),
                 ("C", "fo"), ("C", "ab"), ("C", "y"), ("D", "c0"), ("D", "c1"), ("D", "z"), ("C", "h"), ("D", "q"),
                 ("C", "m0"), ("C", "m1"), ("D", "k"), ("D", "v0"), ("D", "v1"), ("C", "m2")]

        def wait_bank2(pe, i, stage, name):
            here = ORDER.index((stage, name))
            for back, upto in ((0, here), (1, len(ORDER))):
                for st_, n in reversed(ORDER[:upto]):
                    ring, lag = rings[st_]
                    j = i - lag - back
                    if isinstance(i, int) and not 0 <= j < NB:
                        continue
                    ring.wait_emptied(pe, j, n)
                    return

        s_kf = sem("kernel_spectrum_filled")
        s_kr = sem("kernel_spectrum_kept")
        s_s4c = sem("s4d_contracted")
        s_s4d = sem("s4d_contraction_step")
        e_var = sem("e_variance_ready")
        e_rstd = sem("e_inverse_deviation")
        e_step = sem("e_vector_step")
        e_z = sem("e_normed")
        e_tr = sem("e_transposed")
        e_zh = sem("e_tokens_high_part")
        e_zl = sem("e_tokens_split")
        e_zc = sem("e_tokens_copied")
        e_lg = sem("e_logits_ready")
        e_lb = sem("e_logits_biased")
        e_sg = sem("e_gates_ready")
        e_cw = sem("e_gate_weights")
        e_wd = [sem("e_gate_loaded"), sem("e_up_loaded"), sem("e_down_loaded")]
        e_wh = sem("e_expert_weights_high_part")
        e_wl = sem("e_expert_weights_split")
        e_gu = sem("e_gate_up_filled")
        e_si = sem("e_silu_done")
        e_h = sem("e_hidden_ready")
        e_hh = sem("e_hidden_high_part")
        e_hl = sem("e_hidden_split")
        e_o = sem("e_down_filled")
        e_oa = sem("e_down_added")
        s_out = sem("output_written")

        def wait_apart(eng, semaphore, count):
            if not isinstance(count, int):
                eng.lower_val(count)
            eng.wait_ge(s_x, 16)
            eng.wait_ge(semaphore, count)

        block = ctx.enter_context(nc.Block())

        def iterations(eng, body):
            for i in range(3):
                body(i, True, i >= 1, i >= 2)
            with eng.Fori(3, NB - 1) as i:
                body(i, True, True, True)
            body(NB - 1, True, True, True)
            body(NB, False, True, True)
            body(NB + 1, False, False, True)

        @block.sync
        def _(sp):
            sp.dma_start(X, t["x"].rearrange("b t d -> t b d")).then_inc(s_x, 16)

            def context(j):
                sp.dma_start(ctx_sb, t["ctx_768"][j].rearrange("(j p) c -> p j c", p=GC)).then_inc(s_ctx, 16)

            def weight(k):
                name, parts, a, b, _ = weights[k]
                sp.dma_start(staged(k, parts, a, b), kview(name, a)).then_inc(s_staged(k)[0], 16)

            weight(0)
            weight(1)
            context(0)
            for dst, src in consts:
                sp.dma_start(dst, src).then_inc(s_const, 16)
            for k in range(2, NW):
                sp.wait_ge(s_lo, k - 1 if k < NFIRST else k)
                weight(k)

            def body(i, has_a, has_d):
                if has_d:
                    j = i - 1
                    if not isinstance(i, int) or i < NB:
                        ra.wait_full(sp, i, "c1")
                    context(j)
                    if not isinstance(j, int) or j > 0:
                        wait_apart(sp, d_vm, j)
                    sp.dma_start(vm8, t["mask_BxS2_bf1"][j].partition_broadcast(128)).then_inc(d_vm8, 16)
                if has_a:
                    if has_d:
                        rd.wait_full(sp, i - 1, "c1")
                    else:
                        ra.wait_full(sp, i, "c1")
                    context(i + 1)

            body(0, True, False)
            sp.wait_ge(s_lo, NW)
            body(1, True, True)
            with sp.Fori(2, NB - 1) as i:
                body(i, True, True)
            body(NB - 1, False, True)
            rd.wait_full(sp, NB - 2, "c1")
            body(NB, False, True)
            sp.wait_ge(c_xo, NB)
            for e in range(NEXP):
                if e >= 1:
                    sp.wait_ge(e_wl, 3 * e)
                sp.dma_start(estage[:, 0, :].rearrange("p (k n) -> p k n", k=2),
                             t["e_gate"][e].rearrange("(k p) n -> p k n", p=128)).then_inc(e_wd[0], 16)
                sp.dma_start(estage[:, 1, :].rearrange("p (k n) -> p k n", k=2),
                             t["e_up"][e].rearrange("(k p) n -> p k n", p=128)).then_inc(e_wd[1], 16)
                sp.dma_start(estage[:, 2, :].rearrange("p (k n) -> p k n", k=4),
                             t["e_down"][e].rearrange("(k p) n -> p k n", p=128)).then_inc(e_wd[2], 16)
            sp.wait_ge(e_oa, NEXP * NB)
            sp.dma_start(out.rearrange("b t d -> t b d"), X).then_inc(s_out, 16)
            sp.wait_ge(s_out, 16)

        @block.tensor
        def _(pe):
            mm = nc.tensor.matmul
            A = slice(None)

            def mm3(o, lh, rh, first, last):
                mm(o, lh[0], rh[0], start=first, stop=False)
                mm(o, lh[0], rh[1], start=False, stop=False)
                return mm(o, lh[1], rh[0], start=False, stop=last)

            def part(p, *ix):
                return p[0][ix], p[1][ix]

            def turn(o, src, m):
                for k, x in enumerate(src):
                    i = nc.tensor.transpose(o[:, k * m:(k + 1) * m], x, identf[0:m, 0:m])
                return i

            def body(i, has_a, has_b, has_c):
                a, b, d, c = i, i - 1, i - 1, i - 2
                if has_a:
                    pe.wait_ge(s_ctx, 16 * (i * 2 if not isinstance(i, int) else max(1, 2 * i)))
                    for k in range(2):
                        ra.wait_free(pe, a, f"c{k}")
                        turn(bank(ra.bank[f"c{k}"], CK, G), [ctx_sb[:, j, k * CK:(k + 1) * CK] for j in range(GJ)],
                             GC).then_inc(ra.full, 1)
                    pe.wait_ge(a_xn, a + 1)
                    ra.wait_free(pe, a, "xn")
                    turn(bank(ra.bank["xn"], 128, 2 * T), [xn[:, 0:128], xn[:, 128:256]], T).then_inc(ra.full, 1)
                if isinstance(i, int) and i == 0:
                    pe.wait_ge(s_lo, NFIRST)
                if isinstance(i, int) and i == 1:
                    pe.wait_ge(s_lo, NW)

                def a_q(q):
                    ra.wait_free(pe, a, f"q{q}")
                    for m in range(4):
                        for k in range(2):
                            x = (q * 4 + m) * 128
                            n = mm3(bank(ra.bank[f"q{q}"], 128, T, m * T), part(wq, A, k, slice(x, x + 128)),
                                    part(xT, A, k, A), k == 0, k == 1)
                    n.then_inc(ra.full, 1)

                def a_k(m):
                    ra.wait_free(pe, a, f"k{m}")
                    for k in range(2):
                        n = mm3(bank(ra.bank[f"k{m}"], 128, G), part(wk, A, k, slice(m * 128, m * 128 + 128)),
                                part(cT, A, k, A), k == 0, k == 1)
                    n.then_inc(ra.full, 1)

                def a_v(m):
                    half, j = m // 3, m % 3
                    ra.wait_free(pe, a, f"v{m}")
                    for k in range(2):
                        n = mm3(bank(ra.bank[f"v{m}"], GC, 512), part(cT, A, k, slice(j * GC, j * GC + GC)),
                                part(wv, A, k, slice(half * 512, half * 512 + 512)), k == 0, k == 1)
                    n.then_inc(ra.full, 1)

                def a_scores(h):
                    r = 64 * (h % 2)
                    mm(bank(4 + h % 2, T, G), qT[r:r + 64, h // 2, :], kT[r:r + 64, h // 2 % KR, :], start=True,
                       stop=True).then_inc(a_S, 1)

                def a_turn(h):
                    pe.wait_ge(a_E, a * H0 + h + 1)
                    if h or not isinstance(a, int) or a:
                        pe.wait_ge(a_pk, a * H0 + h)
                    turn(bank(6, GC, GJ * T), [Pr[:, h % 2, j * GC:(j + 1) * GC] for j in range(GJ)],
                         T).then_inc(a_pt, 1)

                def a_pv(h):
                    if h == 0:
                        ra.wait_act(pe, a, "v2")
                    if h == 8:
                        ra.wait_act(pe, a, "v5")
                        pe.wait_ge(a_On, a * 2 + 1)
                    pe.wait_ge(a_pk, a * H0 + h + 1)
                    for j in range(GJ):
                        n = mm(bank(7, T, DH0, (h % 8) * DH0), PTs[:, h % 2, j * T:(j + 1) * T],
                               V[:, j, h * DH0:(h + 1) * DH0], start=(j == 0), stop=(j == GJ - 1))
                    if h % 8 == 7:
                        n.then_inc(a_O, 1)

                def a_o(q):
                    pe.wait_ge(a_On, a * 2 + q + 1)
                    ra.wait_free(pe, a, f"o{q}")
                    turn(bank(ra.bank[f"o{q}"], 128, 4 * T), [On[:, m * 128:(m + 1) * 128] for m in range(4)],
                         T).then_inc(ra.full, 1)

                def a_wo():
                    ra.wait_emptied(pe, a, "o0")
                    ra.wait_free(pe, a, "wo")
                    for m in range(8):
                        if m == 4:
                            ra.wait_emptied(pe, a, "o1")
                        n = mm3(bank(ra.bank["wo"], T, D), part(aT, A, m, A), part(wo, A, m, A), m == 0, m == 7)
                    n.then_inc(ra.full, 1)

                def b_turn(n, src, cnt, count):
                    pe.wait_ge(b_q, b * 2 + count)
                    wait_bank2(pe, i, "B", n)
                    for k in range(cnt):
                        x = nc.tensor.transpose(bank16(2, 128, cnt * T)[:, k * T:(k + 1) * T],
                                                src[:, k * 128:(k + 1) * 128], identb[0:T, 0:T])
                    x.then_inc(rb.full, 1)

                def b_m(m):
                    if m == 0:
                        rb.wait_act(pe, b, "t1")
                    wait_bank2(pe, i, "B", f"m{m}")
                    for k in range(2):
                        n = mm(bank(2, T, 512), hq1[:, k, :], w1q[:, k, m * 512:(m + 1) * 512], start=(k == 0),
                               stop=(k == 1))
                    n.then_inc(rb.full, 1)

                def b_out():
                    wait_bank2(pe, i, "B", "m2")
                    for k in range(8):
                        n = mm(bank(2, T, D), hq2[:, k, :], w2q[:, k, :], start=(k == 0), stop=(k == 7))
                    n.then_inc(rb.full, 1)

                def scores1(j, h):
                    if h or not isinstance(j, int) or j:
                        pe.wait_ge(c_E, j * H1 + h)
                    r = 32 * h
                    mm(bank(3, T, G), ones_b[r:r + 1, :], vmb[r:r + 1, :], start=True, stop=False)
                    mm(bank(3, T, G), q1T[r:r + 32, :], k1T[r:r + 32, :], start=False, stop=True).then_inc(c_S, 1)

                def d_ctx(k):
                    if k == 0:
                        pe.wait_ge(s_ctx, 16 * (2 * d + 3 if not isinstance(d, int) else min(32, 2 * d + 3)))
                    wait_bank2(pe, i, "D", f"c{k}")
                    turn(bank(2, CK, G), [ctx_sb[:, j, k * CK:(k + 1) * CK] for j in range(GJ)],
                         GC).then_inc(rd.full, 1)

                def d_z():
                    pe.wait_ge(d_zn, d + 1)
                    wait_bank2(pe, i, "D", "z")
                    turn(bank(2, 128, 2 * T), [zn[:, 0:128], zn[:, 128:256]], T).then_inc(rd.full, 1)

                def d_q():
                    rd.wait_emptied(pe, d, "z")
                    wait_bank2(pe, i, "D", "q")
                    for k in range(2):
                        n = mm3(bank(2, 128, T), part(uq, A, k, A), part(zT, A, k, A), k == 0, k == 1)
                    n.then_inc(rd.full, 1)

                def d_k():
                    wait_bank2(pe, i, "D", "k")
                    for k in range(2):
                        n = mm3(bank(2, 128, G), part(uk, A, k, A), part(cTc, A, k, A), k == 0, k == 1)
                    n.then_inc(rd.full, 1)

                def d_v(n_, js):
                    wait_bank2(pe, i, "D", n_)
                    for j in js:
                        for k in range(2):
                            n = mm3(bank(2, GC, D, (j % 2) * D), part(cTc, A, k, slice(j * GC, j * GC + GC)),
                                    part(uv, A, k, A), k == 0, k == 1)
                    n.then_inc(rd.full, 1)

                def c_at():
                    wait_bank2(pe, i, "C", "at")
                    for j in range(GJ):
                        for h in range(H1):
                            if j == 0:
                                pe.wait_ge(c_dg, c * H1 + h + 1)
                            n = mm(bank(2, GC, T, j * T), P1[:, h, j * GC:(j + 1) * GC], dg[:, h, :],
                                   start=(h == 0), stop=(h == H1 - 1))
                    n.then_inc(rc.full, 1)

                def c_ct():
                    wait_bank2(pe, i, "C", "ct")
                    for m in range(2):
                        for j in range(GJ):
                            n = mm(bank(2, 128, T, m * T), V1[:, j, m * 128:(m + 1) * 128],
                                   atT[:, j * T:(j + 1) * T], start=(j == 0), stop=(j == GJ - 1))
                    n.then_inc(rc.full, 1)

                def c_film(n_, u):
                    wait_bank2(pe, i, "C", n_)
                    for k in range(2):
                        n = mm3(bank(2, T, 2 * D), part(ctT, A, k, A), part(u, A, k, A), k == 0, k == 1)
                    n.then_inc(rc.full, 1)

                def c_ab():
                    pe.wait_ge(c_x1, c + 1)
                    wait_bank2(pe, i, "C", "ab")
                    for m in range(2):
                        n = mm(bank(2, T, D, m * D), dft[:, m, :], x1, start=True, stop=True)
                    n.then_inc(rc.full, 1)

                def c_y():
                    pe.wait_ge(c_Y, c * 2 + 2)
                    wait_bank2(pe, i, "C", "y")
                    for m in range(2):
                        n = mm(bank(2, T, D), dft[:, 2 + m, :], Y[:, m * D:(m + 1) * D], start=(m == 0), stop=(m == 1))
                    n.then_inc(rc.full, 1)

                def c_h():
                    pe.wait_ge(c_h2, c + 1)
                    wait_bank2(pe, i, "C", "h")
                    turn(bank(2, 128, 2 * T), [h2[:, 0:128], h2[:, 128:256]], T).then_inc(rc.full, 1)

                def c_m(q):
                    rc.wait_emptied(pe, c, "h")
                    wait_bank2(pe, i, "C", f"m{q}")
                    for m in range(4):
                        for k in range(2):
                            x = (q * 4 + m) * 128
                            n = mm3(bank(2, 128, T, m * T), part(u1, A, k, slice(x, x + 128)),
                                    part(h2T, A, k, A), k == 0, k == 1)
                    n.then_inc(rc.full, 1)

                def c_out():
                    pe.wait_ge(c_hl, c + 1)
                    wait_bank2(pe, i, "C", "m2")
                    for m in range(8):
                        n = mm3(bank(2, T, D), part(hidT, A, m, A), part(u2, A, m, A), m == 0, m == 7)
                    n.then_inc(rc.full, 1)

                if has_a:
                    ra.wait_emptied(pe, a, "xn")
                    a_q(0)
                    a_q(1)
                    a_k(0)
                if has_b:
                    b_turn("t1", q1, 2, 1)
                if has_a:
                    a_v(0)
                if has_c:
                    scores1(c, 1)
                if has_a:
                    a_v(1)
                if has_b:
                    b_m(0)
                if has_a:
                    a_v(2)
                    a_k(1)
                if has_b:
                    b_m(1)
                if has_a:
                    ra.wait_act(pe, a, "k0")
                    a_scores(0)
                    a_scores(1)
                for h in range(H0):
                    if has_a:
                        a_turn(h)
                        if h + 2 < H0:
                            if h % 2 == 0:
                                ra.wait_act(pe, a, f"k{h // 2 + 1}")
                            a_scores(h + 2)
                        if h >= 1:
                            a_pv(h - 1)
                        if h in (1, 3, 5, 7, 9, 11):
                            if h == 11:
                                a_k(7)
                            else:
                                a_k((h + 3) // 2)
                        if h in (2, 4, 6):
                            a_v(h // 2 + 2)
                        if h == 10:
                            a_o(0)
                    if isinstance(i, int) and i == 0 and h in (1, 2):
                        pe.wait_ge(s_wab, h)
                        mm(bank(4 - h, 128, 1), ones_f, wab[:, h - 1:h], start=True, stop=True).then_inc(s_wsum, 1)
                    if has_c:
                        if h == 1:
                            scores1(c, 2)
                        if h == 4:
                            scores1(c, 3)
                        if h == 8:
                            c_at()
                        if h == 9:
                            rc.wait_act(pe, c, "at")
                            c_ct()
                        if h == 10:
                            rc.wait_emptied(pe, c, "ct")
                            c_film("fi", ufi)
                        if h == 11:
                            c_film("fo", ufo)
                        if h == 12 and isinstance(i, int) and i == 2:
                            pe.wait_ge(s_s4c, 2 * PA)
                            wait_bank2(pe, i, "C", "ab")
                            for m in range(2):
                                n = nc.tensor.transpose(bank(2, T, 128, m * 128), kpow[:, m, :], identf)
                            n.then_inc(s_kf, 1)
                            for q in range(2):
                                pe.wait_ge(s_kr, 1 + q)
                                for m in range(2):
                                    n = mm(bank(2, T, D, m * D), dft[:, 4 + q * 2 + m, :], kt, start=True, stop=True)
                                n.then_inc(s_kf, 1)
                            pe.wait_ge(s_kr, 3)
                        if h == 12:
                            c_ab()
                        if h == 13:
                            c_y()
                    if has_b:
                        if h == 6:
                            b_turn("t2", q2, 8, 2)
                        if h == 7:
                            rb.wait_act(pe, b, "t2")
                            b_out()
                        if h in (13, 14):
                            d_ctx(h - 13)
                        if h == 15:
                            d_z()
                if has_a:
                    a_pv(H0 - 1)
                if has_c:
                    c_h()
                if has_b:
                    d_q()
                if has_a:
                    a_o(1)
                if has_c:
                    c_m(0)
                    c_m(1)
                if has_b:
                    d_k()
                    d_v("v0", (0, 1))
                if has_a:
                    a_wo()
                if has_b:
                    d_v("v1", (2,))
                    rd.wait_act(pe, d, "k")
                    pe.wait_ge(d_vm, d + 1)
                    scores1(d, 0)
                if has_c:
                    c_out()

            pe.wait_ge(s_const, 16 * NCONST)
            iterations(pe, body)

            with pe.Fori(0, NB) as b:
                pe.wait_ge(e_z, b + 1)
                for k in range(2):
                    i = nc.tensor.transpose(bank(0, 128, T, k * T), ze[:, k * 128:(k + 1) * 128], identf[0:T, 0:T])
                i.then_inc(e_tr, 1)
                pe.wait_ge(e_zl, b + 1)
                for k in range(2):
                    i = mm3(bank(1, T, 8), part(zt_t, A, k, A), part((wr_hi, wr_lo), A, k, A), k == 0, k == 1)
                i.then_inc(e_lg, 1)
            pe.wait_ge(e_zc, 2 * NB)

            def expert(e, f):
                def gate_up(c):
                    tok = slice(c * CH, (c + 1) * CH)
                    for i4 in range(4):
                        n = (e * NCH + c) * 4 + i4
                        cs = slice(i4 * 128, i4 * 128 + 128)
                        pe.wait_ge(e_h, n - 1) if not isinstance(n, int) or n >= 2 else None
                        for k in range(2):
                            mm3(bank(2 * (i4 % 2), 128, CH), part(eg[f], A, k, cs), part(ZT, A, k, tok), k == 0, k == 1)
                        for k in range(2):
                            i = mm3(bank(2 * (i4 % 2) + 1, 128, CH), part(eu[f], A, k, cs), part(ZT, A, k, tok), k == 0,
                                    k == 1)
                        i.then_inc(e_gu, 1)

                def down(c):
                    for s in range(CHB):
                        n = (e * NCH + c) * CHB + s
                        if s == 0:
                            pe.wait_ge(e_hl, ((e * NCH + c) + 1) * 4)
                        pe.wait_ge(e_oa, n - 3) if not isinstance(n, int) or n >= 4 else None
                        for m in range(4):
                            i = mm3(bank(4 + s, T, D), part(hT[c % 2], A, m, slice(s * T, s * T + T)),
                                    part(ed[f], A, m, A), m == 0, m == 3)
                        i.then_inc(e_o, 1)

                pe.wait_ge(e_wl, e * 3 + 3)
                gate_up(0)
                for c in range(1, NCH):
                    gate_up(c)
                    down(c - 1)
                down(NCH - 1)

            expert(0, 0)
            with pe.Fori(0, (NEXP - 1) // 2) as g:
                expert(g * 2 + 1, 1)
                expert(g * 2 + 2, 0)

        @block.scalar
        def _(act):
            def copy(o, i, scale=1.0):
                return nc.scalar.activation(o, i, ACT.Copy, scale=scale)

            n_hi = [0]

            def weight(k):
                _, parts, a, b, dst = weights[k]
                if isinstance(dst, tuple):
                    act.wait_ge(*s_staged(k))
                    copy(dst[0], staged(k, parts, a, b), WS).then_inc(s_hi, 1)

            weight(0)
            weight(1)
            act.wait_ge(s_const, 16 * NCONST)
            nc.scalar.activation(dtc, ldt, ACT.Exp).then_inc(s_s4a, 1)
            act.wait_ge(s_s4v, S4_RE)
            nc.scalar.activation(s4["th"], s4["re"], ACT.Tanh, scale=0.5).then_inc(s_s4a, 1)
            act.wait_ge(s_s4v, S4_ANG)
            nc.scalar.activation(s4["s"], s4["k"], ACT.Sin).then_inc(s_s4a, 1)
            nc.scalar.activation(s4["sh"], s4["k"], ACT.Sin, scale=0.5).then_inc(s_s4a, 1)
            weight(2)
            weight(3)
            copy(identb, identf).then_inc(s_misc, 1)
            copy(wr_hi, wr_f, WS).then_inc(s_misc, 1)
            copy(tmask, tmask8).then_inc(s_misc, 1)

            def keep(ring, i, name, dst, src, scale=1.0):
                ring.wait_full(act, i, name)
                copy(dst, src, scale).then_inc(ring.act, 1)

            def halves(x, m=2):
                return x.rearrange("p (k t) -> p k t", k=m)

            def body(i, has_a, has_b, has_c):
                a, b, d, c = i, i - 1, i - 1, i - 2

                def a_keep_k(m):
                    keep(ra, a, f"k{m}", kT[:, m % KR, :], bank(ra.bank[f"k{m}"], 128, G), IWS)

                def a_keep_v(m):
                    half, j = m // 3, m % 3
                    keep(ra, a, f"v{m}", V[:, j, half * 512:half * 512 + 512], bank(ra.bank[f"v{m}"], GC, 512), IWS)

                def a_exp(h):
                    act.wait_ge(a_mx, a * H0 + h + 1)
                    if h >= 2:
                        act.wait_ge(a_pt, a * H0 + h - 1)
                    nc.scalar.activation(Pr[:, h % 2, :], bank(4 + h % 2, T, G), ACT.Exp, bias=nmx[:, h:h + 1],
                                         accum_out=rsum[:, h:h + 1]).then_inc(a_E, 1)

                def c_exp(h):
                    act.wait_ge(c_nm, c * H1 + h + 1)
                    nc.scalar.activation(P1[:, h, :], bank(3, T, G), ACT.Exp, bias=nmx1[:, h:h + 1],
                                         scale=DH1 ** -0.5).then_inc(c_E, 1)

                if has_a:
                    for k in range(2):
                        keep(ra, a, f"c{k}", cT[0][:, k, :], bank(ra.bank[f"c{k}"], CK, G))
                    keep(ra, a, "xn", xT[0], halves(bank(ra.bank["xn"], 128, 2 * T)))
                    for q in range(2):
                        keep(ra, a, f"q{q}", qT[:, q * 4:q * 4 + 4, :], halves(bank(ra.bank[f"q{q}"], 128, 4 * T), 4),
                             IWS * DH0 ** -0.5)
                    a_keep_k(0)
                if has_b:
                    keep(rb, b, "t1", hq1, halves(bank16(2, 128, 2 * T)))
                if has_a:
                    a_keep_v(0)
                if has_c:
                    c_exp(0)
                if has_a:
                    a_keep_v(1)
                    a_keep_v(2)
                    a_keep_k(1)
                    a_exp(0)
                    a_exp(1)
                for h in range(H0):
                    if has_a:
                        act.wait_ge(a_pt, a * H0 + h + 1)
                        copy(PTs[:, h % 2, :], bank(6, GC, GJ * T)).then_inc(a_pk, 1)
                        if h + 2 < H0:
                            a_exp(h + 2)
                        if h in (1, 3, 5, 7, 9, 11):
                            a_keep_k(7 if h == 11 else (h + 3) // 2)
                        if h in (2, 4, 6):
                            a_keep_v(h // 2 + 2)
                        if h == 10:
                            keep(ra, a, "o0", aT[0][:, 0:4, :], halves(bank(ra.bank["o0"], 128, 4 * T), 4))
                    if isinstance(i, int) and i == 0 and 1 <= h < 1 + NW - NFIRST:
                        weight(NFIRST + h - 1)
                    if has_c and h in (0, 3, 6):
                        c_exp(h // 3 + 1)
                    if has_b:
                        if h == 0:
                            for m in range(2):
                                rb.wait_dve(act, b, f"m{m}")
                                u = ub[:, m * 512:(m + 1) * 512]
                                nc.scalar.activation(u, u, ACT.Gelu).then_inc(b_g, 1)
                        if h == 6:
                            keep(rb, b, "t2", hq2, halves(bank16(2, 128, 8 * T), 8))
                    if has_c:
                        if h == 8:
                            keep(rc, c, "at", atT, bank(2, GC, GJ * T))
                        if h == 9:
                            keep(rc, c, "ct", ctT[0], halves(bank(2, 128, 2 * T)))
                        if h == 12 and isinstance(i, int) and i == 2:
                            act.wait_ge(s_kf, 1)
                            copy(kt, bank(2, T, D)).then_inc(s_kr, 1)
                            for q in range(2):
                                act.wait_ge(s_kf, 2 + q)
                                copy(coef[:, q * 2:q * 2 + 2, :], halves(bank(2, T, 2 * D))).then_inc(s_kr, 1)
                    if has_b:
                        if h in (13, 14):
                            keep(rd, d, f"c{h - 13}", cTc[0][:, h - 13, :], bank(2, CK, G))
                        if h == 15:
                            keep(rd, d, "z", zT[0], halves(bank(2, 128, 2 * T)))
                if has_c:
                    keep(rc, c, "h", h2T[0], halves(bank(2, 128, 2 * T)))
                if has_b:
                    keep(rd, d, "q", q1T, bank(2, 128, T), IWS)
                if has_a:
                    keep(ra, a, "o1", aT[0][:, 4:8, :], halves(bank(ra.bank["o1"], 128, 4 * T), 4))
                if has_c:
                    for q in range(2):
                        rc.wait_full(act, c, f"m{q}")
                        for m in range(4):
                            n = nc.scalar.activation(hid[:, q * 4 + m, :], bank(2, 128, T, m * T), ACT.Gelu,
                                                     bias=b1col[:, q * 4 + m:q * 4 + m + 1], scale=IWS)
                        n.then_inc(rc.act, 1)
                    rc.wait_act(act, c, "m1")
                    copy(hidT[0], hid).then_inc(c_hh, 1)
                if has_b:
                    keep(rd, d, "k", k1T, bank(2, 128, G), IWS)
                    keep(rd, d, "v0", V1[:, 0:2, :], halves(bank(2, GC, 2 * D)), IWS)
                    keep(rd, d, "v1", V1[:, 2, :], bank(2, GC, D), IWS)

            iterations(act, body)

            with act.Fori(0, NB) as b:
                act.wait_ge(e_tr, b + 1)
                act.wait_ge(e_zc, b * 2)
                copy(zt_t[0], bank(0, 128, 2 * T).rearrange("p (k t) -> p k t", k=2)).then_inc(e_zh, 1)
                act.wait_ge(e_lb, b + 1)
                nc.scalar.activation(pr[:, 0:8], lg, ACT.Sigmoid).then_inc(e_sg, 1)

            def expert_weights(e, f):
                for k, dst in enumerate((eg[f][0], eu[f][0], ed[f][0])):
                    act.wait_ge(e_wd[k], (e + 1) * 16)
                    copy(dst, estage[:, k, :].rearrange("p (a b) -> p a b", a=(2, 2, 4)[k]), WS).then_inc(e_wh, 1)

            def expert(e, f, ahead):
                for c in range(NCH):
                    for i4 in range(4):
                        n = (e * NCH + c) * 4 + i4
                        act.wait_ge(e_gu, n + 1)
                        act.wait_ge(e_h, n - 1) if not isinstance(n, int) or n >= 2 else None
                        nc.scalar.activation(sg[:, i4 % 2, :], bank(2 * (i4 % 2), 128, CH), ACT.Silu,
                                             scale=IWS).then_inc(e_si, 1)
                        act.wait_ge(e_h, n + 1)
                        if i4 == 0:
                            k = (e * NCH + c) * CHB
                            act.wait_ge(e_o, k - CHB) if not isinstance(k, int) or k >= 2 * CHB else None
                        copy(hT[c % 2][0][:, i4, :], hf[:, i4 % 2, :]).then_inc(e_hh, 1)
                    if c == 1 and ahead:
                        act.wait_ge(e_o, e * NB)
                        expert_weights(e + 1, 1 - f)

            act.wait_ge(c_xo, NB)
            expert_weights(0, 0)
            expert(0, 0, True)
            with act.Fori(0, (NEXP - 1) // 2 - 1) as g:
                expert(g * 2 + 1, 1, True)
                expert(g * 2 + 2, 0, True)
            expert(NEXP - 2, 1, True)
            expert(NEXP - 1, 0, False)

        @block.gpsimd
        def _(pool):
            def tt(o, a, b, op):
                return nc.gpsimd.tensor_tensor(o, a, b, op)

            nc.gpsimd.memset(ones_f, 1.0).then_inc(s_pmisc, 1)
            nc.gpsimd.memset(ones_b, 1.0).then_inc(s_pmisc, 1)
            nc.gpsimd.memset(neghalf, -0.5).then_inc(s_pmisc, 1)
            pool.wait_ge(s_pmisc, 3)
            pool.wait_ge(s_x, 16)
            pool.wait_ge(s_const, 16 * NCONST)

            def rsqrt(var_sem, rstd_sem, n):
                pool.wait_ge(var_sem, n + 1)
                tt(rstd, ve, neghalf, ALU.pow).then_inc(rstd_sem, 1)

            def s4d_powers(h):
                n = [h * S4P_HALF]

                def link(ins):
                    n[0] += 1
                    ins.then_inc(s_s4p, 1)
                    pool.wait_ge(s_s4p, n[0])

                def cmul(o, a, c, m):
                    cr_, ci_ = (x.to_broadcast([128, m, NST]) for x in c)
                    f1, f2 = p1[:, 0:m, :], p2[:, 0:m, :]
                    link(tt(f1, a[0], cr_, ALU.mult))
                    link(tt(f2, a[1], ci_, ALU.mult))
                    link(tt(o[0], f1, f2, ALU.subtract))
                    link(tt(f1, a[0], ci_, ALU.mult))
                    link(tt(f2, a[1], cr_, ALU.mult))
                    link(tt(o[1], f1, f2, ALU.add))

                def at(p, lo, hi):
                    return p[0][:, lo:hi, :], p[1][:, lo:hi, :]

                v, u = (vr, vi), (ur, ui)
                pool.wait_ge(s_s4v, S4V_ALL)
                pool.wait_ge(s_lo, NFIRST)
                if h:
                    pool.wait_ge(s_s4c, PA)
                link(nc.gpsimd.memset(vr[:, 0, :], 1.0))
                link(nc.gpsimd.memset(vi[:, 0, :], 0.0))
                link(nc.gpsimd.tensor_copy(vr[:, 1, :], s4["zr"][:, h, :]))
                link(nc.gpsimd.tensor_copy(vi[:, 1, :], s4["zi"][:, h, :]))
                link(nc.gpsimd.tensor_copy(ur[:, 0, :], s4["dr"][:, h, :]))
                link(nc.gpsimd.tensor_copy(ui[:, 0, :], s4["di"][:, h, :]))
                for m in (1, 2, 4, 8):
                    cmul(at(v, m + 1, 2 * m + 1), at(v, 1, m + 1), at(v, m, m + 1), m)
                for m in range(PA - 1):
                    cmul(at(u, m + 1, m + 2), at(u, m, m + 1), at(v, PBS, PBS + 1), 1)
                assert n[0] == (h + 1) * S4P_HALF, n[0]

            rsqrt(a_var, a_rstd, 0)
            pool.wait_ge(a_xn, 1)
            tt(X[:, 0, :], X[:, 0, :], bo_r, ALU.add).then_inc(a_xb, 1)

            def body(i, has_a, has_b, has_c):
                b, d, c = i - 1, i - 1, i - 2

                def diagonal(h):
                    wait_apart(pool, c_r, c * H1 + h + 1)
                    nc.gpsimd.tensor_scalar(dg[:, h, :], identf[0:T, 0:T], r2[:, h:h + 1], 1.0, ALU.mult,
                                            ALU.mult).then_inc(c_dg, 1)

                if has_c:
                    if not isinstance(c, int) or c > 0:
                        wait_apart(pool, c_xo, c)
                    wait_apart(pool, d_zn, c + 1)
                    nc.gpsimd.tensor_copy(z, zn).then_inc(c_z, 1)
                if has_b:
                    rsqrt(b_var, b_rstd, b * 3)
                    pool.wait_ge(b_z, b + 1)
                    tt(X[:, bass.ds(b, 1), :].rearrange("p o d -> p (o d)"), X[:, bass.ds(b, 1), :].rearrange("p o d -> p (o d)"), b2_r, ALU.add).then_inc(b_xb, 1)
                    rsqrt(b_var, b_rstd, b * 3 + 1)
                if isinstance(i, int) and i < 2:
                    s4d_powers(i)
                if has_c:
                    diagonal(0)
                    diagonal(1)
                if has_b:
                    rsqrt(b_var, b_rstd, b * 3 + 2)
                if has_c:
                    diagonal(2)
                    rsqrt(c_var, c_rstd, c * 3)
                    diagonal(3)
                if has_b:
                    rsqrt(d_var, d_rstd, d)
                    if not isinstance(d, int) or d > 0:
                        pool.wait_ge(c_S, d * H1)
                    wait_apart(pool, d_vm8, d * 16 + 16)
                    nc.gpsimd.tensor_scalar(vmb, vm8, MASKED, -MASKED, ALU.mult, ALU.add).then_inc(d_vm, 1)
                if has_c:
                    pool.wait_ge(c_x1, c + 1)
                    tt(xd, x1, dsk_r, ALU.mult).then_inc(c_xd, 1)
                    rsqrt(c_var, c_rstd, c * 3 + 1)
                if has_a and not (isinstance(i, int) and i == NB - 1):
                    rsqrt(a_var, a_rstd, i + 1)
                    pool.wait_ge(a_xn, i + 2)
                    x = X[:, i + 1, :]
                    tt(x, x, bo_r, ALU.add).then_inc(a_xb, 1)
                if has_c:
                    rsqrt(c_var, c_rstd, c * 3 + 2)

            iterations(pool, body)
            with pool.Fori(0, NB) as b:
                rsqrt(e_var, e_rstd, b)
                pool.wait_ge(e_zl, b + 1)
                for k in range(2):
                    nc.gpsimd.tensor_copy(ZT[k][:, :, bass.ds(b * T, T)], zt_t[k]).then_inc(e_zc, 1)

        @block.vector
        def _(dve):
            V_ = nc.vector

            def ts(o, i, a, b, op0, op1=None):
                return V_.tensor_scalar(o, i, a, b, op0, op1) if op1 is not None else V_.tensor_scalar(o, i, a, None, op0)

            def tt(o, a, b, op):
                return V_.tensor_tensor(o, a, b, op)

            def stt(o, a, s, b, op0, op1, **kw):
                return V_.scalar_tensor_tensor(o, a, s, b, op0, op1, **kw)

            def halves(x, m=2):
                return x.rearrange("p (k t) -> p k t", k=m)

            n_set = [0]

            def linkset(ins):
                n_set[0] += 1
                ins.then_inc(s_dset, 1)
                dve.wait_ge(s_dset, n_set[0])

            def weight(k):
                _, parts, a, b, dst = weights[k]
                src = staged(k, parts, a, b)
                if isinstance(dst, tuple):
                    dve.wait_ge(s_hi, sum(isinstance(w_[4], tuple) for w_ in weights[:k + 1]))
                    stt(dst[1], src, WS, dst[0], ALU.mult, ALU.subtract).then_inc(s_lo, 1)
                    return
                q = k - NFIRST
                dve.wait_ge(*s_staged(k))
                flat = stage[0]
                V_.tensor_reduce(wab[:, q:q + 1], flat, AX_X, ALU.add, apply_absolute_value=True).then_inc(s_wab, 1)
                dve.wait_ge(s_wsum, q + 1)
                linkset(ts(wmean[:, q:q + 1], bank(3 - q, 128, 1), 1.0 / (a * b * 128), EPS, ALU.mult, ALU.max))
                linkset(V_.reciprocal(wsc[:, q:q + 1], wmean[:, q:q + 1]))
                linkset(ts(flat, flat, wsc[:, q:q + 1], 1.0, ALU.mult, ALU.min))
                linkset(ts(flat, flat, -1.0, MAGIC, ALU.max, ALU.add))
                ts(dst, src, -MAGIC, None, ALU.add).then_inc(s_lo, 1)

            def layer_norm(link, var_sem, rstd_sem, n, dst, src, width=D):
                for c in range(0, width, 512):
                    e = min(width, c + 512)
                    link(V_.bn_stats(st[:, c // 512, :], src[:, c:e]), hold=(e == width))
                k = (width + 511) // 512
                link(V_.bn_aggr(mv, st[:, 0:k, :]))
                ts(ve, mv[:, 1:2], EPS, None, ALU.add).then_inc(var_sem, 1)
                dve.wait_ge(rstd_sem, n + 1)
                return ts(dst, src, mv[:, 0:1], rstd, ALU.subtract, ALU.mult)

            class Link:
                def __init__(self, s, per):
                    self.s, self.per, self.n = s, per, 0

                def at(self, i):
                    self.i, self.n = i, 0
                    return self

                def __call__(self, ins, hold=False):
                    self.n += 1
                    ins.then_inc(self.s, 1)
                    (wait_apart if hold else type(dve).wait_ge)(dve, self.s, self.i * self.per + self.n)

                def done(self):
                    assert self.n == self.per, self.n

            def split_low(ring, i, name, lo, hi, src):
                ring.wait_act(dve, i, name)
                tt(lo, src, hi, ALU.subtract).then_inc(ring.dve, 1)

            linka, linkb, linkc, linkd = Link(a_step, 2), Link(b_step, B_LINKS), Link(c_step, C_LINKS), Link(d_step, 2)

            def a_norm(j):
                layer_norm(linka.at(j), a_var, a_rstd, j, xn, X[:, j, :]).then_inc(a_xn, 1)

            dve.wait_ge(s_x, 16)
            a_norm(0)
            weight(0)
            weight(1)
            dve.wait_ge(s_const, 16 * NCONST)
            n4 = [0]

            def link4(ins):
                n4[0] += 1
                ins.then_inc(s_s4v, 1)
                dve.wait_ge(s_s4v, n4[0])

            f = s4
            dve.wait_ge(s_s4a, 1)
            dtb = dtc.rearrange("p (h o) -> p h o", o=1).to_broadcast([128, 2, NST])
            link4(tt(f["re"], f["ar"], dtb, ALU.mult))
            link4(tt(f["im"], f["ai"], dtb, ALU.mult))
            assert S4_RE == 1
            link4(ts(f["t1"], f["im"], 1.0 / TWO_PI, MAGIC, ALU.mult, ALU.add))
            link4(ts(f["t1"], f["t1"], -MAGIC, None, ALU.add))
            link4(stt(f["k"], f["t1"], -TP1, f["im"], ALU.mult, ALU.add))
            link4(stt(f["k"], f["t1"], -TP2, f["k"], ALU.mult, ALU.add))
            link4(stt(f["k"], f["t1"], -TP3, f["k"], ALU.mult, ALU.add))
            link4(ts(f["k"], f["k"], 3.1415925, -3.1415925, ALU.min, ALU.max))
            assert n4[0] == S4_ANG
            dve.wait_ge(s_s4a, 4)
            link4(ts(f["t1"], f["th"], -1.0, 1.0, ALU.mult, ALU.add))
            link4(V_.reciprocal(f["t2"], f["t1"]))
            link4(stt(f["e1"], f["th"], 2.0, f["t2"], ALU.mult, ALU.mult))
            link4(stt(f["t2"], f["sh"], -2.0, f["sh"], ALU.mult, ALU.mult))
            link4(ts(f["re"], f["e1"], 1.0, None, ALU.add))
            link4(ts(f["im"], f["t2"], 1.0, None, ALU.add))
            link4(tt(f["zr"], f["re"], f["im"], ALU.mult))
            link4(tt(f["zi"], f["re"], f["s"], ALU.mult))
            link4(tt(f["t1"], f["e1"], f["im"], ALU.mult))
            link4(tt(f["mr"], f["t1"], f["t2"], ALU.add))
            link4(tt(f["t1"], f["ar"], f["ar"], ALU.mult))
            link4(tt(f["t2"], f["ai"], f["ai"], ALU.mult))
            link4(tt(f["t1"], f["t1"], f["t2"], ALU.add))
            link4(V_.reciprocal(f["e1"], f["t1"]))
            link4(tt(f["t1"], f["mr"], f["ar"], ALU.mult))
            link4(tt(f["t2"], f["zi"], f["ai"], ALU.mult))
            link4(tt(f["re"], f["t1"], f["t2"], ALU.add))
            link4(tt(f["t1"], f["zi"], f["ar"], ALU.mult))
            link4(tt(f["t2"], f["mr"], f["ai"], ALU.mult))
            link4(tt(f["im"], f["t1"], f["t2"], ALU.subtract))
            link4(stt(f["re"], f["re"], 2.0, f["e1"], ALU.mult, ALU.mult))
            link4(stt(f["im"], f["im"], 2.0, f["e1"], ALU.mult, ALU.mult))
            link4(tt(f["t1"], f["cr"], f["re"], ALU.mult))
            link4(tt(f["t2"], f["ci"], f["im"], ALU.mult))
            link4(tt(f["dr"], f["t1"], f["t2"], ALU.subtract))
            link4(tt(f["t1"], f["cr"], f["im"], ALU.mult))
            link4(tt(f["t2"], f["ci"], f["re"], ALU.mult))
            link4(tt(f["di"], f["t1"], f["t2"], ALU.add))
            assert n4[0] == S4V_ALL, n4[0]

            weight(2)
            weight(3)

            def s4d_contract(h, a):
                n0 = (h * PA + a) * 3
                dve.wait_ge(s_s4p, (h + 1) * S4P_HALF)
                if n0:
                    dve.wait_ge(s_s4c, h * PA + a)
                tt(p1, vr[:, 0:PBS, :], ur[:, a:a + 1, :].to_broadcast([128, PBS, NST]), ALU.mult).then_inc(s_s4d, 1)
                tt(p2, vi[:, 0:PBS, :], ui[:, a:a + 1, :].to_broadcast([128, PBS, NST]), ALU.mult).then_inc(s_s4d, 1)
                dve.wait_ge(s_s4d, n0 + 2)
                tt(p1, p1, p2, ALU.subtract).then_inc(s_s4d, 1)
                dve.wait_ge(s_s4d, n0 + 3)
                V_.tensor_reduce(kpow[:, h, a * PBS:(a + 1) * PBS], p1, AX_X, ALU.add).then_inc(s_s4c, 1)

            def small_constants():
                dve.wait_ge(s_misc, 3)
                linkset(ts(mbi, mbi, mg, None, ALU.mult))
                linkset(ts(mbo, mbo, mg, None, ALU.mult))
                linkset(ts(mbi[:, 0:D], mbi[:, 0:D], 1.0, None, ALU.add))
                linkset(ts(mbo[:, 0:D], mbo[:, 0:D], 1.0, None, ALU.add))
                linkset(ts(mgs, mg, IWS, None, ALU.mult))
                linkset(stt(wr_lo, wr_f, WS, wr_hi, ALU.mult, ALU.subtract))

            def quantize(link, dst, src, qf, dq, wm):
                link(V_.tensor_reduce(amax, src, AX_X, ALU.max, apply_absolute_value=True))
                link(ts(amc, amax, EPS, None, ALU.max))
                link(V_.reciprocal(rcp, amc))
                link(ts(qsc, rcp, 127.0, None, ALU.mult))
                link(ts(dq, amc, wm, 1.0 / 127.0, ALU.mult, ALU.mult))
                link(ts(qf, src, qsc, MAGIC, ALU.mult, ALU.add))
                ts(dst, qf, -MAGIC, 127.0, ALU.add, ALU.min).then_inc(b_q, 1)

            def body(i, has_a, has_b, has_c):
                a, b, d, c = i, i - 1, i - 1, i - 2
                if has_b:
                    linkb.at(b)
                if has_c:
                    linkc.at(c)

                def row_max(h):
                    dve.wait_ge(a_S, a * H0 + h + 1)
                    V_.tensor_reduce(nmx[:, h:h + 1], bank(4 + h % 2, T, G), AX_X, ALU.max, negate=True).then_inc(a_mx, 1)

                def a_norm_heads(q):
                    dve.wait_ge(a_E, a * H0 + q * 8 + 8)
                    V_.reciprocal(rinv[:, q * 8:q * 8 + 8], rsum[:, q * 8:q * 8 + 8]).then_inc(a_ri, 1)
                    dve.wait_ge(a_O, a * 2 + q + 1)
                    if q:
                        ra.wait_full(dve, a, "o0")
                    dve.wait_ge(a_ri, a * 2 + q + 1)
                    tt(halves(On, 8), halves(bank(7, T, 512), 8),
                       rinv[:, q * 8:q * 8 + 8].rearrange("p (h o) -> p h o", o=1).to_broadcast([T, 8, DH0]),
                       ALU.mult).then_inc(a_On, 1)

                def a_low_o(q):
                    split_low(ra, a, f"o{q}", aT[1][:, q * 4:q * 4 + 4, :], aT[0][:, q * 4:q * 4 + 4, :],
                              halves(bank(ra.bank[f"o{q}"], 128, 4 * T), 4))

                def b_hidden(m):
                    rb.wait_full(dve, b, f"m{m}")
                    cs = slice(m * 512, (m + 1) * 512)
                    stt(ub[:, cs], bank(2, T, 512), dq1, b1row[:, cs], ALU.mult, ALU.add).then_inc(rb.dve, 1)

                def top(h, rounds):
                    for r in rounds:
                        src = bank(3, T, G) if r == 0 else R1
                        m8 = top8[:, h % 2, r, :]
                        if r == 0:
                            wait_apart(dve, c_S, c * H1 + h + 1)
                        V_.max(m8, src).then_inc(c_top, 1)
                        if r:
                            wait_apart(dve, c_top, (c * H1 + h) * 4 + r + 1)
                            linkc(V_.match_replace(R1, m8, src, NEG), hold=(r < 3))
                        else:
                            dve.wait_ge(c_top, (c * H1 + h) * 4 + r + 1)
                            linkc(ts(nmx1[:, h:h + 1], m8[:, 0:1], -(DH1 ** -0.5), None, ALU.mult), hold=True)
                            V_.match_replace(R1, m8, src, NEG).then_inc(c_nm, 1)
                            wait_apart(dve, c_nm, c * H1 + h + 1)

                def top_probs(h):
                    dve.wait_ge(c_E, c * H1 + h + 1)
                    linkc(stt(P1[:, h, :], R1, 0.9 * NEG, P1[:, h, :], ALU.is_lt, ALU.mult, accum_out=sum1[:, h:h + 1]))
                    linkc(V_.reciprocal(r1[:, h:h + 1], sum1[:, h:h + 1]))
                    ts(r2[:, h:h + 1], r1[:, h:h + 1], tmask[:, bass.ds(c, 1)], 1.0 / H1, ALU.mult,
                       ALU.mult).then_inc(c_r, 1)

                if has_a:
                    for k in range(2):
                        split_low(ra, a, f"c{k}", cT[1][:, k, :], cT[0][:, k, :], bank(ra.bank[f"c{k}"], CK, G))
                    split_low(ra, a, "xn", xT[1], xT[0], halves(bank(ra.bank["xn"], 128, 2 * T)))
                if has_b:
                    layer_norm(linkb, b_var, b_rstd, b * 3, zb, X[:, b, :]).then_inc(b_z, 1)
                    wait_apart(dve, b_z, b + 1)
                    linkb(layer_norm(linkb, b_var, b_rstd, b * 3 + 1, zb, zb))
                    linkb(tt(zb, zb, g1_r, ALU.mult))
                    linkb(tt(zb, zb, h1_r, ALU.add))
                    quantize(linkb, q1, zb, zb, dq1, wmean[0:T, 0:1])
                if has_c:
                    top(0, (0, 1))
                if has_b:
                    b_hidden(0)
                if has_c:
                    top(0, (2,))
                if has_b:
                    b_hidden(1)
                if has_c:
                    top(0, (3,))
                    top_probs(0)
                if has_a:
                    row_max(0)
                    row_max(1)
                for h in range(H0):
                    if has_a and h + 2 < H0:
                        row_max(h + 2)
                    if isinstance(i, int) and i == 0:
                        if 1 <= h < 1 + NW - NFIRST:
                            weight(NFIRST + h - 1)
                        if h == 10:
                            small_constants()
                    if isinstance(i, int) and i < 2 and 6 <= h < 6 + PA:
                        s4d_contract(i, h - 6)
                    if has_c:
                        if h in (0, 3, 6):
                            top(h // 3 + 1, (0, 1))
                        if h in (1, 4, 7):
                            top(h // 3 + 1, (2, 3))
                            top_probs(h // 3 + 1)
                    if has_b:
                        if h == 2:
                            wait_apart(dve, b_g, b * 2 + 2)
                            linkb(layer_norm(linkb, b_var, b_rstd, b * 3 + 2, ub, ub, HID))
                        if h == 4:
                            linkb(tt(ub, ub, g2row, ALU.mult))
                            linkb(tt(ub, ub, h2row, ALU.add))
                        if h == 5:
                            quantize(linkb, q2, ub, ub, dq2, wmean[0:T, 1:2])
                    if has_c and h == 5:
                        wait_apart(dve, c_z, c + 1)
                        linkc(layer_norm(linkc, c_var, c_rstd, c * 3, x1, z))
                    if has_a and h == 8:
                        a_norm_heads(0)
                    if has_b and h == 8:
                        rb.wait_full(dve, b, "m2")
                        dve.wait_ge(b_xb, b + 1)
                        stt(X[:, b, :], bank(2, T, D), dq2, X[:, b, :], ALU.mult, ALU.add).then_inc(rb.dve, 1)
                        rb.wait_dve(dve, b, "m2")
                    if has_c and h == 8:
                        linkc(tt(x1, x1, gi_r, ALU.mult))
                        linkc(tt(x1, x1, hi_r, ALU.add), hold=True)
                    if has_b and h == 9:
                        if has_c:
                            wait_apart(dve, c_z, c + 1)
                        layer_norm(linkd.at(d), d_var, d_rstd, d, zn, X[:, d, :]).then_inc(d_zn, 1)
                    if has_c:
                        if h == 9:
                            split_low(rc, c, "ct", ctT[1], ctT[0], halves(bank(2, 128, 2 * T)))
                        if h == 10:
                            rc.wait_full(dve, c, "fi")
                            stt(mi, bank(2, T, 2 * D), mgs, mbi, ALU.mult, ALU.add).then_inc(rc.dve, 1)
                            rc.wait_dve(dve, c, "fi")
                            linkc(tt(x1, x1, mi[:, 0:D], ALU.mult))
                            tt(x1, x1, mi[:, D:2 * D], ALU.add).then_inc(c_x1, 1)
                    if has_a and h == 10:
                        a_low_o(0)
                    if has_c:
                        if h == 11:
                            rc.wait_full(dve, c, "fo")
                            stt(mo, bank(2, T, 2 * D), mgs, mbo, ALU.mult, ALU.add).then_inc(rc.dve, 1)
                        if h == 12:
                            if isinstance(i, int) and i == 2:
                                dve.wait_ge(s_kr, 3)
                            rc.wait_full(dve, c, "ab")
                            ab = bank(2, T, 2 * D)
                            linkc(tt(t1, ab, coef[:, 0:2, :].rearrange("p m d -> p (m d)"), ALU.mult))
                            tt(t2, ab, coef[:, 2:4, :].rearrange("p m d -> p (m d)"), ALU.mult).then_inc(rc.dve, 1)
                            rc.wait_dve(dve, c, "ab")
                            tt(Y[:, 0:D], t1[:, 0:D], t2[:, D:2 * D], ALU.add).then_inc(c_Y, 1)
                            tt(Y[:, D:2 * D], t1[:, D:2 * D], t2[:, 0:D], ALU.add).then_inc(c_Y, 1)
                        if h == 13:
                            rc.wait_full(dve, c, "y")
                            dve.wait_ge(c_xd, c + 1)
                            tt(y, bank(2, T, D), xd, ALU.add).then_inc(rc.dve, 1)
                            rc.wait_dve(dve, c, "y")
                            linkc(tt(y, y, mo[:, 0:D], ALU.mult))
                            linkc(tt(y, y, mo[:, D:2 * D], ALU.add))
                            linkc(tt(z, z, y, ALU.add))
                    if has_b and h == 13:
                        split_low(rd, d, "c0", cTc[1][:, 0, :], cTc[0][:, 0, :], bank(2, CK, G))
                    if has_c and h == 14:
                        linkc(layer_norm(linkc, c_var, c_rstd, c * 3 + 1, y, z))
                        linkc(tt(y, y, gf_r, ALU.mult))
                        tt(h2, y, hf_r, ALU.add).then_inc(c_h2, 1)
                    if has_b and h == 14:
                        split_low(rd, d, "c1", cTc[1][:, 1, :], cTc[0][:, 1, :], bank(2, CK, G))
                    if has_a and h == 14 and not (isinstance(i, int) and i == NB - 1):
                        a_norm(i + 1)
                    if has_b and h == 15:
                        split_low(rd, d, "z", zT[1], zT[0], halves(bank(2, 128, 2 * T)))
                if has_a:
                    a_norm_heads(1)
                if has_c:
                    split_low(rc, c, "h", h2T[1], h2T[0], halves(bank(2, 128, 2 * T)))
                if has_a:
                    a_low_o(1)
                if has_c:
                    linkc(tt(z, z, c2_r, ALU.add))
                    dve.wait_ge(c_hh, c + 1)
                    tt(hidT[1], hid, hidT[0], ALU.subtract).then_inc(c_hl, 1)
                if has_a:
                    ra.wait_full(dve, a, "wo")
                    dve.wait_ge(a_xb, a + 1)
                    stt(X[:, a, :], bank(ra.bank["wo"], T, D), IWS, X[:, a, :], ALU.mult, ALU.add).then_inc(ra.dve, 1)
                    ra.wait_dve(dve, a, "wo")
                if has_c:
                    rc.wait_full(dve, c, "m2")
                    stt(z, bank(2, T, D), IWS, z, ALU.mult, ALU.add).then_inc(rc.dve, 1)
                    rc.wait_dve(dve, c, "m2")
                    linkc(layer_norm(linkc, c_var, c_rstd, c * 3 + 2, y, z))
                    linkc(tt(y, y, go_r, ALU.mult))
                    linkc(tt(y, y, ho_r, ALU.add))
                    tt(X[:, c, :], X[:, c, :], y, ALU.add).then_inc(c_xo, 1)
                    linkc.done()
                if has_b:
                    linkb.done()

            iterations(dve, body)

            link = Link(e_step, E_LINKS)
            dve.wait_ge(c_xo, NB)
            V_.memset(pr[:, 8:16], -1.0)
            V_.memset(pin[:, 2:8], -1.0)
            V_.memset(cw[:, :, 0:1], IWS)
            with dve.Fori(0, NB) as b:
                link.at(b)
                layer_norm(link, e_var, e_rstd, b, ze, X[:, b, :]).then_inc(e_z, 1)
                dve.wait_ge(e_zh, b + 1)
                tt(zt_t[1], bank(0, 128, 2 * T).rearrange("p (k t) -> p k t", k=2), zt_t[0], ALU.subtract).then_inc(e_zl, 1)
                dve.wait_ge(e_lg, b + 1)
                stt(lg, bank(1, T, 8), IWS, rbrow, ALU.mult, ALU.add).then_inc(e_lb, 1)
                wait_apart(dve, e_sg, b + 1)
                link(V_.max(pm8, pr))
                link(V_.tensor_copy(pin[:, 0:2], pm8[:, 0:2]), hold=True)
                link(V_.match_replace(prr, pin, pr, -2.0))
                link(tt(pne, pr[:, 0:8], prr[:, 0:8], ALU.not_equal))
                stt(cw[:, b, 1:9], pne, IWS, pr[:, 0:8], ALU.mult, ALU.mult).then_inc(e_cw, 1)
                link.done()

            def expert_weights(e, f):
                for k, (hi, lo) in enumerate((eg[f], eu[f], ed[f])):
                    dve.wait_ge(e_wh, e * 3 + k + 1)
                    stt(lo, estage[:, k, :].rearrange("p (a b) -> p a b", a=(2, 2, 4)[k]), WS, hi, ALU.mult,
                        ALU.subtract).then_inc(e_wl, 1)

            def expert(e, f, ahead):
                def combine(c):
                    for s in range(CHB):
                        bb = c * CHB + s
                        n = (e * NCH + c) * CHB + s
                        dve.wait_ge(e_o, n + 1)
                        dve.wait_ge(e_oa, n - NB + 1) if not isinstance(n, int) or n >= NB else None
                        stt(X[:, bb, :], bank(4 + s, T, D), cw[:, bb, bass.ds(e, 1)], X[:, bb, :], ALU.mult,
                            ALU.add).then_inc(e_oa, 1)

                for c in range(NCH):
                    for i4 in range(4):
                        n = (e * NCH + c) * 4 + i4
                        dve.wait_ge(e_si, n + 1)
                        dve.wait_ge(e_hl, n - 1) if not isinstance(n, int) or n >= 2 else None
                        stt(hf[:, i4 % 2, :], bank(2 * (i4 % 2) + 1, 128, CH), IWS, sg[:, i4 % 2, :], ALU.mult,
                            ALU.mult).then_inc(e_h, 1)
                        dve.wait_ge(e_hh, n + 1)
                        tt(hT[c % 2][1][:, i4, :], hf[:, i4 % 2, :], hT[c % 2][0][:, i4, :],
                           ALU.subtract).then_inc(e_hl, 1)
                    if c == 1 and ahead:
                        expert_weights(e + 1, 1 - f)
                    if c >= 1:
                        combine(c - 1)
                combine(NCH - 1)

            dve.wait_ge(e_cw, NB)
            expert_weights(0, 0)
            expert(0, 0, True)
            with dve.Fori(0, (NEXP - 1) // 2 - 1) as g:
                expert(g * 2 + 1, 1, True)
                expert(g * 2 + 2, 0, True)
            expert(NEXP - 2, 1, True)
            expert(NEXP - 1, 0, False)


S4_RE = 1
S4_ANG = 8
S4V_ALL = 36
S4P_HALF = 6 + 6 * 10
B_LINKS = 25
C_LINKS = 44
E_LINKS = 6


def _constants():
    n = 2 * T
    k = np.arange(T)
    ang = 2.0 * np.pi * (np.outer(k, k) % n) / n
    sign = (-1.0) ** k
    fa, fb = np.cos(ang), -np.sin(ang)
    fb = fb.copy()
    fb[:, 0] = sign
    scale = np.where(k == 0, 1.0, 2.0)[:, None] / n
    ia = scale * np.cos(ang)
    ib = -scale * np.sin(ang)
    ib[0] = sign / n
    m1 = np.cos(ang)
    m4 = np.cos(ang).copy()
    m4[:, 0] = sign
    m3 = -np.sin(ang)
    m3[:, 0] = 0.0
    m2 = -m3
    dft = np.stack([fa, fb, ia, ib, m1, m4, m3, m2]).astype(np.float32)
    return dft, np.eye(128, dtype=np.float32)


def kernel(**inputs):
    import numpy as _np
    import concourse.bacc as _bacc
    from concourse import mybir as _mybir
    from concourse.bass_utils import run_bass_kernel_spmd as _run

    nc = _bacc.Bacc("TRN2", target_bir_lowering=False, num_devices=1)
    data = {}
    for name, a in inputs.items():
        a = _np.asarray(a)
        if a.dtype == _np.bool_:
            a = a.view(_np.uint8)
        data[name] = a
    data["L1_xattn_mod_gate"] = data["L1_xattn_mod_gate"].reshape(1)
    data["L1_xattn_b1"] = data["L1_xattn_b1"].reshape(8, 128).T
    data["L1_xattn_log_dt"] = data["L1_xattn_log_dt"].reshape(2, 128).T
    for name in ("L0_ffn_w1", "L0_ffn_w2", "L1_ffn_Wr", "mask_BxS_bf1"):
        data[name] = data[name].T
    for new, shared, routed in (("e_gate", "L1_ffn_Wg_s", "L1_ffn_Wg"), ("e_up", "L1_ffn_Wu_s", "L1_ffn_Wu"),
                                ("e_down", "L1_ffn_Wd_s", "L1_ffn_Wd")):
        both = _np.concatenate([data.pop(shared)[None], data.pop(routed)])
        data[new] = both.transpose(0, 2, 1)
    data["dft"], data["ident"] = _constants()
    arrays, args = {}, {}
    for name, a in data.items():
        a = _np.ascontiguousarray(a)
        arrays[f"in_{name}_dram"] = a
        args[name] = nc.dram_tensor(f"in_{name}_dram", a.shape, _mybir.dt.from_np(a.dtype), kind="ExternalInput").ap()
    out = nc.dram_tensor("out_0_dram", (NB, T, D), F32, kind="ExternalOutput").ap()
    build(nc, args, out)
    r = _run(nc, [arrays], core_ids=[0])
    return r.results[0]["out_0_dram"]
```

```python
from contextlib import ExitStack

import numpy as np

import concourse.bass as bass
from concourse import mybir

ALU = mybir.AluOpType
ACT = mybir.ActivationFunctionType
F32 = mybir.dt.float32
F16 = mybir.dt.float16
BF16 = mybir.dt.bfloat16
U8 = mybir.dt.uint8
AX_X = mybir.AxisListType.X

NB, T, D = 16, 112, 256
G, DC = 375, 192
GJ, GC = 3, 125
CO = DC - 128
H0, DH0, IN0 = 16, 64, 1024
H1, DH1 = 4, 32
HID = 1024
NEXP, EI = 9, 512
NST = 64
PA, PBS = 7, 16
KR = 3
CHB = 4
CH = CHB * T
NCH = NB // CHB
WS = 256.0
IWS = 1.0 / WS
MAGIC = 12582912.0
EPS = 1e-5
NEG = -3.0e38
MASKED = 1.0e30
TWO_PI = 6.283185307179586
TP1 = 6.28125
TP2 = float(np.float32(TWO_PI - TP1))
TP3 = float(TWO_PI - TP1 - TP2)




class Ring:

    def __init__(self, items, banks, full, act, dve):
        self.names = [n for n, _ in items]
        self.who = dict(items)
        self.bank = {n: banks[k % len(banks)] for k, n in enumerate(self.names)}
        self.full, self.act, self.dve = full, act, dve
        self.n = len(items)
        self.na = sum("A" in w for _, w in items)
        self.nd = sum("D" in w for _, w in items)

    def upto(self, name, letter):
        k = self.names.index(name)
        return sum(letter in self.who[m] for m in self.names[: k + 1])

    def wait_full(self, eng, i, name):
        eng.wait_ge(self.full, i * self.n + self.names.index(name) + 1)

    def wait_act(self, eng, i, name):
        eng.wait_ge(self.act, i * self.na + self.upto(name, "A"))

    def wait_dve(self, eng, i, name):
        eng.wait_ge(self.dve, i * self.nd + self.upto(name, "D"))

    def wait_emptied(self, eng, i, name):
        if "D" in self.who[name]:
            self.wait_dve(eng, i, name)
        else:
            self.wait_act(eng, i, name)

    def wait_free(self, pe, i, name):
        k = self.names.index(name)
        before = [m for m in self.names[:k] if self.bank[m] == self.bank[name]]
        if before:
            self.wait_emptied(pe, i, before[-1])
            return
        last = [m for m in self.names if self.bank[m] == self.bank[name]][-1]
        if isinstance(i, int) and i == 0:
            return
        self.wait_emptied(pe, i - 1, last)


def build(nc, t, out):
    with ExitStack() as ctx:
        def sem(name):
            return ctx.enter_context(nc.semaphore(name))

        SB = 207 * 1024
        arena = ctx.enter_context(nc.sbuf_tensor("arena", [128, SB], U8))
        top = [0]

        def carve(parts, shape, dt, at=None):
            n = int(np.prod(shape)) * {F32: 4, F16: 2, BF16: 2, U8: 1}[dt]
            start = top[0] if at is None else at[0]
            end = start + (n + 31) // 32 * 32
            if at is None:
                top[0] = end
            else:
                at[0] = end
            assert end <= SB, (end, SB)
            v = arena[0:parts, start:start + n].bitcast(dt)
            if len(shape) == 2:
                v = v.rearrange("p (a b) -> p a b", a=shape[0])
            elif len(shape) == 3:
                v = v.rearrange("p (a b c) -> p a b c", a=shape[0], b=shape[1])
            return v

        psum = ctx.enter_context(nc.psum_tensor("psum", [128, 8, 512], F32))

        def bank(k, parts, n, off=0):
            return psum[0:parts, k, off:off + n]

        def bank16(k, parts, n):
            return psum[0:parts, k, :].bitcast(BF16)[:, 0:n]

        X = carve(T, (NB, D), F32)
        identf = carve(128, (128,), F32)
        identb = carve(128, (128,), BF16)
        neghalf = carve(T, (1,), F32)
        ones_b = carve(128, (T,), BF16)
        ones_f = carve(128, (128,), F32)
        st = carve(T, (2, 6), F32)
        mv = carve(T, (2,), F32)
        ve = carve(T, (1,), F32)
        rstd = carve(T, (1,), F32)
        amax = carve(T, (1,), F32)
        amc = carve(T, (1,), F32)
        qsc = carve(T, (1,), F32)
        dq1 = carve(T, (1,), F32)
        dq2 = carve(T, (1,), F32)
        cw = carve(T, (NB, NEXP), F32)
        rbrow = carve(T, (8,), F32)
        wr_f = carve(128, (2, 8), F32)
        wr_hi = carve(128, (2, 8), F16)
        wr_lo = carve(128, (2, 8), F16)
        kept = top[0]

        def pair(parts, shape):
            return carve(parts, shape, F16), carve(parts, shape, F16)

        wq = pair(128, (2, IN0))
        wk = pair(128, (2, IN0))
        wv = pair(128, (2, IN0))
        wo = pair(128, (8, D))
        w1q = carve(128, (2, HID), BF16)
        w2q = carve(128, (8, D), BF16)
        uq = pair(128, (2, 128))
        uk = pair(128, (2, 128))
        uv = pair(128, (2, D))
        ufi = pair(128, (2, 2 * D))
        ufo = pair(128, (2, 2 * D))
        u1 = pair(128, (2, HID))
        u2 = pair(128, (8, D))
        dft = carve(T, (4, T), F32)
        coef = carve(T, (4, D), F32)
        b1row = carve(T, (HID,), F32)
        g2row = carve(T, (HID,), F32)
        h2row = carve(T, (HID,), F32)
        rows = carve(T, (12, D), F32)
        (bo_r, g1_r, h1_r, b2_r, gi_r, hi_r, go_r, ho_r, gf_r, hf_r, dsk_r, c2_r) = (rows[:, k, :] for k in range(12))
        mbi = carve(T, (2 * D,), F32)
        mbo = carve(T, (2 * D,), F32)
        b1col = carve(128, (8,), F32)
        mg = carve(T, (1,), F32)
        mgs = carve(T, (1,), F32)
        tmask8 = carve(T, (NB,), U8)
        tmask = carve(T, (NB,), F32)
        wmean = carve(128, (2,), F32)
        wsc = carve(128, (2,), F32)
        wab = carve(128, (2,), F32)
        ldt = carve(128, (2,), F32)
        dtc = carve(128, (2,), F32)
        kpow = carve(128, (2, T), F32)
        work = top[0]

        ctx_sb = carve(GC, (GJ, DC), F32)         
        cT = pair(128, (2, G)), pair(128, (2, G))
        xn = carve(T, (D,), F32)
        xT = pair(128, (2, T))
        qT = carve(128, (H0, T), F32)
        kT = carve(128, (KR, G), F32)
        V = carve(GC, (GJ, IN0), F32)
        Pr = carve(T, (2, G), F32)
        PTs = carve(GC, (2, GJ * T), F32)
        nmx = carve(T, (H0,), F32)
        rsum = carve(T, (H0,), F32)
        rinv = carve(T, (H0,), F32)
        On = carve(T, (512,), F32)
        aT = pair(128, (8, T))
        zb = xn
        q1 = carve(T, (D,), BF16)
        hq1 = carve(128, (2, T), BF16)
        ub = carve(T, (HID,), F32)
        q2 = carve(T, (HID,), BF16)
        hq2 = carve(128, (8, T), BF16)
        work = top[0]
        zn = carve(T, (D,), F32)
        zT = pair(128, (2, T))
        q1T = carve(128, (T,), F32)
        k1T = carve(128, (G,), F32)
        V1 = carve(GC, (GJ, D), F32)
        vm8 = carve(128, (G,), U8)
        vmb = carve(128, (G,), BF16)
        z = carve(T, (D,), F32)
        work_c = top[0]
        top8 = carve(T, (2, 4, 8), F32)
        nmx1 = carve(T, (H1,), F32)
        R1 = carve(T, (G,), F32)
        P1 = carve(T, (H1, G), F32)
        sum1 = carve(T, (H1,), F32)
        r1 = carve(T, (H1,), F32)
        r2 = carve(T, (H1,), F32)
        dg = carve(T, (H1, T), F32)
        later = [top[0]]
        atT = carve(GC, (GJ * T,), F32)
        ctT = pair(128, (2, T))
        h2T = carve(128, (2, T), F16, later), carve(128, (2, T), F16, later)
        h2 = carve(T, (D,), F32, later)
        assert later[0] <= top[0]
        later = [top[0]]
        mi = carve(T, (2 * D,), F32)
        Y = mi
        mo = carve(T, (2 * D,), F32)
        hidT = carve(128, (8, T), F16, later), carve(128, (8, T), F16, later)
        assert later[0] <= top[0]
        x1 = carve(T, (D,), F32)
        y = x1
        xd = carve(T, (D,), F32)
        later = [top[0]]
        t1 = carve(T, (2 * D,), F32)
        t2 = carve(T, (2 * D,), F32)
        once = [later[0]]
        hid = carve(128, (8, T), F32, later)
        dft_k = carve(T, (4, T), F32, once)
        kt = carve(T, (D,), F32, once)
        assert max(later[0], once[0]) <= top[0]
        assert top[0] <= SB
        w = [work]
        stage = [carve(128, (2048,), F32, w)]
        assert w[0] <= work_c
        w = [work_c]
        s4 = {n: carve(128, (2, NST), F32, w) for n in ("zr", "zi", "dr", "di")}
        dead = w[0]
        s4.update({n: carve(128, (2, NST), F32, w) for n in
                   ("ar", "ai", "cr", "ci", "re", "im", "th", "k", "s", "sh", "e1", "mr", "t1", "t2")})
        w = [dead]
        p1 = carve(128, (PBS, NST), F32, w)
        p2 = carve(128, (PBS, NST), F32, w)
        vr = carve(128, (PBS + 1, NST), F32, w)
        vi = carve(128, (PBS + 1, NST), F32, w)
        ur = carve(128, (PA, NST), F32, w)
        ui = carve(128, (PA, NST), F32, w)
        assert w[0] <= SB
        stage.append(arena[0:128, SB - 8192:SB].bitcast(F32))
        w = [kept]
        ZT = carve(128, (2, NB * T), F16, w), carve(128, (2, NB * T), F16, w)
        ste = carve(T, (CHB, 6), F32, w)
        mve = carve(T, (CHB, 2), F32, w)
        vee = carve(T, (CHB,), F32, w)
        rstde = carve(T, (CHB,), F32, w)
        ze = carve(T, (CHB, D), F32, w)
        zt_t = carve(128, (2, CH), F16, w), carve(128, (2, CH), F16, w)
        pr = carve(T, (CHB, 16), F32, w)
        pm8 = carve(T, (CHB, 8), F32, w)
        pin = carve(T, (CHB, 8), F32, w)
        prr = carve(T, (CHB, 16), F32, w)
        pne = carve(T, (CHB, 8), F32, w)
        lg = carve(T, (CHB, 8), F32, w)
        estage = carve(128, (3, 1024), F32, w)
        eg = [(carve(128, (2, EI), F16, w), carve(128, (2, EI), F16, w)) for _ in range(2)]
        eu = [(carve(128, (2, EI), F16, w), carve(128, (2, EI), F16, w)) for _ in range(2)]
        ed = [(carve(128, (4, D), F16, w), carve(128, (4, D), F16, w)) for _ in range(2)]
        sg = carve(128, (2, CH), F32, w)
        hf = carve(128, (2, CH), F32, w)
        hT = [(carve(128, (4, CH), F16, w), carve(128, (4, CH), F16, w)) for _ in range(2)]

        s_x = sem("x_loaded")
        s_const = sem("constants_loaded")
        s_stage = [sem("weight_staged_even"), sem("weight_staged_odd")]
        s_hi = sem("weight_high_part")
        s_lo = sem("weight_done")
        s_wab = sem("weight_rows_summed")
        s_wsum = sem("weight_magnitude_summed")
        s_misc = sem("small_constants_ready")
        s_pmisc = sem("pool_constants_ready")
        s_dset = sem("vector_setup_step")
        s_s4a = sem("s4d_activation")
        s_s4v = sem("s4d_vector_step")
        s_s4p = sem("s4d_pool_step")

        consts = []
        for k, n in enumerate(("L0_xattn_bo", "L0_ffn_ln1_g", "L0_ffn_ln1_b", "L0_ffn_b2", "L1_xattn_g_norm_in",
                               "L1_xattn_b_norm_in", "L1_xattn_g_norm_out", "L1_xattn_b_norm_out", "L1_xattn_g_ffn",
                               "L1_xattn_b_ffn", "L1_xattn_D_skip", "L1_xattn_b2")):
            consts.append((rows[:, k, :], t[n].partition_broadcast(T)))
        consts += [(b1row, t["L0_ffn_b1"].partition_broadcast(T)), (g2row, t["L0_ffn_ln2_g"].partition_broadcast(T)),
                   (h2row, t["L0_ffn_ln2_b"].partition_broadcast(T)),
                   (mbi, t["L1_xattn_b_film_in"].partition_broadcast(T)),
                   (mbo, t["L1_xattn_b_film_out"].partition_broadcast(T)),
                   (b1col, t["L1_xattn_b1"]),
                   (mg, t["L1_xattn_mod_gate"].partition_broadcast(T)),
                   (rbrow, t["L1_ffn_rb"].partition_broadcast(T)),
                   (tmask8, t["mask_BxS_bf1"]),
                   (wr_f, t["L1_ffn_Wr"].rearrange("(k p) e -> p k e", p=128)),
                   (dft, t["dft"][0:4].rearrange("m p k -> p m k")),
                   (identf, t["ident"]),
                   (ldt, t["L1_xattn_log_dt"])]
        for n, k in (("L1_xattn_A_re", "ar"), ("L1_xattn_A_im", "ai"), ("L1_xattn_C_re", "cr"), ("L1_xattn_C_im", "ci")):
            consts.append((s4[k], t[n].rearrange("(h p) n -> p h n", p=128)))
        NCONST = len(consts)

        def kview(name, k):
            return t[name].rearrange("(k p) n -> p k n", k=k)

        splits = [("L0_xattn_Wq", 128, 2, IN0, wq), ("L0_xattn_Wk", 128, 2, IN0, wk), ("L0_xattn_Wv", 128, 2, IN0, wv),
                  ("L0_xattn_Wo", 128, 8, D, wo),
                  ("L1_xattn_Wq", 128, 2, 128, uq), ("L1_xattn_Wk", 128, 2, 128, uk), ("L1_xattn_Wv", 128, 2, D, uv),
                  ("L1_xattn_W_film_in", 128, 2, 2 * D, ufi), ("L1_xattn_W_film_out", 128, 2, 2 * D, ufo),
                  ("L1_xattn_W1", 128, 2, HID, u1), ("L1_xattn_W2", 128, 8, D, u2)]
        quants = [("L0_ffn_w1", 128, 2, HID, w1q), ("L0_ffn_w2", 128, 8, D, w2q)]
        NSPL = len(splits)
        NW = NSPL + len(quants)

        NFIRST = 4

        def staged(k, parts, a, b):
            return stage[k % 2 if k < NFIRST else 0][0:parts, 0:a * b].rearrange("p (a b) -> p a b", a=a)

        def s_staged(k):
            return s_stage[k % 2 if k < NFIRST else 0], 16 * (k // 2 + 1 if k < NFIRST else NFIRST // 2 + k - NFIRST + 1)

        weights = splits[:NFIRST] + quants + splits[NFIRST:]

        s_ctx = sem("context_loaded")
        a_var = sem("a_variance_ready")
        a_rstd = sem("a_inverse_deviation")
        a_step = sem("a_vector_step")
        a_xn = sem("a_normed")
        a_xb = sem("a_bias_added")
        a_S = sem("a_scores_ready")
        a_mx = sem("a_maximum_ready")
        a_E = sem("a_probs_ready")
        a_pt = sem("a_probs_transposed")
        a_pk = sem("a_transposed_kept")
        a_O = sem("a_head_outputs_ready")
        a_ri = sem("a_sums_inverted")
        a_On = sem("a_outputs_normed")
        ra = Ring([("q0", "A"), ("q1", "A"), ("k0", "A"), ("k1", "A"), ("v0", "A"), ("v1", "A"), ("v2", "A"),
                   ("k2", "A"), ("v3", "A"), ("k3", "A"), ("v4", "A"), ("k4", "A"), ("v5", "A"), ("k5", "A"),
                   ("k6", "A"), ("k7", "A"), ("o0", "AD")], (0, 1), sem("a_bank_filled"),
                  sem("a_bank_read_by_scalar"), sem("a_bank_read_by_vector"))
        ro = Ring([("o1", "AD"), ("wo", "D")], (7, 6), sem("a_end_filled"), sem("a_end_read_by_scalar"),
                  sem("a_end_read_by_vector"))
        rp = Ring([("c0", "AD"), ("xn", "AD"), ("c1", "AD")], (3,), sem("p_bank_filled"),
                  sem("p_bank_read_by_scalar"), sem("p_bank_read_by_vector"))
        b_var = sem("b_variance_ready")
        b_rstd = sem("b_inverse_deviation")
        b_step = sem("b_vector_step")
        b_rcp = sem("b_quantizer_scales")
        b_z = sem("b_normed")
        b_xb = sem("b_bias_added")
        b_q = sem("b_quantized")
        b_g = sem("b_gelu_done")
        rb = Ring([("t1", "A"), ("m0", "D"), ("m1", "D"), ("t2", "A"), ("m2", "D")], (2,),
                  sem("b_bank_filled"), sem("b_bank_read_by_scalar"), sem("b_bank_read_by_vector"))
        d_vm8 = sem("d_mask_loaded")
        d_vm = sem("d_mask_bias_ready")
        d_var = sem("d_variance_ready")
        d_rstd = sem("d_inverse_deviation")
        d_step = sem("d_vector_step")
        d_zn = sem("d_normed")
        rd = Ring([("k", "A"), ("z", "AD"), ("v0", "A"), ("v1", "A"), ("q", "A")], (3,),
                  sem("d_bank_filled"), sem("d_bank_read_by_scalar"), sem("d_bank_read_by_vector"))
        c_z = sem("c_normed_copied")
        c_var = sem("c_variance_ready")
        c_rstd = sem("c_inverse_deviation")
        c_step = sem("c_vector_step")
        c_step2 = sem("e_end_vector_step")
        c_S = sem("c_scores_ready")
        c_top = sem("c_top_values")
        c_took = sem("c_top_values_taken_out")
        c_nm = sem("c_maximum_scaled")
        c_E = sem("c_exponentials")
        c_r = sem("c_row_factors")
        c_dg = sem("c_diagonals")
        c_zb = sem("c_output_bias_added")
        c_y = sem("c_output_normed")
        c_xn = sem("c_input_normed")
        c_zy = sem("c_state_output_added")
        c_pool = sem("c_pool_step")
        c_x1 = sem("c_modulated")
        c_xd = sem("c_skip_term")
        c_Y = sem("c_spectrum_ready")
        c_h2 = sem("c_ffn_input")
        c_hh = sem("c_hidden_high_part")
        c_hl = sem("c_hidden_split")
        c_xo = sem("c_residual_updated")
        rc = Ring([("at", "A"), ("ct", "AD"), ("fi", "D"), ("fo", "D"), ("ab", "D"), ("y", "D"), ("h", "AD"),
                   ("m0", "A"), ("m1", "A"), ("m2", "D")], (2,), sem("c_bank_filled"), sem("c_bank_read_by_scalar"),
                  sem("c_bank_read_by_vector"))
        rings = {"P": (rp, -1), "B": (rb, 1), "D": (rd, 1), "C": (rc, 2), "E": (rc, 3)}
        ORDER = {2: [("E", "h"), ("E", "m0"), ("E", "m1"), ("B", "t1"), ("B", "m0"), ("B", "m1"), ("E", "m2"),
                     ("D", "k"), ("B", "t2"), ("B", "m2"), ("C", "at"), ("C", "ct"), ("C", "fi"), ("C", "fo"),
                     ("C", "ab"), ("C", "y")],
                 3: [("D", "z"), ("D", "v0"), ("D", "v1"), ("D", "q"), ("P", "c0"), ("P", "xn"), ("P", "c1")]}

        def wait_bank(pe, i, bank_, stage, name=None):
            order = ORDER[bank_]
            here = order.index((stage, name)) if name else len(order)
            for back, upto in ((0, here), (1, len(order)), (2, len(order))):
                for st_, n in reversed(order[:upto]):
                    ring, lag = rings[st_]
                    j = i - lag - back
                    if isinstance(i, int) and not 0 <= j < NB:
                        continue
                    ring.wait_emptied(pe, j, n)
                    return

        s_dftk = sem("kernel_transforms_loaded")
        s_kf = sem("kernel_spectrum_filled")
        s_kr = sem("kernel_spectrum_kept")
        s_s4c = sem("s4d_contracted")
        s_s4d = sem("s4d_contraction_step")
        e_var = sem("e_variance_ready")
        e_rstd = sem("e_inverse_deviation")
        e_step = sem("e_vector_step")
        e_top = sem("e_routing_step")
        e_z = sem("e_normed")
        e_tr = sem("e_transposed")
        e_zh = sem("e_tokens_high_part")
        e_zl = sem("e_tokens_split")
        e_zc = sem("e_tokens_copied")
        e_lg = sem("e_logits_ready")
        e_lb = sem("e_logits_biased")
        e_sg = sem("e_gates_ready")
        e_cw = sem("e_gate_weights")
        e_wd = [sem("e_gate_loaded"), sem("e_up_loaded"), sem("e_down_loaded")]
        e_wh = sem("e_expert_weights_high_part")
        e_wl = sem("e_expert_weights_split")
        e_gu = sem("e_gate_up_filled")
        e_si = sem("e_silu_done")
        e_h = sem("e_hidden_ready")
        e_hh = sem("e_hidden_high_part")
        e_hl = sem("e_hidden_split")
        e_o = sem("e_down_filled")
        e_oa = sem("e_down_added")
        s_out = sem("output_written")

        def wait_apart(eng, semaphore, count):
            if not isinstance(count, int):
                eng.lower_val(count)
            eng.wait_ge(s_x, 16)
            eng.wait_ge(semaphore, count)

        block = ctx.enter_context(nc.Block())

        def iterations(eng, body):
            def at(i, f, n):
                body(i, f, n < NB - 1, n < NB, 1 <= n <= NB, 2 <= n <= NB + 1, 3 <= n)

            for i in range(3):
                at(i, i % 2, i)
            with eng.Fori(0, (NB - 4) // 2) as g:
                at(g * 2 + 3, 1, 3)
                at(g * 2 + 4, 0, 4)
            for i in range(NB - 1, NB + 3):
                at(i, i % 2, i)

        @block.sync
        def _(sp):
            sp.dma_start(X, t["x"].rearrange("b t d -> t b d")).then_inc(s_x, 16)

            def context(j):
                sp.dma_start(ctx_sb, t["ctx_768"][j].rearrange("(j p) c -> p j c", p=GC)).then_inc(s_ctx, 16)

            def weight(k):
                name, parts, a, b, _ = weights[k]
                sp.dma_start(staged(k, parts, a, b), kview(name, a)).then_inc(s_staged(k)[0], 16)

            weight(0)
            weight(1)
            context(0)
            for dst, src in consts:
                sp.dma_start(dst, src).then_inc(s_const, 16)
            for k in range(2, NW):
                sp.wait_ge(s_lo, k - 1 if k < NFIRST else k)
                weight(k)

            def mask(j):
                if not isinstance(j, int) or j > 0:
                    wait_apart(sp, d_vm, j)
                sp.dma_start(vm8, t["mask_BxS2_bf1"][j].partition_broadcast(128)).then_inc(d_vm8, 16)

            def next_context(i):
                rp.wait_full(sp, i, "c1")
                context(i + 1)

            next_context(0)
            sp.wait_ge(s_lo, NW)
            next_context(1)
            mask(0)
            sp.wait_ge(s_s4c, 2 * PA)
            sp.dma_start(dft_k, t["dft"][4:8].rearrange("m p k -> p m k")).then_inc(s_dftk, 16)
            with sp.Fori(2, NB - 1) as i:
                next_context(i)
                mask(i - 1)
            mask(NB - 2)
            mask(NB - 1)
            sp.wait_ge(c_xo, NB)
            for e in range(NEXP):
                if e >= 1:
                    sp.wait_ge(e_wl, 3 * e)
                sp.dma_start(estage[:, 0, :].rearrange("p (k n) -> p k n", k=2),
                             t["e_gate"][e].rearrange("(k p) n -> p k n", p=128)).then_inc(e_wd[0], 16)
                sp.dma_start(estage[:, 1, :].rearrange("p (k n) -> p k n", k=2),
                             t["e_up"][e].rearrange("(k p) n -> p k n", p=128)).then_inc(e_wd[1], 16)
                sp.dma_start(estage[:, 2, :].rearrange("p (k n) -> p k n", k=4),
                             t["e_down"][e].rearrange("(k p) n -> p k n", p=128)).then_inc(e_wd[2], 16)
            sp.wait_ge(e_oa, NEXP * NB)
            sp.dma_start(out.rearrange("b t d -> t b d"), X).then_inc(s_out, 16)
            sp.wait_ge(s_out, 16)

        @block.tensor
        def _(pe):
            mm = nc.tensor.matmul
            A = slice(None)

            def mm3(o, lh, rh, first, last):
                mm(o, lh[0], rh[0], start=first, stop=False)
                mm(o, lh[0], rh[1], start=False, stop=False)
                return mm(o, lh[1], rh[0], start=False, stop=last)

            def part(p, *ix):
                return p[0][ix], p[1][ix]

            def turn(o, src, m):
                for k, x in enumerate(src):
                    i = nc.tensor.transpose(o[:, k * m:(k + 1) * m], x, identf[0:m, 0:m])
                return i

            def body(i, f, has_p, has_a, has_b, has_c, has_e):
                a, b, d, c, e = i, i - 1, i - 1, i - 2, i - 3
                if isinstance(i, int) and i == 0:
                    pe.wait_ge(s_lo, NFIRST)
                if isinstance(i, int) and i == 1:
                    pe.wait_ge(s_lo, NW)

                def a_q(q):
                    ra.wait_free(pe, a, f"q{q}")
                    for m in range(4):
                        for k in range(2):
                            x = (q * 4 + m) * 128
                            n = mm3(bank(ra.bank[f"q{q}"], 128, T, m * T), part(wq, A, k, slice(x, x + 128)),
                                    part(xT, A, k, A), k == 0, k == 1)
                    n.then_inc(ra.full, 1)

                def a_k(m):
                    ra.wait_free(pe, a, f"k{m}")
                    for k in range(2):
                        n = mm3(bank(ra.bank[f"k{m}"], 128, G), part(wk, A, k, slice(m * 128, m * 128 + 128)),
                                part(cT[f], A, k, A), k == 0, k == 1)
                    n.then_inc(ra.full, 1)

                def a_v(m):
                    half, j = m // 3, m % 3
                    ra.wait_free(pe, a, f"v{m}")
                    for k in range(2):
                        n = mm3(bank(ra.bank[f"v{m}"], GC, 512), part(cT[f], A, k, slice(j * GC, j * GC + GC)),
                                part(wv, A, k, slice(half * 512, half * 512 + 512)), k == 0, k == 1)
                    n.then_inc(ra.full, 1)

                def a_scores(h):
                    mm(bank(4 + h % 2, T, G), qT[:, h, :], kT[:, h // 2 % KR, :], start=True,
                       stop=True).then_inc(a_S, 1)

                def a_turn(h):
                    pe.wait_ge(a_E, a * H0 + h + 1)
                    if h:
                        pe.wait_ge(a_pk, a * H0 + h)
                    elif has_b:
                        ro.wait_dve(pe, b, "wo")
                    turn(bank(6, GC, GJ * T), [Pr[:, h % 2, j * GC:(j + 1) * GC] for j in range(GJ)],
                         T).then_inc(a_pt, 1)

                def a_pv(h):
                    if h == 0:
                        ra.wait_act(pe, a, "v2")
                        if has_b:
                            ro.wait_emptied(pe, b, "o1")
                    if h == 8:
                        ra.wait_act(pe, a, "v5")
                        pe.wait_ge(a_On, a * 2 + 1)
                    pe.wait_ge(a_pk, a * H0 + h + 1)
                    for j in range(GJ):
                        n = mm(bank(7, T, DH0, (h % 8) * DH0), PTs[:, h % 2, j * T:(j + 1) * T],
                               V[:, j, h * DH0:(h + 1) * DH0], start=(j == 0), stop=(j == GJ - 1))
                    if h % 8 == 7:
                        n.then_inc(a_O, 1)

                def a_o(ring, j, q):
                    pe.wait_ge(a_On, j * 2 + q + 1)
                    if q == 0:
                        ra.wait_free(pe, j, "o0")
                    turn(bank(ring.bank[f"o{q}"], 128, 4 * T), [On[:, m * 128:(m + 1) * 128] for m in range(4)],
                         T).then_inc(ring.full, 1)

                def a_wo():
                    ra.wait_emptied(pe, b, "o0")
                    pe.wait_ge(a_pk, b * H0 + H0)
                    for m in range(8):
                        if m == 4:
                            ro.wait_emptied(pe, b, "o1")
                        n = mm3(bank(ro.bank["wo"], T, D), part(aT, A, m, A), part(wo, A, m, A), m == 0, m == 7)
                    n.then_inc(ro.full, 1)

                def b_turn(n, src, cnt, count):
                    pe.wait_ge(b_q, b * 2 + count)
                    wait_bank(pe, i, 2, "B", n)
                    for k in range(cnt):
                        x = nc.tensor.transpose(bank16(2, 128, cnt * T)[:, k * T:(k + 1) * T],
                                                src[:, k * 128:(k + 1) * 128], identb[0:T, 0:T])
                    x.then_inc(rb.full, 1)

                def b_m(m):
                    if m == 0:
                        rb.wait_act(pe, b, "t1")
                    wait_bank(pe, i, 2, "B", f"m{m}")
                    for k in range(2):
                        n = mm(bank(2, T, 512), hq1[:, k, :], w1q[:, k, m * 512:(m + 1) * 512], start=(k == 0),
                               stop=(k == 1))
                    n.then_inc(rb.full, 1)

                def b_out():
                    wait_bank(pe, i, 2, "B", "m2")
                    for k in range(8):
                        n = mm(bank(2, T, D), hq2[:, k, :], w2q[:, k, :], start=(k == 0), stop=(k == 7))
                    n.then_inc(rb.full, 1)

                def scores1(j, h):
                    if h:
                        pe.wait_ge(c_E, j * H1 + h)
                    else:
                        rd.wait_act(pe, j, "q")
                        pe.wait_ge(d_vm, j + 1)
                        wait_bank(pe, i - 1, 3, "end")
                    r = 32 * h
                    mm(bank(3, T, G), ones_b[r:r + 1, :], vmb[r:r + 1, :], start=True, stop=False)
                    mm(bank(3, T, G), q1T[r:r + 32, :], k1T[r:r + 32, :], start=False, stop=True).then_inc(c_S, 1)

                def d_z():
                    pe.wait_ge(d_zn, d + 1)
                    if has_c:
                        pe.wait_ge(c_E, c * H1 + H1)
                    wait_bank(pe, i, 3, "D", "z")
                    turn(bank(3, 128, 2 * T), [zn[:, 0:128], zn[:, 128:256]], T).then_inc(rd.full, 1)

                def d_q():
                    rd.wait_emptied(pe, d, "z")
                    wait_bank(pe, i, 3, "D", "q")
                    for k in range(2):
                        n = mm3(bank(3, 128, T), part(uq, A, k, A), part(zT, A, k, A), k == 0, k == 1)
                    n.then_inc(rd.full, 1)

                def d_k():
                    wait_bank(pe, i, 2, "D", "k")
                    for k in range(2):
                        n = mm3(bank(2, 128, G), part(uk, A, k, A), part(cT[1 - f], A, k, A), k == 0, k == 1)
                    n.then_inc(rd.full, 1)

                def d_v(n_, js):
                    wait_bank(pe, i, 3, "D", n_)
                    for j in js:
                        for k in range(2):
                            n = mm3(bank(3, GC, D, (j % 2) * D), part(cT[1 - f], A, k, slice(j * GC, j * GC + GC)),
                                    part(uv, A, k, A), k == 0, k == 1)
                    n.then_inc(rd.full, 1)

                def c_at():
                    wait_bank(pe, i, 2, "C", "at")
                    for j in range(GJ):
                        for h in range(H1):
                            if j == 0:
                                pe.wait_ge(c_dg, c * H1 + h + 1)
                            n = mm(bank(2, GC, T, j * T), P1[:, h, j * GC:(j + 1) * GC], dg[:, h, :],
                                   start=(h == 0), stop=(h == H1 - 1))
                    n.then_inc(rc.full, 1)

                def c_ct():
                    wait_bank(pe, i, 2, "C", "ct")
                    for m in range(2):
                        for j in range(GJ):
                            n = mm(bank(2, 128, T, m * T), V1[:, j, m * 128:(m + 1) * 128],
                                   atT[:, j * T:(j + 1) * T], start=(j == 0), stop=(j == GJ - 1))
                    n.then_inc(rc.full, 1)

                def c_film(n_, u):
                    wait_bank(pe, i, 2, "C", n_)
                    for k in range(2):
                        n = mm3(bank(2, T, 2 * D), part(ctT, A, k, A), part(u, A, k, A), k == 0, k == 1)
                    n.then_inc(rc.full, 1)

                def c_ab():
                    pe.wait_ge(c_x1, c + 1)
                    wait_bank(pe, i, 2, "C", "ab")
                    for m in range(2):
                        n = mm(bank(2, T, D, m * D), dft[:, m, :], x1, start=True, stop=True)
                    n.then_inc(rc.full, 1)

                def c_y():
                    pe.wait_ge(c_Y, c * 2 + 2)
                    wait_bank(pe, i, 2, "C", "y")
                    for m in range(2):
                        n = mm(bank(2, T, D), dft[:, 2 + m, :], Y[:, m * D:(m + 1) * D], start=(m == 0), stop=(m == 1))
                    n.then_inc(rc.full, 1)

                def e_h():
                    pe.wait_ge(c_h2, e + 1)
                    wait_bank(pe, i, 2, "E", "h")
                    turn(bank(2, 128, 2 * T), [h2[:, 0:128], h2[:, 128:256]], T).then_inc(rc.full, 1)

                def e_m(q):
                    rc.wait_emptied(pe, e, "h")
                    wait_bank(pe, i, 2, "E", f"m{q}")
                    for m in range(4):
                        for k in range(2):
                            x = (q * 4 + m) * 128
                            n = mm3(bank(2, 128, T, m * T), part(u1, A, k, slice(x, x + 128)),
                                    part(h2T, A, k, A), k == 0, k == 1)
                    n.then_inc(rc.full, 1)

                def e_out():
                    pe.wait_ge(c_hl, e + 1)
                    wait_bank(pe, i, 2, "E", "m2")
                    for m in range(8):
                        n = mm3(bank(2, T, D), part(hidT, A, m, A), part(u2, A, m, A), m == 0, m == 7)
                    n.then_inc(rc.full, 1)

                if has_a:
                    rp.wait_emptied(pe, a, "xn")
                    a_q(0)
                if has_c:
                    scores1(c, 0)
                if has_b:
                    a_o(ro, b, 1)
                if has_a:
                    a_q(1)
                if has_e:
                    e_h()
                if has_a:
                    rp.wait_emptied(pe, a, "c1")
                    a_k(0)
                    a_k(1)
                if has_b:
                    a_wo()
                if has_a:
                    ra.wait_act(pe, a, "k0")
                    a_scores(0)
                    a_scores(1)
                    a_v(0)
                if has_e:
                    e_m(0)
                if has_a:
                    a_v(1)
                if has_e:
                    e_m(1)
                if has_a:
                    a_v(2)
                for h in range(H0):
                    if has_a:
                        a_turn(h)
                        if h + 2 < H0:
                            if h % 2 == 0:
                                ra.wait_act(pe, a, f"k{h // 2 + 1}")
                            a_scores(h + 2)
                    if isinstance(i, int) and i == 0 and h in (1, 2):
                        pe.wait_ge(s_wab, h)
                        mm(bank(4 - h, 128, 1), ones_f, wab[:, h - 1:h], start=True, stop=True).then_inc(s_wsum, 1)
                    if has_p and h == 15:
                        p_tokens(i + 1)
                    if has_e and h == 4:
                        e_out()
                    if has_c:
                        if h == 11:
                            c_at()
                        if h == 12:
                            rc.wait_emptied(pe, c, "ct")
                            c_film("fi", ufi)
                    if has_a:
                        if h >= 1:
                            a_pv(h - 1)
                        if h in (0, 2, 4, 6, 8, 10):
                            a_k(h // 2 + 2)
                        if h in (1, 3, 5):
                            a_v(h // 2 + 3)
                        if h == 10:
                            a_o(ra, a, 0)
                    if has_c:
                        if h in (0, 2, 5):
                            scores1(c, 1 + (h + 1) // 3)
                        if h == 11:
                            rc.wait_act(pe, c, "at")
                            c_ct()
                        if h == 12:
                            c_film("fo", ufo)
                        if h == 13 and isinstance(i, int) and i == 2:
                            pe.wait_ge(s_s4c, 2 * PA)
                            pe.wait_ge(s_dftk, 16)
                            wait_bank(pe, i, 2, "C", "ab")
                            for m in range(2):
                                n = nc.tensor.transpose(bank(2, T, 128, m * 128), kpow[:, m, :], identf)
                            n.then_inc(s_kf, 1)
                            for q in range(2):
                                pe.wait_ge(s_kr, 1 + q)
                                for m in range(2):
                                    n = mm(bank(2, T, D, m * D), dft_k[:, q * 2 + m, :], kt, start=True, stop=True)
                                n.then_inc(s_kf, 1)
                            pe.wait_ge(s_kr, 3)
                        if h == 13:
                            c_ab()
                        if h == 14:
                            c_y()
                    if has_b:
                        if h == 0:
                            b_turn("t1", q1, 2, 1)
                        if h in (1, 2):
                            b_m(h - 1)
                        if h == 6:
                            d_k()
                        if h == 8:
                            b_turn("t2", q2, 8, 2)
                        if h == 9:
                            rb.wait_act(pe, b, "t2")
                            b_out()
                        if h == 11:
                            d_z()
                        if h == 12:
                            d_v("v0", (0, 1))
                        if h == 13:
                            d_v("v1", (2,))
                        if h == 14:
                            d_q()
                    if has_p:
                        if h == 14:
                            p_context(i + 1, 0)
                if has_a:
                    a_pv(H0 - 1)
                if has_p:
                    p_context(i + 1, 1)

            def p_context(j, k):
                if k == 0:
                    pe.wait_ge(s_ctx, 16 * (j + 1))
                wait_bank(pe, j - 1, 3, "P", f"c{k}")
                turn(bank(3, 128, G), [ctx_sb[:, x, k * CO:k * CO + 128] for x in range(GJ)], GC).then_inc(rp.full, 1)

            def p_tokens(j):
                pe.wait_ge(a_xn, j + 1)
                wait_bank(pe, j - 1, 3, "P", "xn")
                turn(bank(3, 128, 2 * T), [xn[:, 0:128], xn[:, 128:256]], T).then_inc(rp.full, 1)

            pe.wait_ge(s_const, 16 * NCONST)
            pe.wait_ge(s_pmisc, 4)
            p_context(0, 0)
            p_tokens(0)
            p_context(0, 1)
            iterations(pe, body)

            with pe.Fori(0, NCH) as g:
                for q in range(CHB):
                    pe.wait_ge(e_z, g * CHB + q + 1)
                    for k in range(2):
                        i = nc.tensor.transpose(bank(k, 128, T, q * T), ze[:, q, k * 128:(k + 1) * 128],
                                                identf[0:T, 0:T])
                i.then_inc(e_tr, 1)
                pe.wait_ge(e_zl, g * 2 + 2)
                for q in range(CHB):
                    for k in range(2):
                        i = mm3(bank(2, T, 8, q * 8), part(zt_t, A, k, slice(q * T, q * T + T)),
                                part((wr_hi, wr_lo), A, k, A), k == 0, k == 1)
                i.then_inc(e_lg, 1)
            pe.wait_ge(e_zc, 2 * NCH)

            def expert(e, f):
                def gate_up(c):
                    tok = slice(c * CH, (c + 1) * CH)
                    for i4 in range(4):
                        n = (e * NCH + c) * 4 + i4
                        cs = slice(i4 * 128, i4 * 128 + 128)
                        pe.wait_ge(e_h, n - 1) if not isinstance(n, int) or n >= 2 else None
                        for k in range(2):
                            mm3(bank(2 * (i4 % 2), 128, CH), part(eg[f], A, k, cs), part(ZT, A, k, tok), k == 0, k == 1)
                        for k in range(2):
                            i = mm3(bank(2 * (i4 % 2) + 1, 128, CH), part(eu[f], A, k, cs), part(ZT, A, k, tok), k == 0,
                                    k == 1)
                        i.then_inc(e_gu, 1)

                def down(c):
                    for s in range(CHB):
                        n = (e * NCH + c) * CHB + s
                        if s == 0:
                            pe.wait_ge(e_hl, ((e * NCH + c) + 1) * 4)
                        pe.wait_ge(e_oa, n - 3) if not isinstance(n, int) or n >= 4 else None
                        for m in range(4):
                            i = mm3(bank(4 + s, T, D), part(hT[c % 2], A, m, slice(s * T, s * T + T)),
                                    part(ed[f], A, m, A), m == 0, m == 3)
                        i.then_inc(e_o, 1)

                pe.wait_ge(e_wl, e * 3 + 3)
                gate_up(0)
                for c in range(1, NCH):
                    gate_up(c)
                    down(c - 1)
                down(NCH - 1)

            expert(0, 0)
            with pe.Fori(0, (NEXP - 1) // 2) as g:
                expert(g * 2 + 1, 1)
                expert(g * 2 + 2, 0)

        @block.scalar
        def _(act):
            def copy(o, i, scale=1.0):
                return nc.scalar.activation(o, i, ACT.Copy, scale=scale)

            def weight(k):
                _, parts, a, b, dst = weights[k]
                if isinstance(dst, tuple):
                    act.wait_ge(*s_staged(k))
                    copy(dst[0], staged(k, parts, a, b), WS).then_inc(s_hi, 1)

            weight(0)
            weight(1)
            act.wait_ge(s_const, 16 * NCONST)
            nc.scalar.activation(dtc, ldt, ACT.Exp).then_inc(s_s4a, 1)
            act.wait_ge(s_s4v, S4_RE)
            nc.scalar.activation(s4["th"], s4["re"], ACT.Tanh, scale=0.5).then_inc(s_s4a, 1)
            act.wait_ge(s_s4v, S4_ANG)
            nc.scalar.activation(s4["s"], s4["k"], ACT.Sin).then_inc(s_s4a, 1)
            nc.scalar.activation(s4["sh"], s4["k"], ACT.Sin, scale=0.5).then_inc(s_s4a, 1)
            weight(2)
            weight(3)
            copy(identb, identf).then_inc(s_misc, 1)
            copy(wr_hi, wr_f, WS).then_inc(s_misc, 1)
            copy(tmask, tmask8).then_inc(s_misc, 1)

            def keep(ring, i, name, dst, src, scale=1.0):
                ring.wait_full(act, i, name)
                copy(dst, src, scale).then_inc(ring.act, 1)

            def halves(x, m=2):
                return x.rearrange("p (k t) -> p k t", k=m)

            def body(i, f, has_p, has_a, has_b, has_c, has_e):
                a, b, d, c, e = i, i - 1, i - 1, i - 2, i - 3

                def a_keep_k(m):
                    keep(ra, a, f"k{m}", kT[:, m % KR, :], bank(ra.bank[f"k{m}"], 128, G), IWS)

                def a_keep_v(m):
                    half, j = m // 3, m % 3
                    keep(ra, a, f"v{m}", V[:, j, half * 512:half * 512 + 512], bank(ra.bank[f"v{m}"], GC, 512), IWS)

                def a_exp(h):
                    act.wait_ge(a_mx, a * H0 + h + 1)
                    if h >= 2:
                        act.wait_ge(a_pt, a * H0 + h - 1)
                    nc.scalar.activation(Pr[:, h % 2, :], bank(4 + h % 2, T, G), ACT.Exp, bias=nmx[:, h:h + 1],
                                         accum_out=rsum[:, h:h + 1]).then_inc(a_E, 1)

                def c_exp(h):
                    act.wait_ge(c_nm, c * H1 + h + 1)
                    act.wait_ge(c_took, (c * H1 + h) * 4 + 1)
                    nc.scalar.activation(P1[:, h, :], bank(3, T, G), ACT.Exp, bias=nmx1[:, h:h + 1],
                                         scale=DH1 ** -0.5).then_inc(c_E, 1)

                def a_keep_q(q):
                    ra.wait_full(act, a, f"q{q}")
                    for r in range(2):
                        rows_ = slice(64 * r, 64 * r + 64)
                        n = copy(qT[rows_, q * 8 + r:q * 8 + 8:2, :],
                                 psum[rows_, ra.bank[f"q{q}"], 0:4 * T].rearrange("p (k t) -> p k t", k=4),
                                 IWS * DH0 ** -0.5)
                    n.then_inc(ra.act, 1)

                def e_hidden(q):
                    rc.wait_full(act, e, f"m{q}")
                    for m in range(4):
                        n = nc.scalar.activation(hid[:, q * 4 + m, :], bank(2, 128, T, m * T), ACT.Gelu,
                                                 bias=b1col[:, q * 4 + m:q * 4 + m + 1], scale=IWS)
                    n.then_inc(rc.act, 1)

                if has_a:
                    a_keep_q(0)
                if has_b:
                    keep(ro, b, "o1", aT[0][:, 4:8, :], halves(bank(ro.bank["o1"], 128, 4 * T), 4))
                if has_a:
                    a_keep_q(1)
                if has_e:
                    keep(rc, e, "h", h2T[0], halves(bank(2, 128, 2 * T)))
                if has_a:
                    a_keep_k(0)
                    a_keep_k(1)
                    a_exp(0)
                    a_exp(1)
                    a_keep_v(0)
                if has_e:
                    e_hidden(0)
                if has_a:
                    a_keep_v(1)
                if has_e:
                    e_hidden(1)
                    rc.wait_act(act, e, "m1")
                    copy(hidT[0], hid).then_inc(c_hh, 1)
                if has_c:
                    c_exp(0)
                if has_a:
                    a_keep_v(2)
                for h in range(H0):
                    if has_a:
                        act.wait_ge(a_pt, a * H0 + h + 1)
                        copy(PTs[:, h % 2, :], bank(6, GC, GJ * T)).then_inc(a_pk, 1)
                    if has_c and h == 11:
                        keep(rc, c, "at", atT, bank(2, GC, GJ * T))
                    if has_a:
                        if h + 2 < H0:
                            a_exp(h + 2)
                        if h in (0, 2, 4, 6, 8, 10):
                            a_keep_k(h // 2 + 2)
                        if h in (1, 3, 5):
                            a_keep_v(h // 2 + 3)
                        if h == 10:
                            keep(ra, a, "o0", aT[0][:, 0:4, :], halves(bank(ra.bank["o0"], 128, 4 * T), 4))
                    if isinstance(i, int) and i == 0 and 1 <= h < 1 + NW - NFIRST:
                        weight(NFIRST + h - 1)
                    if has_c and h in (1, 4, 7):
                        c_exp((h + 2) // 3)
                    if has_b:
                        if h == 0:
                            keep(rb, b, "t1", hq1, halves(bank16(2, 128, 2 * T)))
                        if h == 4:
                            for m in range(2):
                                rb.wait_dve(act, b, f"m{m}")
                                u = ub[:, m * 512:(m + 1) * 512]
                                nc.scalar.activation(u, u, ACT.Gelu).then_inc(b_g, 1)
                        if h == 6:
                            keep(rd, d, "k", k1T, bank(2, 128, G), IWS)
                        if h == 8:
                            keep(rb, b, "t2", hq2, halves(bank16(2, 128, 8 * T), 8))
                    if has_c:
                        if h == 11:
                            keep(rc, c, "ct", ctT[0], halves(bank(2, 128, 2 * T)))
                        if h == 13 and isinstance(i, int) and i == 2:
                            act.wait_ge(s_kf, 1)
                            copy(kt, bank(2, T, D)).then_inc(s_kr, 1)
                            for q in range(2):
                                act.wait_ge(s_kf, 2 + q)
                                copy(coef[:, q * 2:q * 2 + 2, :], halves(bank(2, T, 2 * D))).then_inc(s_kr, 1)
                    if has_b:
                        if h == 11:
                            keep(rd, d, "z", zT[0], halves(bank(3, 128, 2 * T)))
                        if h == 12:
                            keep(rd, d, "v0", V1[:, 0:2, :], halves(bank(3, GC, 2 * D)), IWS)
                        if h == 13:
                            keep(rd, d, "v1", V1[:, 2, :], bank(3, GC, D), IWS)
                        if h == 14:
                            keep(rd, d, "q", q1T, bank(3, 128, T), IWS)
                    if has_p:
                        if h == 14:
                            p_context(i + 1, 1 - f, 0)
                        if h == 15:
                            p_tokens(i + 1)
                if has_p:
                    p_context(i + 1, 1 - f, 1)

            def p_context(j, f, k):
                keep(rp, j, f"c{k}", cT[f][0][:, k, :], bank(3, 128, G))

            def p_tokens(j):
                keep(rp, j, "xn", xT[0], halves(bank(3, 128, 2 * T)))

            p_context(0, 0, 0)
            p_tokens(0)
            p_context(0, 0, 1)
            iterations(act, body)

            def expert_weights(e, f):
                for k, dst in enumerate((eg[f][0], eu[f][0], ed[f][0])):
                    act.wait_ge(e_wd[k], (e + 1) * 16)
                    copy(dst, estage[:, k, :].rearrange("p (a b) -> p a b", a=(2, 2, 4)[k]), WS).then_inc(e_wh, 1)

            def expert(e, f, ahead):
                for c in range(NCH):
                    for i4 in range(4):
                        n = (e * NCH + c) * 4 + i4
                        act.wait_ge(e_gu, n + 1)
                        act.wait_ge(e_h, n - 1) if not isinstance(n, int) or n >= 2 else None
                        nc.scalar.activation(sg[:, i4 % 2, :], bank(2 * (i4 % 2), 128, CH), ACT.Silu,
                                             scale=IWS).then_inc(e_si, 1)
                        act.wait_ge(e_h, n + 1)
                        if i4 == 0:
                            k = (e * NCH + c) * CHB
                            act.wait_ge(e_o, k - CHB) if not isinstance(k, int) or k >= 2 * CHB else None
                        copy(hT[c % 2][0][:, i4, :], hf[:, i4 % 2, :]).then_inc(e_hh, 1)
                    if c == 1 and ahead:
                        act.wait_ge(e_o, e * NB)
                        expert_weights(e + 1, 1 - f)

            act.wait_ge(c_xo, NB)
            expert_weights(0, 0)
            with act.Fori(0, NCH) as g:
                act.wait_ge(e_tr, g + 1)
                for k in range(2):
                    copy(zt_t[0][:, k, :], bank(k, 128, CH)).then_inc(e_zh, 1)
                act.wait_ge(e_lb, g + 1)
                nc.scalar.activation(pr[:, :, 0:8], lg, ACT.Sigmoid).then_inc(e_sg, 1)
                act.wait_ge(e_zc, g * 2 + 2)

            expert(0, 0, True)
            with act.Fori(0, (NEXP - 1) // 2 - 1) as g:
                expert(g * 2 + 1, 1, True)
                expert(g * 2 + 2, 0, True)
            expert(NEXP - 2, 1, True)
            expert(NEXP - 1, 0, False)

        @block.gpsimd
        def _(pool):
            def tt(o, a, b, op):
                return nc.gpsimd.tensor_tensor(o, a, b, op)

            nc.gpsimd.memset(ones_f, 1.0).then_inc(s_pmisc, 1)
            nc.gpsimd.memset(ones_b, 1.0).then_inc(s_pmisc, 1)
            nc.gpsimd.memset(neghalf, -0.5).then_inc(s_pmisc, 1)
            nc.gpsimd.memset(qT, 0.0).then_inc(s_pmisc, 1)
            pool.wait_ge(s_pmisc, 4)
            pool.wait_ge(s_x, 16)
            pool.wait_ge(s_const, 16 * NCONST)

            def rsqrt(var_sem, rstd_sem, n):
                pool.wait_ge(var_sem, n + 1)
                tt(rstd, ve, neghalf, ALU.pow).then_inc(rstd_sem, 1)

            def s4d_powers(h):
                n = [h * S4P_HALF]

                def link(ins):
                    n[0] += 1
                    ins.then_inc(s_s4p, 1)
                    pool.wait_ge(s_s4p, n[0])

                def cmul(o, a, c, m):
                    cr_, ci_ = (x.to_broadcast([128, m, NST]) for x in c)
                    f1, f2 = p1[:, 0:m, :], p2[:, 0:m, :]
                    link(tt(f1, a[0], cr_, ALU.mult))
                    link(tt(f2, a[1], ci_, ALU.mult))
                    link(tt(o[0], f1, f2, ALU.subtract))
                    link(tt(f1, a[0], ci_, ALU.mult))
                    link(tt(f2, a[1], cr_, ALU.mult))
                    link(tt(o[1], f1, f2, ALU.add))

                def at(p, lo, hi):
                    return p[0][:, lo:hi, :], p[1][:, lo:hi, :]

                v, u = (vr, vi), (ur, ui)
                pool.wait_ge(s_s4v, S4V_ALL)
                pool.wait_ge(s_lo, NFIRST)
                if h:
                    pool.wait_ge(s_s4c, PA)
                link(nc.gpsimd.memset(vr[:, 0, :], 1.0))
                link(nc.gpsimd.memset(vi[:, 0, :], 0.0))
                link(nc.gpsimd.tensor_copy(vr[:, 1, :], s4["zr"][:, h, :]))
                link(nc.gpsimd.tensor_copy(vi[:, 1, :], s4["zi"][:, h, :]))
                link(nc.gpsimd.tensor_copy(ur[:, 0, :], s4["dr"][:, h, :]))
                link(nc.gpsimd.tensor_copy(ui[:, 0, :], s4["di"][:, h, :]))
                for m in (1, 2, 4, 8):
                    cmul(at(v, m + 1, 2 * m + 1), at(v, 1, m + 1), at(v, m, m + 1), m)
                for m in range(PA - 1):
                    cmul(at(u, m + 1, m + 2), at(u, m, m + 1), at(v, PBS, PBS + 1), 1)
                assert n[0] == (h + 1) * S4P_HALF, n[0]

            rsqrt(a_var, a_rstd, 0)
            pool.wait_ge(a_xn, 1)
            tt(X[:, 0, :], X[:, 0, :], bo_r, ALU.add).then_inc(a_xb, 1)

            def body(i, f, has_p, has_a, has_b, has_c, has_e):
                b, d, c, e = i - 1, i - 1, i - 2, i - 3

                def diagonal(h):
                    wait_apart(pool, c_r, c * H1 + h + 1)
                    nc.gpsimd.tensor_scalar(dg[:, h, :], identf[0:T, 0:T], r2[:, h:h + 1], 1.0, ALU.mult,
                                            ALU.mult).then_inc(c_dg, 1)

                def cstep(n, ins):
                    ins.then_inc(c_pool, 1)
                    pool.wait_ge(c_pool, c * 3 + n)

                def row(x):
                    return x.rearrange("p o d -> p (o d)")

                if has_e:
                    pool.wait_ge(c_h2, e + 1)
                    tt(z, z, c2_r, ALU.add).then_inc(c_zb, 1)
                if has_b:
                    rsqrt(b_var, b_rstd, b * 3)
                    pool.wait_ge(b_z, b + 1)
                    x = row(X[:, bass.ds(b, 1), :])
                    tt(x, x, b2_r, ALU.add).then_inc(b_xb, 1)
                    rsqrt(b_var, b_rstd, b * 3 + 1)
                if isinstance(i, int) and i < 2:
                    s4d_powers(i)
                if has_c:
                    diagonal(0)
                    diagonal(1)
                if has_e:
                    rsqrt(c_var, c_rstd, e * 3 + 2)
                    pool.wait_ge(c_y, e + 1)
                    x = row(X[:, bass.ds(e, 1), :])
                    tt(x, x, y, ALU.add).then_inc(c_xo, 1)
                if has_c:
                    if not isinstance(c, int) or c > 0:
                        wait_apart(pool, c_xo, c)
                    wait_apart(pool, d_zn, c + 1)
                    nc.gpsimd.tensor_copy(z, zn).then_inc(c_z, 1)
                if has_b:
                    rsqrt(b_var, b_rstd, b * 3 + 2)
                if has_c:
                    diagonal(2)
                    rsqrt(c_var, c_rstd, c * 3)
                    diagonal(3)
                if has_b:
                    rsqrt(d_var, d_rstd, d)
                    if not isinstance(d, int) or d > 0:
                        pool.wait_ge(c_S, d * H1)
                    wait_apart(pool, d_vm8, d * 16 + 16)
                    nc.gpsimd.tensor_scalar(vmb, vm8, MASKED, -MASKED, ALU.mult, ALU.add).then_inc(d_vm, 1)
                if has_p:
                    rsqrt(a_var, a_rstd, i + 1)
                    pool.wait_ge(a_xn, i + 2)
                    x = X[:, i + 1, :]
                    tt(x, x, bo_r, ALU.add).then_inc(a_xb, 1)
                if has_c:
                    pool.wait_ge(c_xn, c + 1)
                    rc.wait_dve(pool, c, "fi")
                    cstep(1, tt(x1, x1, mi[:, 0:D], ALU.mult))
                    tt(x1, x1, mi[:, D:2 * D], ALU.add).then_inc(c_x1, 1)
                    pool.wait_ge(c_x1, c + 1)
                    tt(xd, x1, dsk_r, ALU.mult).then_inc(c_xd, 1)
                    rc.wait_dve(pool, c, "y")
                    cstep(2, tt(y, y, mo[:, 0:D], ALU.mult))
                    cstep(3, tt(y, y, mo[:, D:2 * D], ALU.add))
                    tt(z, z, y, ALU.add).then_inc(c_zy, 1)
                    rsqrt(c_var, c_rstd, c * 3 + 1)

            iterations(pool, body)

            def e_rsqrt(g):
                pool.wait_ge(e_var, g + 1)
                tt(rstde, vee, neghalf.to_broadcast([T, CHB]), ALU.pow).then_inc(e_rstd, 1)

            def e_copy(g):
                pool.wait_ge(e_zl, g * 2 + 2)
                for k in range(2):
                    nc.gpsimd.tensor_copy(ZT[k][:, :, bass.ds(g * CH, CH)], zt_t[k]).then_inc(e_zc, 1)

            e_rsqrt(0)
            with pool.Fori(0, NCH - 1) as g:
                e_rsqrt(g + 1)
                e_copy(g)
            e_copy(NCH - 1)

        @block.vector
        def _(dve):
            V_ = nc.vector

            def ts(o, i, a, b, op0, op1=None):
                return V_.tensor_scalar(o, i, a, b, op0, op1) if op1 is not None else V_.tensor_scalar(o, i, a, None, op0)

            def tt(o, a, b, op):
                return V_.tensor_tensor(o, a, b, op)

            def stt(o, a, s, b, op0, op1, **kw):
                return V_.scalar_tensor_tensor(o, a, s, b, op0, op1, **kw)

            def halves(x, m=2):
                return x.rearrange("p (k t) -> p k t", k=m)

            n_set = [0]

            def linkset(ins):
                n_set[0] += 1
                ins.then_inc(s_dset, 1)
                dve.wait_ge(s_dset, n_set[0])

            def weight(k):
                _, parts, a, b, dst = weights[k]
                src = staged(k, parts, a, b)
                if isinstance(dst, tuple):
                    dve.wait_ge(s_hi, sum(isinstance(w_[4], tuple) for w_ in weights[:k + 1]))
                    stt(dst[1], src, WS, dst[0], ALU.mult, ALU.subtract).then_inc(s_lo, 1)
                    return
                q = k - NFIRST
                dve.wait_ge(*s_staged(k))
                flat = stage[0]
                V_.tensor_reduce(wab[:, q:q + 1], flat, AX_X, ALU.add, apply_absolute_value=True).then_inc(s_wab, 1)
                dve.wait_ge(s_wsum, q + 1)
                linkset(ts(wmean[:, q:q + 1], bank(3 - q, 128, 1), 1.0 / (a * b * 128), EPS, ALU.mult, ALU.max))
                linkset(V_.reciprocal(wsc[:, q:q + 1], wmean[:, q:q + 1]))
                linkset(ts(flat, flat, wsc[:, q:q + 1], 1.0, ALU.mult, ALU.min))
                linkset(ts(flat, flat, -1.0, MAGIC, ALU.max, ALU.add))
                ts(dst, src, -MAGIC, None, ALU.add).then_inc(s_lo, 1)

            def bn_part(link, k, src, width=D):
                link.then(V_.bn_stats(st[:, k, :], src[:, k * 512:min(width, k * 512 + 512)]))

            def bn_sum(link, k):
                link.ready(hold=True)
                link.then(V_.bn_aggr(mv, st[:, 0:k, :]))

            def variance(link, var_sem):
                link.ready()
                ts(ve, mv[:, 1:2], EPS, None, ALU.add).then_inc(var_sem, 1)

            def norm_stats(link, var_sem, src, width=D):
                for c in range(0, width, 512):
                    e = min(width, c + 512)
                    link(V_.bn_stats(st[:, c // 512, :], src[:, c:e]), hold=(e == width))
                k = (width + 511) // 512
                link(V_.bn_aggr(mv, st[:, 0:k, :]))
                ts(ve, mv[:, 1:2], EPS, None, ALU.add).then_inc(var_sem, 1)

            def layer_norm(link, var_sem, rstd_sem, n, dst, src, width=D):
                norm_stats(link, var_sem, src, width)
                dve.wait_ge(rstd_sem, n + 1)
                return ts(dst, src, mv[:, 0:1], rstd, ALU.subtract, ALU.mult)

            def layer_norm_affine(link, var_sem, rstd_sem, n, dst, src, g, h, width=D):
                norm_stats(link, var_sem, src, width)
                dve.wait_ge(rstd_sem, n + 1)
                link(stt(dst, src, mv[:, 0:1], g, ALU.subtract, ALU.mult))
                return stt(dst, dst, rstd, h, ALU.mult, ALU.add)

            class Link:
                def __init__(self, s, per):
                    self.s, self.per, self.n = s, per, 0

                def at(self, i):
                    self.i, self.n = i, 0
                    return self

                def __call__(self, ins, hold=False):
                    self.n += 1
                    ins.then_inc(self.s, 1)
                    (wait_apart if hold else type(dve).wait_ge)(dve, self.s, self.i * self.per + self.n)

                def then(self, ins):
                    self.n += 1
                    ins.then_inc(self.s, 1)

                def ready(self, hold=False):
                    (wait_apart if hold else type(dve).wait_ge)(dve, self.s, self.i * self.per + self.n)

                def done(self):
                    assert self.n == self.per, self.n

            def split_low(ring, i, name, lo, hi, src):
                ring.wait_act(dve, i, name)
                tt(lo, src, hi, ALU.subtract).then_inc(ring.dve, 1)

            linka, linkb, linkc, linkd = Link(a_step, 2), Link(b_step, B_LINKS), Link(c_step, C_LINKS), Link(d_step, 2)
            linke = Link(c_step2, E_END_LINKS)

            def a_norm(j):
                layer_norm(linka.at(j), a_var, a_rstd, j, xn, X[:, j, :]).then_inc(a_xn, 1)

            dve.wait_ge(s_x, 16)
            a_norm(0)
            weight(0)
            weight(1)
            dve.wait_ge(s_const, 16 * NCONST)
            n4 = [0]

            def link4(ins):
                n4[0] += 1
                ins.then_inc(s_s4v, 1)
                dve.wait_ge(s_s4v, n4[0])

            f = s4
            dve.wait_ge(s_s4a, 1)
            dtb = dtc.rearrange("p (h o) -> p h o", o=1).to_broadcast([128, 2, NST])
            link4(tt(f["re"], f["ar"], dtb, ALU.mult))
            link4(tt(f["im"], f["ai"], dtb, ALU.mult))
            assert S4_RE == 1
            link4(ts(f["t1"], f["im"], 1.0 / TWO_PI, MAGIC, ALU.mult, ALU.add))
            link4(ts(f["t1"], f["t1"], -MAGIC, None, ALU.add))
            link4(stt(f["k"], f["t1"], -TP1, f["im"], ALU.mult, ALU.add))
            link4(stt(f["k"], f["t1"], -TP2, f["k"], ALU.mult, ALU.add))
            link4(stt(f["k"], f["t1"], -TP3, f["k"], ALU.mult, ALU.add))
            link4(ts(f["k"], f["k"], 3.1415925, -3.1415925, ALU.min, ALU.max))
            assert n4[0] == S4_ANG
            dve.wait_ge(s_s4a, 4)
            link4(ts(f["t1"], f["th"], -1.0, 1.0, ALU.mult, ALU.add))
            link4(V_.reciprocal(f["t2"], f["t1"]))
            link4(stt(f["e1"], f["th"], 2.0, f["t2"], ALU.mult, ALU.mult))
            link4(stt(f["t2"], f["sh"], -2.0, f["sh"], ALU.mult, ALU.mult))
            link4(ts(f["re"], f["e1"], 1.0, None, ALU.add))
            link4(ts(f["im"], f["t2"], 1.0, None, ALU.add))
            link4(tt(f["zr"], f["re"], f["im"], ALU.mult))
            link4(tt(f["zi"], f["re"], f["s"], ALU.mult))
            link4(tt(f["t1"], f["e1"], f["im"], ALU.mult))
            link4(tt(f["mr"], f["t1"], f["t2"], ALU.add))
            link4(tt(f["t1"], f["ar"], f["ar"], ALU.mult))
            link4(tt(f["t2"], f["ai"], f["ai"], ALU.mult))
            link4(tt(f["t1"], f["t1"], f["t2"], ALU.add))
            link4(V_.reciprocal(f["e1"], f["t1"]))
            link4(tt(f["t1"], f["mr"], f["ar"], ALU.mult))
            link4(tt(f["t2"], f["zi"], f["ai"], ALU.mult))
            link4(tt(f["re"], f["t1"], f["t2"], ALU.add))
            link4(tt(f["t1"], f["zi"], f["ar"], ALU.mult))
            link4(tt(f["t2"], f["mr"], f["ai"], ALU.mult))
            link4(tt(f["im"], f["t1"], f["t2"], ALU.subtract))
            link4(stt(f["re"], f["re"], 2.0, f["e1"], ALU.mult, ALU.mult))
            link4(stt(f["im"], f["im"], 2.0, f["e1"], ALU.mult, ALU.mult))
            link4(tt(f["t1"], f["cr"], f["re"], ALU.mult))
            link4(tt(f["t2"], f["ci"], f["im"], ALU.mult))
            link4(tt(f["dr"], f["t1"], f["t2"], ALU.subtract))
            link4(tt(f["t1"], f["cr"], f["im"], ALU.mult))
            link4(tt(f["t2"], f["ci"], f["re"], ALU.mult))
            link4(tt(f["di"], f["t1"], f["t2"], ALU.add))
            assert n4[0] == S4V_ALL, n4[0]

            weight(2)
            weight(3)

            def s4d_contract(h, a):
                n0 = (h * PA + a) * 3
                dve.wait_ge(s_s4p, (h + 1) * S4P_HALF)
                if n0:
                    dve.wait_ge(s_s4c, h * PA + a)
                tt(p1, vr[:, 0:PBS, :], ur[:, a:a + 1, :].to_broadcast([128, PBS, NST]), ALU.mult).then_inc(s_s4d, 1)
                tt(p2, vi[:, 0:PBS, :], ui[:, a:a + 1, :].to_broadcast([128, PBS, NST]), ALU.mult).then_inc(s_s4d, 1)
                dve.wait_ge(s_s4d, n0 + 2)
                tt(p1, p1, p2, ALU.subtract).then_inc(s_s4d, 1)
                dve.wait_ge(s_s4d, n0 + 3)
                V_.tensor_reduce(kpow[:, h, a * PBS:(a + 1) * PBS], p1, AX_X, ALU.add).then_inc(s_s4c, 1)

            def small_constants():
                dve.wait_ge(s_misc, 3)
                linkset(ts(mbi, mbi, mg, None, ALU.mult))
                linkset(ts(mbo, mbo, mg, None, ALU.mult))
                linkset(ts(mbi[:, 0:D], mbi[:, 0:D], 1.0, None, ALU.add))
                linkset(ts(mbo[:, 0:D], mbo[:, 0:D], 1.0, None, ALU.add))
                linkset(ts(mgs, mg, IWS, None, ALU.mult))
                linkset(stt(wr_lo, wr_f, WS, wr_hi, ALU.mult, ALU.subtract))

            def q_max(link, src):
                link.ready()
                link.then(V_.tensor_reduce(amax, src, AX_X, ALU.max, apply_absolute_value=True))

            def q_step(link):
                link.ready()
                link.then(ts(amc, amax, EPS, 1.0 / 127.0, ALU.max, ALU.mult))

            def q_scales(link, dq, wm):
                link.ready()
                V_.reciprocal(qsc, amc).then_inc(b_rcp, 1)
                ts(dq, amc, wm, None, ALU.mult).then_inc(b_rcp, 1)

            def q_round(link, n, src):
                dve.wait_ge(b_rcp, n)
                link.then(ts(src, src, qsc, MAGIC, ALU.mult, ALU.add))

            def q_clip(link, dst, src):
                link.ready()
                ts(dst, src, -MAGIC, 127.0, ALU.add, ALU.min).then_inc(b_q, 1)

            def body(i, f, has_p, has_a, has_b, has_c, has_e):
                a, b, d, c, e = i, i - 1, i - 1, i - 2, i - 3
                if has_b:
                    linkb.at(b)
                if has_c:
                    linkc.at(c)
                if has_e:
                    linke.at(e)

                def row_max(h):
                    dve.wait_ge(a_S, a * H0 + h + 1)
                    V_.tensor_reduce(nmx[:, h:h + 1], bank(4 + h % 2, T, G), AX_X, ALU.max, negate=True).then_inc(a_mx, 1)

                def a_norm_heads(j, q):
                    dve.wait_ge(a_E, j * H0 + q * 8 + 8)
                    V_.reciprocal(rinv[:, q * 8:q * 8 + 8], rsum[:, q * 8:q * 8 + 8]).then_inc(a_ri, 1)
                    dve.wait_ge(a_O, j * 2 + q + 1)
                    if q:
                        ra.wait_full(dve, j, "o0")
                    dve.wait_ge(a_ri, j * 2 + q + 1)
                    tt(halves(On, 8), halves(bank(7, T, 512), 8),
                       rinv[:, q * 8:q * 8 + 8].rearrange("p (h o) -> p h o", o=1).to_broadcast([T, 8, DH0]),
                       ALU.mult).then_inc(a_On, 1)

                def a_low_o(ring, j, q):
                    split_low(ring, j, f"o{q}", aT[1][:, q * 4:q * 4 + 4, :], aT[0][:, q * 4:q * 4 + 4, :],
                              halves(bank(ring.bank[f"o{q}"], 128, 4 * T), 4))

                def b_hidden(m):
                    rb.wait_full(dve, b, f"m{m}")
                    cs = slice(m * 512, (m + 1) * 512)
                    stt(ub[:, cs], bank(2, T, 512), dq1, b1row[:, cs], ALU.mult, ALU.add).then_inc(rb.dve, 1)

                def top_max(h, r):
                    n = (c * H1 + h) * 4 + r
                    if r == 0:
                        wait_apart(dve, c_S, c * H1 + h + 1)
                    else:
                        wait_apart(dve, c_took, n)
                    V_.max(top8[:, h % 2, r, :], bank(3, T, G) if r == 0 else R1).then_inc(c_top, 1)

                def top_take(h, r):
                    n = (c * H1 + h) * 4 + r
                    m8 = top8[:, h % 2, r, :]
                    if r == 0:
                        dve.wait_ge(c_top, n + 1)
                        ts(nmx1[:, h:h + 1], m8[:, 0:1], -(DH1 ** -0.5), None, ALU.mult).then_inc(c_nm, 1)
                    wait_apart(dve, c_top, n + 1)
                    V_.match_replace(R1, m8, bank(3, T, G) if r == 0 else R1, NEG).then_inc(c_took, 1)

                def top_probs(h):
                    dve.wait_ge(c_E, c * H1 + h + 1)
                    dve.wait_ge(c_took, (c * H1 + h) * 4 + 4)
                    linkc.then(stt(P1[:, h, :], R1, 0.9 * NEG, P1[:, h, :], ALU.is_lt, ALU.mult,
                                   accum_out=sum1[:, h:h + 1]))

                def top_recip(h):
                    linkc.ready()
                    linkc.then(V_.reciprocal(r1[:, h:h + 1], sum1[:, h:h + 1]))

                def top_factor(h):
                    linkc.ready()
                    ts(r2[:, h:h + 1], r1[:, h:h + 1], tmask[:, bass.ds(c, 1)], 1.0 / H1, ALU.mult,
                       ALU.mult).then_inc(c_r, 1)

                if has_e:
                    split_low(rc, e, "h", h2T[1], h2T[0], halves(bank(2, 128, 2 * T)))
                if has_b:
                    a_low_o(ro, b, 1)
                if has_a:
                    row_max(0)
                    row_max(1)
                if has_b:
                    ro.wait_full(dve, b, "wo")
                    dve.wait_ge(a_xb, b + 1)
                    stt(X[:, b, :], bank(ro.bank["wo"], T, D), IWS, X[:, b, :], ALU.mult, ALU.add).then_inc(ro.dve, 1)
                if has_c:
                    top_max(0, 0)
                if has_b:
                    wait_apart(dve, ro.dve, b * ro.nd + ro.nd)
                    bn_part(linkb, 0, X[:, b, :])
                if has_c:
                    top_take(0, 0)
                if has_b:
                    bn_sum(linkb, 1)
                if has_c:
                    top_max(0, 1)
                if has_b:
                    variance(linkb, b_var)
                if has_c:
                    top_take(0, 1)
                if has_b:
                    dve.wait_ge(b_rstd, b * 3 + 1)
                    ts(zb, X[:, b, :], mv[:, 0:1], rstd, ALU.subtract, ALU.mult).then_inc(b_z, 1)
                if has_c:
                    top_max(0, 2)
                if has_b:
                    wait_apart(dve, b_z, b + 1)
                    bn_part(linkb, 0, zb)
                if has_c:
                    top_take(0, 2)
                if has_b:
                    bn_sum(linkb, 1)
                if has_c:
                    top_max(0, 3)
                if has_b:
                    variance(linkb, b_var)
                if has_c:
                    top_take(0, 3)
                if has_b:
                    dve.wait_ge(b_rstd, b * 3 + 2)
                    linkb(stt(zb, zb, mv[:, 0:1], g1_r, ALU.subtract, ALU.mult))
                    linkb.then(stt(zb, zb, rstd, h1_r, ALU.mult, ALU.add))
                if has_a:
                    row_max(2)
                if has_b:
                    q_max(linkb, zb)
                    q_step(linkb)
                    q_scales(linkb, dq1, wmean[0:T, 0:1])
                    q_round(linkb, b * 4 + 2, zb)
                    q_clip(linkb, q1, zb)
                for h in range(H0):
                    if has_a and 0 < h < H0 - 2:
                        row_max(h + 2)
                    if has_a and h == 8:
                        a_norm_heads(a, 0)
                    if isinstance(i, int) and i == 0:
                        if 1 <= h < 1 + NW - NFIRST:
                            weight(NFIRST + h - 1)
                        if h == 10:
                            small_constants()
                    if isinstance(i, int) and i < 2 and 6 <= h < 6 + PA:
                        s4d_contract(i, h - 6)
                    if h == 0:
                        if has_c:
                            top_probs(0)
                        if has_e:
                            dve.wait_ge(c_hh, e + 1)
                            tt(hidT[1], hid, hidT[0], ALU.subtract).then_inc(c_hl, 1)
                        if has_c:
                            top_recip(0)
                            top_factor(0)
                    if h == 1 and has_c:
                        top_max(1, 0)
                        top_take(1, 0)
                        top_max(1, 1)
                        top_take(1, 1)
                    if has_b and h in (2, 3):
                        b_hidden(h - 2)
                    if h == 2 and has_c:
                        top_max(1, 2)
                        top_take(1, 2)
                        top_max(1, 3)
                        top_take(1, 3)
                    if h == 3 and has_c:
                        top_probs(1)
                        top_recip(1)
                        top_factor(1)
                    if h == 4:
                        if has_e:
                            rc.wait_full(dve, e, "m2")
                            dve.wait_ge(c_zb, e + 1)
                            stt(z, bank(2, T, D), IWS, z, ALU.mult, ALU.add).then_inc(rc.dve, 1)
                        if has_c:
                            top_max(2, 0)
                        if has_e:
                            wait_apart(dve, rc.dve, e * rc.nd + rc.nd)
                            bn_part(linke, 0, z)
                        if has_c:
                            top_take(2, 0)
                        if has_e:
                            bn_sum(linke, 1)
                        if has_c:
                            top_max(2, 1)
                        if has_e:
                            variance(linke, c_var)
                        if has_c:
                            top_take(2, 1)
                        if has_e:
                            dve.wait_ge(c_rstd, e * 3 + 3)
                            linke.then(stt(y, z, mv[:, 0:1], go_r, ALU.subtract, ALU.mult))
                        if has_c:
                            top_max(2, 2)
                        if has_e:
                            linke.ready()
                            stt(y, y, rstd, ho_r, ALU.mult, ALU.add).then_inc(c_y, 1)
                    if h == 5:
                        if has_b:
                            wait_apart(dve, b_g, b * 2 + 2)
                            bn_part(linkb, 0, ub, HID)
                        if has_c:
                            top_take(2, 2)
                        if has_b:
                            bn_part(linkb, 1, ub, HID)
                        if has_c:
                            top_max(2, 3)
                        if has_b:
                            bn_sum(linkb, 2)
                        if has_c:
                            top_take(2, 3)
                        if has_b:
                            variance(linkb, b_var)
                    if h == 6:
                        if has_c:
                            top_probs(2)
                        if has_b:
                            dve.wait_ge(b_rstd, b * 3 + 3)
                            linkb.then(stt(ub, ub, mv[:, 0:1], g2row, ALU.subtract, ALU.mult))
                        if has_c:
                            top_recip(2)
                            top_factor(2)
                        if has_b:
                            linkb.ready()
                            linkb.then(stt(ub, ub, rstd, h2row, ALU.mult, ALU.add))
                    if h == 7:
                        if has_b:
                            q_max(linkb, ub)
                        if has_c:
                            top_max(3, 0)
                        if has_b:
                            q_step(linkb)
                        if has_c:
                            top_take(3, 0)
                        if has_b:
                            q_scales(linkb, dq2, wmean[0:T, 1:2])
                            q_round(linkb, b * 4 + 4, ub)
                            q_clip(linkb, q2, ub)
                    if h == 8 and has_c:
                        top_max(3, 1)
                        top_take(3, 1)
                        top_max(3, 2)
                        top_take(3, 2)
                    if h == 9:
                        if has_c:
                            wait_apart(dve, c_z, c + 1)
                            bn_part(linkc, 0, z)
                            top_max(3, 3)
                            bn_sum(linkc, 1)
                            top_take(3, 3)
                            variance(linkc, c_var)
                            top_probs(3)
                            dve.wait_ge(c_rstd, c * 3 + 1)
                            linkc.then(stt(x1, z, mv[:, 0:1], gi_r, ALU.subtract, ALU.mult))
                            top_recip(3)
                            top_factor(3)
                            linkc.ready()
                            stt(x1, x1, rstd, hi_r, ALU.mult, ALU.add).then_inc(c_xn, 1)
                    if has_b and h == 10:
                        rb.wait_full(dve, b, "m2")
                        dve.wait_ge(b_xb, b + 1)
                        stt(X[:, b, :], bank(2, T, D), dq2, X[:, b, :], ALU.mult, ALU.add).then_inc(rb.dve, 1)
                        wait_apart(dve, rb.dve, b * rb.nd + rb.nd)
                        if has_c:
                            wait_apart(dve, c_z, c + 1)
                        layer_norm(linkd.at(d), d_var, d_rstd, d, zn, X[:, d, :]).then_inc(d_zn, 1)
                    if has_c and h == 11:
                        split_low(rc, c, "ct", ctT[1], ctT[0], halves(bank(2, 128, 2 * T)))
                    if has_b and h == 11:
                        split_low(rd, d, "z", zT[1], zT[0], halves(bank(3, 128, 2 * T)))
                    if has_a and h == 10:
                        a_low_o(ra, a, 0)
                    if has_c and h == 12:
                        rc.wait_full(dve, c, "fi")
                        stt(mi, bank(2, T, 2 * D), mgs, mbi, ALU.mult, ALU.add).then_inc(rc.dve, 1)
                    if has_p and h == 12:
                        a_norm(i + 1)
                    if has_c and h == 13:
                        rc.wait_full(dve, c, "fo")
                        stt(mo, bank(2, T, 2 * D), mgs, mbo, ALU.mult, ALU.add).then_inc(rc.dve, 1)
                    if has_c and h == 14:
                        if isinstance(i, int) and i == 2:
                            dve.wait_ge(s_kr, 3)
                        rc.wait_full(dve, c, "ab")
                        ab = bank(2, T, 2 * D)
                        linkc(tt(t1, ab, coef[:, 0:2, :].rearrange("p m d -> p (m d)"), ALU.mult))
                        tt(t2, ab, coef[:, 2:4, :].rearrange("p m d -> p (m d)"), ALU.mult).then_inc(rc.dve, 1)
                        rc.wait_dve(dve, c, "ab")
                        tt(Y[:, 0:D], t1[:, 0:D], t2[:, D:2 * D], ALU.add).then_inc(c_Y, 1)
                        tt(Y[:, D:2 * D], t1[:, D:2 * D], t2[:, 0:D], ALU.add).then_inc(c_Y, 1)
                    if has_c and h == 15:
                        rc.wait_full(dve, c, "y")
                        dve.wait_ge(c_xd, c + 1)
                        tt(y, bank(2, T, D), xd, ALU.add).then_inc(rc.dve, 1)
                    if has_p and h == 14:
                        p_context(i + 1, 1 - f, 0)
                    if has_p and h == 15:
                        p_tokens(i + 1)
                if has_p:
                    p_context(i + 1, 1 - f, 1)
                if has_a:
                    a_norm_heads(a, 1)
                if has_c:
                    wait_apart(dve, c_zy, c + 1)
                    layer_norm_affine(linkc, c_var, c_rstd, c * 3 + 1, h2, z, gf_r, hf_r).then_inc(c_h2, 1)
                    linkc.done()
                if has_e:
                    linke.done()
                if has_b:
                    linkb.done()

            def p_context(j, f, k):
                split_low(rp, j, f"c{k}", cT[f][1][:, k, :], cT[f][0][:, k, :], bank(3, 128, G))

            def p_tokens(j):
                split_low(rp, j, "xn", xT[1], xT[0], halves(bank(3, 128, 2 * T)))

            p_context(0, 0, 0)
            p_tokens(0)
            p_context(0, 0, 1)
            iterations(dve, body)

            lnorm, ltop = Link(e_step, E_NORM_LINKS), Link(e_top, E_TOP_LINKS)
            dve.wait_ge(c_xo, NB)
            V_.memset(pr[:, :, 8:16], -1.0)
            V_.memset(pin[:, :, 2:8], -1.0)
            V_.memset(cw[:, :, 0:1], IWS)

            def e_norm(g):
                lnorm.at(g)
                for q in range(CHB):
                    lnorm.then(V_.bn_stats(ste[:, q, :], X[:, g * CHB + q, :]))
                lnorm.ready(hold=True)
                for q in range(CHB):
                    lnorm.then(V_.bn_aggr(mve[:, q, :], ste[:, q:q + 1, :]))
                lnorm.ready()
                ts(vee, mve[:, :, 1:2].rearrange("p q o -> p (q o)"), EPS, None, ALU.add).then_inc(e_var, 1)
                dve.wait_ge(e_rstd, g + 1)
                for q in range(CHB):
                    ts(ze[:, q, :], X[:, g * CHB + q, :], mve[:, q, 0:1], rstde[:, q:q + 1], ALU.subtract,
                       ALU.mult).then_inc(e_z, 1)
                lnorm.done()

            def e_split(g):
                for k in range(2):
                    dve.wait_ge(e_zh, g * 2 + k + 1)
                    tt(zt_t[1][:, k, :], bank(k, 128, CH), zt_t[0][:, k, :], ALU.subtract).then_inc(e_zl, 1)

            def e_route(g):
                ltop.at(g)
                dve.wait_ge(e_lg, g + 1)
                stt(lg, bank(2, T, CHB * 8).rearrange("p (q e) -> p q e", q=CHB), IWS,
                    rbrow.rearrange("p (o e) -> p o e", o=1).to_broadcast([T, CHB, 8]), ALU.mult,
                    ALU.add).then_inc(e_lb, 1)
                wait_apart(dve, e_sg, g + 1)
                for q in range(CHB):
                    ltop.then(V_.max(pm8[:, q, :], pr[:, q, :]))
                ltop.ready()
                ltop.then(V_.tensor_copy(pin[:, :, 0:2], pm8[:, :, 0:2]))
                ltop.ready(hold=True)
                for q in range(CHB):
                    ltop.then(V_.match_replace(prr[:, q, :], pin[:, q, :], pr[:, q, :], -2.0))
                ltop.ready()
                ltop.then(tt(pne, pr[:, :, 0:8], prr[:, :, 0:8], ALU.not_equal))
                ltop.ready()
                stt(cw[:, bass.ds(g * CHB, CHB), 1:9], pne, IWS, pr[:, :, 0:8], ALU.mult, ALU.mult).then_inc(e_cw, 1)
                ltop.done()

            e_norm(0)
            with dve.Fori(0, NCH - 1) as g:
                e_split(g)
                e_norm(g + 1)
                e_route(g)
            e_split(NCH - 1)
            e_route(NCH - 1)

            def expert_weights(e, f):
                for k, (hi, lo) in enumerate((eg[f], eu[f], ed[f])):
                    dve.wait_ge(e_wh, e * 3 + k + 1)
                    stt(lo, estage[:, k, :].rearrange("p (a b) -> p a b", a=(2, 2, 4)[k]), WS, hi, ALU.mult,
                        ALU.subtract).then_inc(e_wl, 1)

            def expert(e, f, ahead):
                def combine(c):
                    for s in range(CHB):
                        bb = c * CHB + s
                        n = (e * NCH + c) * CHB + s
                        dve.wait_ge(e_o, n + 1)
                        dve.wait_ge(e_oa, n - NB + 1) if not isinstance(n, int) or n >= NB else None
                        stt(X[:, bb, :], bank(4 + s, T, D), cw[:, bb, bass.ds(e, 1)], X[:, bb, :], ALU.mult,
                            ALU.add).then_inc(e_oa, 1)

                for c in range(NCH):
                    for i4 in range(4):
                        n = (e * NCH + c) * 4 + i4
                        dve.wait_ge(e_si, n + 1)
                        dve.wait_ge(e_hl, n - 1) if not isinstance(n, int) or n >= 2 else None
                        stt(hf[:, i4 % 2, :], bank(2 * (i4 % 2) + 1, 128, CH), IWS, sg[:, i4 % 2, :], ALU.mult,
                            ALU.mult).then_inc(e_h, 1)
                        dve.wait_ge(e_hh, n + 1)
                        tt(hT[c % 2][1][:, i4, :], hf[:, i4 % 2, :], hT[c % 2][0][:, i4, :],
                           ALU.subtract).then_inc(e_hl, 1)
                    if c == 1 and ahead:
                        expert_weights(e + 1, 1 - f)
                    if c >= 1:
                        combine(c - 1)
                combine(NCH - 1)

            dve.wait_ge(e_cw, NCH)
            expert_weights(0, 0)
            expert(0, 0, True)
            with dve.Fori(0, (NEXP - 1) // 2 - 1) as g:
                expert(g * 2 + 1, 1, True)
                expert(g * 2 + 2, 0, True)
            expert(NEXP - 2, 1, True)
            expert(NEXP - 1, 0, False)


S4_RE = 1
S4_ANG = 8
S4V_ALL = 36
S4P_HALF = 6 + 6 * 10
B_LINKS = 17
C_LINKS = 15
E_END_LINKS = 3
E_NORM_LINKS = 2 * CHB
E_TOP_LINKS = 2 * CHB + 2


def _constants():
    n = 2 * T
    k = np.arange(T)
    ang = 2.0 * np.pi * (np.outer(k, k) % n) / n
    sign = (-1.0) ** k
    fa, fb = np.cos(ang), -np.sin(ang)
    fb = fb.copy()
    fb[:, 0] = sign
    scale = np.where(k == 0, 1.0, 2.0)[:, None] / n
    ia = scale * np.cos(ang)
    ib = -scale * np.sin(ang)
    ib[0] = sign / n
    m1 = np.cos(ang)
    m4 = np.cos(ang).copy()
    m4[:, 0] = sign
    m3 = -np.sin(ang)
    m3[:, 0] = 0.0
    m2 = -m3
    dft = np.stack([fa, fb, ia, ib, m1, m4, m3, m2]).astype(np.float32)
    return dft, np.eye(128, dtype=np.float32)


def kernel(**inputs):
    import numpy as _np
    import concourse.bacc as _bacc
    from concourse import mybir as _mybir
    from concourse.bass_utils import run_bass_kernel_spmd as _run

    nc = _bacc.Bacc("TRN2", target_bir_lowering=False, num_devices=1)
    data = {}
    for name, a in inputs.items():
        a = _np.asarray(a)
        if a.dtype == _np.bool_:
            a = a.view(_np.uint8)
        data[name] = a
    data["L1_xattn_mod_gate"] = data["L1_xattn_mod_gate"].reshape(1)
    data["L1_xattn_b1"] = data["L1_xattn_b1"].reshape(8, 128).T
    data["L1_xattn_log_dt"] = data["L1_xattn_log_dt"].reshape(2, 128).T
    for name in ("L0_xattn_Wk", "L0_xattn_Wv", "L1_xattn_Wk", "L1_xattn_Wv"):
        w = data[name]
        data[name] = _np.concatenate([w[:128], _np.zeros((2 * 128 - DC, w.shape[1]), w.dtype), w[128:]])
    for name in ("L0_ffn_w1", "L0_ffn_w2", "L1_ffn_Wr", "mask_BxS_bf1"):
        data[name] = data[name].T
    for new, shared, routed in (("e_gate", "L1_ffn_Wg_s", "L1_ffn_Wg"), ("e_up", "L1_ffn_Wu_s", "L1_ffn_Wu"),
                                ("e_down", "L1_ffn_Wd_s", "L1_ffn_Wd")):
        both = _np.concatenate([data.pop(shared)[None], data.pop(routed)])
        data[new] = both.transpose(0, 2, 1)
    data["dft"], data["ident"] = _constants()
    arrays, args = {}, {}
    for name, a in data.items():
        a = _np.ascontiguousarray(a)
        arrays[f"in_{name}_dram"] = a
        args[name] = nc.dram_tensor(f"in_{name}_dram", a.shape, _mybir.dt.from_np(a.dtype), kind="ExternalInput").ap()
    out = nc.dram_tensor("out_0_dram", (NB, T, D), F32, kind="ExternalOutput").ap()
    build(nc, args, out)
    r = _run(nc, [arrays], core_ids=[0])
    return r.results[0]["out_0_dram"]
```
